# Optimizing a Trainium2 kernel written in Bass

```python
import numpy as np
import jax
import jax.numpy as jnp

def _softmax(x, axis=-1):
    return jax.nn.softmax(x, axis=axis)

def _gelu(x):
    return jax.nn.gelu(x, approximate=True)

def _silu(x):
    return jax.nn.silu(x)

def _sigmoid(x):
    return jax.nn.sigmoid(x)

def _layernorm(x, axis=-1, eps=1e-05):
    m = jnp.mean(x, axis=axis, keepdims=True)
    v = jnp.var(x, axis=axis, keepdims=True)
    return (x - m) / jnp.sqrt(v + eps)

def _scatter_add(tgt, idx, src, axis=0):
    return tgt.at[idx].add(src)

def _segment_sum(src, seg, n):
    return jax.ops.segment_sum(src, seg, n)
kernel_name = 'mk_flamingo_gated_d1_seqx_r2_10562b'

def setup_inputs(seed: int=0):
    np.random.seed(seed)
    _w = jnp.asarray

    def _rec_inputs():
        import jax
        import jax.numpy as jnp
        _rk = jax.random.key(seed)
        x = -0.0003929 + 0.9999 * jax.random.normal(jax.random.fold_in(_rk, 1), (2, 1024, 2048), jnp.float32)
        _lenS = 1024 - jax.random.randint(jax.random.fold_in(_rk, 7), (2,), 0, max(1, 1024 // 4) + 1, jnp.int32)
        _lenS2 = 2048 - jax.random.randint(jax.random.fold_in(_rk, 8), (2,), 0, max(1, 2048 // 4) + 1, jnp.int32)
        pos_BxS = jnp.broadcast_to(jnp.arange(1024, dtype=jnp.int32), (2, 1024))
        _ctx_1024P = jax.random.normal(jax.random.fold_in(_rk, 12), (2, 16, 512), jnp.float32)
        _ctx_1024c = jax.random.dirichlet(jax.random.fold_in(_rk, 512), 0.3 * jnp.ones((16,), jnp.float32), (2, 2048))
        _ctx_1024t = jnp.einsum('bsk,bkd->bsd', _ctx_1024c, _ctx_1024P)
        _ctx_1024t = _ctx_1024t * jax.lax.rsqrt(jnp.mean(jnp.square(_ctx_1024t)) + 1e-12) * 0.953939
        ctx_1024 = 6.77073e-06 + 0.0199965 * (_ctx_1024t + 0.3 * jax.random.normal(jax.random.fold_in(_rk, 612), (2, 2048, 512), jnp.float32))
        _g = jax.random.normal(jax.random.fold_in(_rk, 9001), (2, 1), jnp.float32)
        _g = jnp.sign(_g) * jnp.maximum(jnp.abs(_g), 1.0) + (_g == 0) * 1.0
        g_xattn = _g[0]
        g_ffn = _g[1]
        return (x, pos_BxS, ctx_1024, g_xattn, g_ffn)
    x, pos_BxS, ctx_1024, g_xattn, g_ffn = _rec_inputs()

    def _L0_xattn_setup():
        import jax, jax.numpy as jnp
        import numpy as np
        H = 512
        C = 4
        RH = 16
        HS = H // RH
        DR = 8
        M = 2048
        NH = 16
        HD = H // NH
        A_SIZE = (C - 1) * RH
        B_SIZE = C * RH
        EPS = 1e-05
        SSM_EPS = 1e-05

        def rat_read(res, W, gamma, beta, num_outputs):
            b, l, _ = res.shape
            x = res.reshape(b, l, H, C)
            y = jnp.einsum('blhc,hoc->bloh', x, W)
            mu = y.mean(-1, keepdims=True)
            var = y.var(-1, keepdims=True)
            yn = (y - mu) * jax.lax.rsqrt(var + EPS)
            yn = yn * gamma.reshape(num_outputs, H) + beta.reshape(num_outputs, H)
            return yn.reshape(b, l, num_outputs * H)

        def rope(x, pos):
            half = HD // 2
            inv = 1.0 / 10000.0 ** (jnp.arange(half, dtype=jnp.float32) / half)
            ang = pos.astype(jnp.float32)[..., None] * inv
            cos = jnp.cos(ang)[:, :, None, :]
            sin = jnp.sin(ang)[:, :, None, :]
            x1, x2 = (x[..., :half], x[..., half:])
            return jnp.concatenate([x1 * cos - x2 * sin, x2 * cos + x1 * sin], axis=-1)

        def attention(qkv_in, qkv_w, pos):
            b, l, _ = qkv_in.shape
            q, k, v = jnp.split(qkv_in, 3, axis=-1)
            q = jnp.einsum('bli,oi->blo', q, qkv_w[0]).reshape(b, l, NH, HD)
            k = jnp.einsum('bli,oi->blo', k, qkv_w[1]).reshape(b, l, NH, HD)
            v = jnp.einsum('bli,oi->blo', v, qkv_w[2]).reshape(b, l, NH, HD)
            q = rope(q, pos)
            k = rope(k, pos)
            scores = jnp.einsum('bqhd,bkhd->bhqk', q, k) / np.sqrt(HD).astype(np.float32)
            mask = jnp.tril(jnp.ones((l, l), dtype=bool))
            scores = jnp.where(mask, scores, jnp.float32(-1e+30))
            p = jax.nn.softmax(scores, axis=-1)
            o = jnp.einsum('bhqk,bkhd->bqhd', p, v)
            return o.reshape(b, l, H)

        def rat_write(res, y, wod_w, wab_w, wab_b, du_w, du_b):
            b, l, _ = res.shape
            o_d = y @ wod_w.T
            A_B = y @ wab_w.T + wab_b
            out = o_d[..., :H]
            delta_low = o_d[..., H:]
            A_logit = A_B[..., :A_SIZE]
            B_proj = A_B[..., A_SIZE:2 * A_SIZE]
            B_skip = A_B[..., 2 * A_SIZE:]
            delta = jax.nn.softplus(delta_low @ du_w.T + du_b)
            hs = res.reshape(b, l, HS, RH, C)
            out = out.reshape(b, l, HS, RH, 1)
            delta = delta.reshape(b, l, HS, RH, 1)
            A_logit = A_logit.reshape(b, l, 1, RH, C - 1)
            B_proj = B_proj.reshape(b, l, 1, RH, C - 1)
            B_skip = B_skip.reshape(b, l, 1, RH, 1)
            A_neg = -jax.nn.softplus(A_logit)
            A_bar = jnp.exp(delta * A_neg)
            B_bar = (A_bar - 1.0) / (A_neg - SSM_EPS) * B_proj
            B_bar_skip = delta * B_skip
            A_full = jnp.concatenate([A_bar, jnp.ones_like(A_bar[..., :1])], axis=-1)
            B_full = jnp.concatenate([B_bar, B_bar_skip], axis=-1)
            return (hs * A_full + out * B_full).reshape(b, l, H * C)

        def layer_forward(hidden_states, position_ids, attn_read_w, attn_read_g, attn_read_b, qkv_w, attn_wod_w, attn_wab_w, attn_wab_b, attn_du_w, attn_du_b, mlp_read_w, mlp_read_g, mlp_read_b, mlp_in_w, mlp_wod_w, mlp_wab_w, mlp_wab_b, mlp_du_w, mlp_du_b):
            qkv_in = rat_read(hidden_states, attn_read_w, attn_read_g, attn_read_b, 3)
            attn_out = attention(qkv_in, qkv_w, position_ids)
            hidden_states = rat_write(hidden_states, attn_out, attn_wod_w, attn_wab_w, attn_wab_b, attn_du_w, attn_du_b)
            mlp_in = rat_read(hidden_states, mlp_read_w, mlp_read_g, mlp_read_b, 2)
            g_in, u_in = (mlp_in[..., :H], mlp_in[..., H:])
            gate = jnp.einsum('bli,oi->blo', g_in, mlp_in_w[0])
            up = jnp.einsum('bli,oi->blo', u_in, mlp_in_w[1])
            mlp_out = jax.nn.silu(gate) * up
            hidden_states = rat_write(hidden_states, mlp_out, mlp_wod_w, mlp_wab_w, mlp_wab_b, mlp_du_w, mlp_du_b)
            return hidden_states
        key = jax.random.key(seed)
        ks = jax.random.split(key, 20)
        B, L = (2, 1024)
        s = 0.02
        return {'hidden_states': jax.random.normal(ks[0], (B, L, H * C), jnp.float32), 'position_ids': jnp.tile(jnp.arange(L, dtype=jnp.int64), (B, 1)), 'attn_read_w': jax.random.normal(ks[1], (H, 3, C), jnp.float32) / np.sqrt(C).astype(np.float32), 'attn_read_g': jnp.ones((3 * H,), jnp.float32), 'attn_read_b': jnp.zeros((3 * H,), jnp.float32), 'qkv_w': jax.random.normal(ks[2], (3, H, H), jnp.float32) * s, 'attn_wod_w': jax.random.normal(ks[3], (H + DR, H), jnp.float32) * s, 'attn_wab_w': jax.random.normal(ks[4], (A_SIZE + B_SIZE, H), jnp.float32) * s, 'attn_wab_b': jax.random.normal(ks[5], (A_SIZE + B_SIZE,), jnp.float32) * s, 'attn_du_w': jax.random.normal(ks[6], (H, DR), jnp.float32) * s, 'attn_du_b': jax.random.normal(ks[7], (H,), jnp.float32) * s, 'mlp_read_w': jax.random.normal(ks[8], (H, 2, C), jnp.float32) / np.sqrt(C).astype(np.float32), 'mlp_read_g': jnp.ones((2 * H,), jnp.float32), 'mlp_read_b': jnp.zeros((2 * H,), jnp.float32), 'mlp_in_w': jax.random.normal(ks[9], (2, M, H), jnp.float32) * s, 'mlp_wod_w': jax.random.normal(ks[10], (H + DR, M), jnp.float32) * s, 'mlp_wab_w': jax.random.normal(ks[11], (A_SIZE + B_SIZE, M), jnp.float32) * s, 'mlp_wab_b': jax.random.normal(ks[12], (A_SIZE + B_SIZE,), jnp.float32) * s, 'mlp_du_w': jax.random.normal(ks[13], (H, DR), jnp.float32) * s, 'mlp_du_b': jax.random.normal(ks[14], (H,), jnp.float32) * s}
    _L0_xattn_all = _L0_xattn_setup()
    _L0_xattn_in = {k: v for k, v in _L0_xattn_all.items() if k in ('attn_read_w', 'attn_read_g', 'attn_read_b', 'qkv_w', 'attn_wod_w', 'attn_wab_w', 'attn_wab_b', 'attn_du_w', 'attn_du_b', 'mlp_read_w', 'mlp_read_g', 'mlp_read_b', 'mlp_wod_w', 'mlp_wab_w', 'mlp_wab_b', 'mlp_du_w', 'mlp_du_b')}
    del _L0_xattn_all

    def _L0_ffn_setup():
        import jax, jax.numpy as jnp
        import numpy as np
        D_IN, D_OUT = (2048, 2048)
        B, S = (2, 1024)
        key = jax.random.key(seed)
        kx, kw = jax.random.split(key)
        x = jax.random.normal(kx, (B, S, D_IN), dtype=jnp.float32)
        w = jax.random.normal(kw, (D_IN, D_OUT), dtype=jnp.float32)
        sign = jnp.where(w >= 0, 1.0, -1.0).astype(jnp.float32)
        scale = jnp.abs(w).mean().astype(jnp.float32)
        return {'x': x, 'sign': sign, 'scale': scale}
    _L0_ffn_all = _L0_ffn_setup()
    _L0_ffn_in = {k: v for k, v in _L0_ffn_all.items() if k in ('sign', 'scale')}
    del _L0_ffn_all
    return {'x': x, 'pos_BxS': pos_BxS, 'ctx_1024': ctx_1024, 'g_xattn': g_xattn, 'g_ffn': g_ffn, 'L0_xattn_attn_read_w': _L0_xattn_in['attn_read_w'], 'L0_xattn_attn_read_g': _L0_xattn_in['attn_read_g'], 'L0_xattn_attn_read_b': _L0_xattn_in['attn_read_b'], 'L0_xattn_qkv_w': _L0_xattn_in['qkv_w'], 'L0_xattn_attn_wod_w': _L0_xattn_in['attn_wod_w'], 'L0_xattn_attn_wab_w': _L0_xattn_in['attn_wab_w'], 'L0_xattn_attn_wab_b': _L0_xattn_in['attn_wab_b'], 'L0_xattn_attn_du_w': _L0_xattn_in['attn_du_w'], 'L0_xattn_attn_du_b': _L0_xattn_in['attn_du_b'], 'L0_xattn_mlp_read_w': _L0_xattn_in['mlp_read_w'], 'L0_xattn_mlp_read_g': _L0_xattn_in['mlp_read_g'], 'L0_xattn_mlp_read_b': _L0_xattn_in['mlp_read_b'], 'L0_xattn_mlp_wod_w': _L0_xattn_in['mlp_wod_w'], 'L0_xattn_mlp_wab_w': _L0_xattn_in['mlp_wab_w'], 'L0_xattn_mlp_wab_b': _L0_xattn_in['mlp_wab_b'], 'L0_xattn_mlp_du_w': _L0_xattn_in['mlp_du_w'], 'L0_xattn_mlp_du_b': _L0_xattn_in['mlp_du_b'], 'L0_ffn_sign': _L0_ffn_in['sign'], 'L0_ffn_scale': _L0_ffn_in['scale']}

def reference(x, pos_BxS, ctx_1024, g_xattn, g_ffn, L0_xattn_attn_read_w, L0_xattn_attn_read_g, L0_xattn_attn_read_b, L0_xattn_qkv_w, L0_xattn_attn_wod_w, L0_xattn_attn_wab_w, L0_xattn_attn_wab_b, L0_xattn_attn_du_w, L0_xattn_attn_du_b, L0_xattn_mlp_read_w, L0_xattn_mlp_read_g, L0_xattn_mlp_read_b, L0_xattn_mlp_wod_w, L0_xattn_mlp_wab_w, L0_xattn_mlp_wab_b, L0_xattn_mlp_du_w, L0_xattn_mlp_du_b, L0_ffn_sign, L0_ffn_scale):
    import jax
    import jax.numpy as jnp

    def _L0_xattn_ref(hidden_states, position_ids, attn_read_w, attn_read_g, attn_read_b, qkv_w, attn_wod_w, attn_wab_w, attn_wab_b, attn_du_w, attn_du_b, mlp_read_w, mlp_read_g, mlp_read_b, mlp_in_w, mlp_wod_w, mlp_wab_w, mlp_wab_b, mlp_du_w, mlp_du_b):
        import jax, jax.numpy as jnp
        import numpy as np
        H = 512
        C = 4
        RH = 16
        HS = H // RH
        DR = 8
        M = 2048
        NH = 16
        HD = H // NH
        A_SIZE = (C - 1) * RH
        B_SIZE = C * RH
        EPS = 1e-05
        SSM_EPS = 1e-05

        def rat_read(res, W, gamma, beta, num_outputs):
            b, l, _ = res.shape
            x = res.reshape(b, l, H, C)
            y = jnp.einsum('blhc,hoc->bloh', x, W)
            mu = y.mean(-1, keepdims=True)
            var = y.var(-1, keepdims=True)
            yn = (y - mu) * jax.lax.rsqrt(var + EPS)
            yn = yn * gamma.reshape(num_outputs, H) + beta.reshape(num_outputs, H)
            return yn.reshape(b, l, num_outputs * H)

        def rope(x, pos):
            half = HD // 2
            inv = 1.0 / 10000.0 ** (jnp.arange(half, dtype=jnp.float32) / half)
            ang = pos.astype(jnp.float32)[..., None] * inv
            cos = jnp.cos(ang)[:, :, None, :]
            sin = jnp.sin(ang)[:, :, None, :]
            x1, x2 = (x[..., :half], x[..., half:])
            return jnp.concatenate([x1 * cos - x2 * sin, x2 * cos + x1 * sin], axis=-1)

        def attention(qkv_in, qkv_w, pos):
            b, l, _ = qkv_in.shape
            q, k, v = jnp.split(qkv_in, 3, axis=-1)
            q = jnp.einsum('bli,oi->blo', q, qkv_w[0]).reshape(b, l, NH, HD)
            k = jnp.einsum('bli,oi->blo', k, qkv_w[1]).reshape(b, l, NH, HD)
            v = jnp.einsum('bli,oi->blo', v, qkv_w[2]).reshape(b, l, NH, HD)
            q = rope(q, pos)
            k = rope(k, pos)
            scores = jnp.einsum('bqhd,bkhd->bhqk', q, k) / np.sqrt(HD).astype(np.float32)
            mask = jnp.tril(jnp.ones((l, l), dtype=bool))
            scores = jnp.where(mask, scores, jnp.float32(-1e+30))
            p = jax.nn.softmax(scores, axis=-1)
            o = jnp.einsum('bhqk,bkhd->bqhd', p, v)
            return o.reshape(b, l, H)

        def rat_write(res, y, wod_w, wab_w, wab_b, du_w, du_b):
            b, l, _ = res.shape
            o_d = y @ wod_w.T
            A_B = y @ wab_w.T + wab_b
            out = o_d[..., :H]
            delta_low = o_d[..., H:]
            A_logit = A_B[..., :A_SIZE]
            B_proj = A_B[..., A_SIZE:2 * A_SIZE]
            B_skip = A_B[..., 2 * A_SIZE:]
            delta = jax.nn.softplus(delta_low @ du_w.T + du_b)
            hs = res.reshape(b, l, HS, RH, C)
            out = out.reshape(b, l, HS, RH, 1)
            delta = delta.reshape(b, l, HS, RH, 1)
            A_logit = A_logit.reshape(b, l, 1, RH, C - 1)
            B_proj = B_proj.reshape(b, l, 1, RH, C - 1)
            B_skip = B_skip.reshape(b, l, 1, RH, 1)
            A_neg = -jax.nn.softplus(A_logit)
            A_bar = jnp.exp(delta * A_neg)
            B_bar = (A_bar - 1.0) / (A_neg - SSM_EPS) * B_proj
            B_bar_skip = delta * B_skip
            A_full = jnp.concatenate([A_bar, jnp.ones_like(A_bar[..., :1])], axis=-1)
            B_full = jnp.concatenate([B_bar, B_bar_skip], axis=-1)
            return (hs * A_full + out * B_full).reshape(b, l, H * C)

        def layer_forward(hidden_states, position_ids, attn_read_w, attn_read_g, attn_read_b, qkv_w, attn_wod_w, attn_wab_w, attn_wab_b, attn_du_w, attn_du_b, mlp_read_w, mlp_read_g, mlp_read_b, mlp_in_w, mlp_wod_w, mlp_wab_w, mlp_wab_b, mlp_du_w, mlp_du_b):
            qkv_in = rat_read(hidden_states, attn_read_w, attn_read_g, attn_read_b, 3)
            attn_out = attention(qkv_in, qkv_w, position_ids)
            hidden_states = rat_write(hidden_states, attn_out, attn_wod_w, attn_wab_w, attn_wab_b, attn_du_w, attn_du_b)
            mlp_in = rat_read(hidden_states, mlp_read_w, mlp_read_g, mlp_read_b, 2)
            g_in, u_in = (mlp_in[..., :H], mlp_in[..., H:])
            gate = jnp.einsum('bli,oi->blo', g_in, mlp_in_w[0])
            up = jnp.einsum('bli,oi->blo', u_in, mlp_in_w[1])
            mlp_out = jax.nn.silu(gate) * up
            hidden_states = rat_write(hidden_states, mlp_out, mlp_wod_w, mlp_wab_w, mlp_wab_b, mlp_du_w, mlp_du_b)
            return hidden_states
        return layer_forward(hidden_states, position_ids, attn_read_w, attn_read_g, attn_read_b, qkv_w, attn_wod_w, attn_wab_w, attn_wab_b, attn_du_w, attn_du_b, mlp_read_w, mlp_read_g, mlp_read_b, mlp_in_w, mlp_wod_w, mlp_wab_w, mlp_wab_b, mlp_du_w, mlp_du_b)

    def _L0_ffn_ref(x, sign, scale):
        import jax, jax.numpy as jnp
        import numpy as np
        D_IN, D_OUT = (2048, 2048)
        B, S = (2, 1024)
        s = jax.nn.softplus(scale)
        return jnp.einsum('bsi,io->bso', x, sign) * s
    x = x + jnp.tanh(g_xattn[0]) * _L0_xattn_ref(_layernorm(x, axis=-1), pos_BxS, L0_xattn_attn_read_w, L0_xattn_attn_read_g, L0_xattn_attn_read_b, L0_xattn_qkv_w, L0_xattn_attn_wod_w, L0_xattn_attn_wab_w, L0_xattn_attn_wab_b, L0_xattn_attn_du_w, L0_xattn_attn_du_b, L0_xattn_mlp_read_w, L0_xattn_mlp_read_g, L0_xattn_mlp_read_b, ctx_1024, L0_xattn_mlp_wod_w, L0_xattn_mlp_wab_w, L0_xattn_mlp_wab_b, L0_xattn_mlp_du_w, L0_xattn_mlp_du_b)
    x = x + jnp.tanh(g_ffn[0]) * _L0_ffn_ref(_layernorm(x, axis=-1), L0_ffn_sign, L0_ffn_scale)
    return x

_drawn_inputs = setup_inputs


def setup_inputs(seed=0):
    import zlib

    import numpy as np

    out = dict(_drawn_inputs(seed))
    spreads = {'L0_xattn_attn_read_g': (1.0, 0.2),
     'L0_xattn_attn_read_b': (0.0, 0.1),
     'L0_xattn_mlp_read_g': (1.0, 0.2),
     'L0_xattn_mlp_read_b': (0.0, 0.1)}
    factors = {}
    for name, (base, spread) in spreads.items():
        noise = np.random.default_rng([zlib.crc32(name.encode()), seed]).standard_normal(out[name].shape)
        drawn = base * np.exp(spread * noise) if base else spread * noise
        out[name] = jnp.asarray(drawn.astype(out[name].dtype))
    for name, factor in factors.items():
        out[name] = (out[name] * factor).astype(out[name].dtype)
    return out
```

```python
from contextlib import ExitStack

import concourse.bass as bass
from concourse import mybir

F32 = mybir.dt.float32
F32R = mybir.dt.float32r
I32 = mybir.dt.int32
ALU = mybir.AluOpType
ACT = mybir.ActivationFunctionType
AX = mybir.AxisListType

P = 128
B, L = 2, 1024
H, C = 512, 4
D = H * C
NF = D // P
HC = H // P
NH, HD = 16, 32
RH = 16
DR = 8
M = 2048
NM = M // P
T = 512
NB = B * L // T
TT = T // P
KT = L // P
NA = (C - 1) * RH
ROWS = DR + 2 * NA + RH
WALL = H + ROWS
NX = 2 * HC + 2 * C - 1
EPS = 1e-5
NEG = -1e30
STACK = 3 * HD


class Event:

    def __init__(self, ctx, nc, name, per=1, unit=1, credit=0):
        self.sem = ctx.enter_context(nc.semaphore(name))
        self.per, self.unit, self.credit = per, unit, credit

    def value(self, i, k):
        return i * (self.per * self.unit) + (k * self.unit + self.credit)

    def wait(self, eng, i=0, k=1):
        assert not isinstance(k, int) or k * self.unit + self.credit > 0, "a wait's value stays positive"
        eng.wait_ge(self.sem, self.value(i, k))

    def fire(self, instruction):
        instruction.then_inc(self.sem, self.unit)


def setup_phase(nc, io, t):
    with ExitStack() as ctx:
        def ev(name, **k):
            return Event(ctx, nc, "s0_" + name, **k)

        raw = ctx.enter_context(nc.sbuf_tensor("qkv_raw", [P, 3 * HC * H], F32))
        pos_i = ctx.enter_context(nc.sbuf_tensor("pos_i", [P, B * KT], I32))
        pos_f = ctx.enter_context(nc.sbuf_tensor("pos_f", [P, B * KT], F32))
        inv = ctx.enter_context(nc.sbuf_tensor("inv_freq", [P, HD // 2], F32))
        ang = ctx.enter_context(nc.sbuf_tensor("ang", [P, 2, B * KT, HD // 2], F32))
        turns = ctx.enter_context(nc.sbuf_tensor("turns", [P, 2, B * KT, HD // 2], F32))
        gates = ctx.enter_context(nc.sbuf_tensor("gates", [P, 3], F32))
        g_tmp = ctx.enter_context(nc.sbuf_tensor("g_tmp", [P, 4], F32))
        idf = t["ident"]
        loaded = ev("loaded", unit=16)
        w_loaded = ev("w_loaded", unit=16)
        high = ev("high")
        dve = ev("dve")
        act = ev("act")
        low = ev("low")
        loads = [(pos_i[:], io["pos"]), (inv[:], io["inv_freq"]), (gates[:], io["gates"]),
                 (idf[:], io["ident"]), (t["masks"][:], io["masks"]), (t["read1"][:], io["read1"]),
                 (t["read1_gb"][:], io["read1_gb"])]
        with nc.Block() as block:
            @block.sync
            def _(eng):
                for dst, src in loads:
                    loaded.fire(eng.dma_start(dst, src))
                w_loaded.fire(eng.dma_start(raw[:], io["qkv"]))
                loaded.wait(eng, k=len(loads))
                w_loaded.wait(eng)

            @block.vector
            def _(eng):
                n = 0

                def link(ins):
                    nonlocal n
                    n += 1
                    dve.fire(ins)
                    dve.wait(eng, k=n)

                link(eng.memset(t["ones_d"][:], 1.0 / D))
                link(eng.memset(t["ones_h"][:], 1.0 / H))
                link(eng.memset(t["eps"][:], EPS))
                loaded.wait(eng, k=len(loads))
                link(eng.tensor_copy(pos_f[:], pos_i[:]))
                pb = pos_f[:].unsqueeze(2).to_broadcast([P, B * KT, HD // 2])
                ib = inv[:].unsqueeze(1).to_broadcast([P, B * KT, HD // 2])
                link(eng.tensor_tensor(ang[:, 0], pb, ib, ALU.mult))
                link(eng.tensor_scalar(turns[:, 0], ang[:, 0], 1 / 6.283185307179586, None, ALU.mult))
                link(eng.tensor_scalar(turns[:, 1], turns[:, 0], 0.25, None, ALU.add))
                link(eng.tensor_scalar(turns[:], turns[:], 12582912.0, None, ALU.add))
                link(eng.tensor_scalar(turns[:], turns[:], -12582912.0, None, ALU.add))
                link(eng.tensor_scalar(ang[:, 1], ang[:, 0], 1.0, None, ALU.mult))
                for part in (6.28125, 0.0019350051879882812, 3.0199157663446e-07):
                    link(eng.scalar_tensor_tensor(ang[:], turns[:], -part, ang[:], ALU.mult, ALU.add))
                link(eng.tensor_scalar(ang[:, 1], ang[:, 1], 1.5707963267948966, None, ALU.add))
                link(eng.tensor_scalar(ang[:], ang[:], 3.1415925, -3.1415925, ALU.min, ALU.max))
                act.wait(eng, k=2)
                halves = t["cos"][:].rearrange("p t (a j) -> p t a j", a=2)
                sins = t["sin"][:].rearrange("p t (a j) -> p t a j", a=2)
                for a in range(2):
                    link(eng.tensor_copy(halves[:, :, a], turns[:, 1]))
                link(eng.tensor_scalar(sins[:, :, 0], turns[:, 0], -1.0, None, ALU.mult))
                link(eng.tensor_copy(sins[:, :, 1], turns[:, 0]))
                link(eng.tensor_scalar(g_tmp[:, 3:4], gates[:, 2:3], 0.0, None, ALU.max))
                link(eng.scalar_tensor_tensor(g_tmp[:, 2:3], g_tmp[:, 3:4], -2.0, gates[:, 2:3], ALU.mult, ALU.add))
                act.wait(eng, k=5)
                link(eng.tensor_tensor(g_tmp[:, 3:4], g_tmp[:, 3:4], g_tmp[:, 2:3], ALU.add))
                link(eng.tensor_tensor(t["gate"][:, 1:2], g_tmp[:, 1:2], g_tmp[:, 3:4], ALU.mult))
                link(eng.tensor_copy(t["gate"][:, 0:1], g_tmp[:, 0:1]))
                w_loaded.wait(eng)
                high.wait(eng)
                low.fire(eng.tensor_tensor(t["qkv_l"][:], raw[:], t["qkv_h"][:].bitcast(F32), ALU.subtract))
                low.wait(eng)

            @block.scalar
            def _(eng):
                n = 0

                def link(ins):
                    nonlocal n
                    n += 1
                    act.fire(ins)
                    act.wait(eng, k=n)

                w_loaded.wait(eng)
                high.fire(eng.activation(t["qkv_h"][:], raw[:], ACT.Copy))
                dve.wait(eng, k=15)
                link(eng.activation(turns[:, 0], ang[:, 0], ACT.Sin))
                link(eng.activation(turns[:, 1], ang[:, 1], ACT.Sin))
                loaded.wait(eng, k=len(loads))
                link(eng.activation(g_tmp[:, 0:2], gates[:, 0:2], ACT.Tanh))
                dve.wait(eng, k=21)
                link(eng.activation(g_tmp[:, 2:3], g_tmp[:, 2:3], ACT.Exp))
                link(eng.activation(g_tmp[:, 2:3], g_tmp[:, 2:3], ACT.Ln, bias=1.0))
                eng.activation(t["ident_r"][:], idf[:], ACT.Copy)
                link(eng.activation(t["masks_r"][:], t["masks"][:], ACT.Copy))


class Chain:

    def __init__(self, ctx, nc, name, per):
        self.event, self.at = Event(ctx, nc, name, per=per), 0

    def link(self, eng, i, instruction):
        self.at += 1
        self.event.fire(instruction)
        self.event.wait(eng, i, self.at)

    def close(self):
        assert self.at == self.event.per, (self.at, self.event.per)


def read_phase(nc, io, t):
    with ExitStack() as ctx:
        def ev(name, **k):
            return Event(ctx, nc, "s1_" + name, **k)

        def sb(name, shape, dt=F32):
            return ctx.enter_context(nc.sbuf_tensor(name, shape, dt))

        X = sb("X", [P, NF, T])
        SQ = sb("SQ", [P, 2, HC, T])
        Y = sb("Y", [P, 3, HC, T])
        ZH = sb("ZH", [P, HC, T], F32R)
        ZL = sb("ZL", [P, HC, T], F32R)
        R = sb("R", [P, 4, T])
        RT = sb("RT", [P, 2, H])
        OUT = sb("OUT", [P, TT, H])
        ps = ctx.enter_context(nc.psum_tensor("ps1", [P, 8, 512], F32))
        MEAN, VAR, YM, YV, PJ = 0, 1, 2, 3, 4

        x_in = ev("x_in", unit=16)
        xn_out = ev("xn_out", unit=16, credit=16)
        mean, cent, var, xn = ev("mean"), ev("cent"), ev("var"), ev("xn")
        sq = ev("sq", per=7)
        sq_used = ev("sq_used", per=7, credit=1)
        rs = ev("rs", per=4)
        y = ev("y", per=3, credit=1)
        ym, yc, yv, z, zh, zl = (ev(n, per=3) for n in ("ym", "yc", "yv", "z", "zh", "zl"))
        pj = ev("pj", per=3 * TT, credit=1)
        pjq_used = ev("pjq_used", per=2 * TT)
        pjv_used = ev("pjv_used", per=TT, credit=TT)
        qk_ready = ev("qk_ready", per=2 * TT)
        stored = [ev(f"stored{tt}", per=3, unit=16, credit=16) for tt in range(TT)]

        with nc.Block() as block:
            @block.gpsimd
            def _(eng):
                with eng.Fori(0, NB) as i:
                    xn_out.wait(eng, i, 0)
                    y.wait(eng, i, 0)
                    x_in.fire(eng.dma_start(X[:], io["x"][:, :, bass.ds(i * T, T)]))

            @block.sync
            def _(eng):
                eng.sem_inc(xn_out.sem, 16)
                for tt in range(TT):
                    eng.sem_inc(stored[tt].sem, 16)
                with eng.Fori(0, B) as b, eng.Fori(0, L // T) as half:
                    i = b * (L // T) + half
                    xn.wait(eng, i)
                    xn_out.fire(eng.dma_start(io["xn"][:, :, bass.ds(i * T, T)], X[:]))
                    for o in range(3):
                        for tt in range(TT):
                            if o < 2:
                                qk_ready.wait(eng, i, o * TT + tt + 1)
                            else:
                                pjv_used.wait(eng, i, tt + 1)
                            stored[tt].fire(eng.dma_start(
                                io["qkv_s"][:, o, bass.ds(b * (NH // 2), NH // 2), bass.ds(half * TT + tt, 1), :],
                                OUT[:, tt].rearrange("p (h a d) -> p h a d", h=NH // 2, a=1)))
                xn_out.wait(eng, NB - 1)
                for tt in range(TT):
                    stored[tt].wait(eng, NB - 1, 3)

            @block.tensor
            def _(eng):
                with eng.Fori(0, NB) as i:
                    x_in.wait(eng, i)
                    for f in range(NF):
                        mm = eng.matmul(ps[:, MEAN], t["ones_d"][:], X[:, f], start=f == 0, stop=f == NF - 1)
                    mean.fire(mm)
                    for g in range(4):
                        sq.wait(eng, i, g + 1)
                        for f in range(4):
                            mm = eng.matmul(ps[:, VAR], t["ones_d"][:], SQ[:, g % 2, f],
                                            start=g + f == 0, stop=g + f == 6)
                        sq_used.fire(mm)

                    def y_mean(o):
                        y.wait(eng, i, o + 1)
                        if o:
                            yc.wait(eng, i, o)
                        for hc in range(HC):
                            mm = eng.matmul(ps[:, YM], t["ones_h"][:], Y[:, o, hc], start=hc == 0, stop=hc == HC - 1)
                        ym.fire(mm)

                    def y_var(o):
                        sq.wait(eng, i, 5 + o)
                        if o:
                            rs.wait(eng, i, o + 1)
                        for hc in range(HC):
                            mm = eng.matmul(ps[:, YV], t["ones_h"][:], SQ[:, o % 2, hc],
                                            start=hc == 0, stop=hc == HC - 1)
                        sq_used.fire(mm)

                    def project(o):
                        zh.wait(eng, i, o + 1)
                        zl.wait(eng, i, o + 1)
                        for tt in range(TT):
                            n = o * TT + tt
                            if o == 0:
                                pjv_used.wait(eng, i, n + 1 - TT)
                            else:
                                pjq_used.wait(eng, i, n + 1 - TT)
                            step = 0
                            for ic in range(HC):
                                for zz, ww in ((ZH, "qkv_h"), (ZL, "qkv_h"), (ZH, "qkv_l")):
                                    mm = eng.matmul(ps[:, PJ + tt], zz[:, ic, tt * P:(tt + 1) * P],
                                                    t[ww][:, bass.ts(o * HC + ic, H)],
                                                    start=step == 0, stop=step == 3 * HC - 1)
                                    step += 1
                            pj.fire(mm)

                    y_mean(0)
                    y_mean(1)
                    y_var(0)
                    y_mean(2)
                    y_var(1)
                    project(0)
                    y_var(2)
                    project(1)
                    project(2)

            @block.scalar
            def _(eng):
                eng.preload_act_table_set("natural_log_exp_and_others")
                eng.sem_inc(pjv_used.sem, TT)
                chain = Chain(ctx, nc, "s1_act", 4)
                with eng.Fori(0, NB) as i:
                    def square(k, out, src):
                        sq_used.wait(eng, i, max(k - 1, 0))
                        sq.fire(eng.activation(out, src, ACT.Square))

                    def rstd(k, bank):
                        chain.link(eng, i, eng.activation(R[:, k], ps[:, bank], ACT.Ln, bias=t["eps"][:]))
                        rs.fire(eng.activation(R[:, k], R[:, k], ACT.Exp, scale=-0.5))

                    cent.wait(eng, i)
                    for g in range(4):
                        square(g, SQ[:, g % 2], X[:, 4 * g:4 * g + 4])
                    sq_used.wait(eng, i, 4)
                    rstd(0, VAR)

                    def y_square(o):
                        yc.wait(eng, i, o + 1)
                        square(4 + o, SQ[:, o % 2], Y[:, o])

                    def y_rstd(o):
                        sq_used.wait(eng, i, 5 + o)
                        rstd(1 + o, YV)

                    def z_high(o):
                        z.wait(eng, i, o + 1)
                        pj.wait(eng, i, o * TT)
                        zh.fire(eng.activation(ZH[:], Y[:, o], ACT.Copy))

                    y_square(0)
                    y_square(1)
                    y_rstd(0)
                    y_square(2)
                    y_rstd(1)
                    z_high(0)
                    y_rstd(2)
                    z_high(1)
                    z_high(2)
                    for tt in range(TT):
                        pj.wait(eng, i, 2 * TT + tt + 1)
                        stored[tt].wait(eng, i, 2)
                        pjv_used.fire(eng.activation(OUT[:, tt], ps[:, PJ + tt], ACT.Copy))
                    chain.close()

            @block.vector
            def _(eng):
                eng.sem_inc(y.sem, 1)
                eng.sem_inc(sq_used.sem, 1)
                eng.sem_inc(pj.sem, 1)
                chain = Chain(ctx, nc, "s1_dve", 3 * 3 + 3)
                w, gb = t["read1"], t["read1_gb"]
                with eng.Fori(0, NB) as i:
                    mean.wait(eng, i)
                    cent.fire(eng.tensor_tensor(X[:], X[:], ps[:, MEAN].unsqueeze(1).to_broadcast([P, NF, T]), ALU.subtract))
                    rs.wait(eng, i, 1)
                    xn.fire(eng.tensor_tensor(X[:], X[:], R[:, 0].unsqueeze(1).to_broadcast([P, NF, T]), ALU.mult))
                    xn.wait(eng, i)

                    def read(o):
                        for c in range(C):
                            for hc in range(HC):
                                ww = w[:, hc, o, c:c + 1]
                                if c == 0:
                                    ins = eng.tensor_scalar(Y[:, o, hc], X[:, c * HC + hc], ww, None, ALU.mult)
                                else:
                                    ins = eng.scalar_tensor_tensor(Y[:, o, hc], X[:, c * HC + hc], ww, Y[:, o, hc],
                                                                   ALU.mult, ALU.add)
                            if c < C - 1:
                                chain.link(eng, i, ins)
                        y.fire(ins)

                    def centre(o):
                        ym.wait(eng, i, o + 1)
                        yc.fire(eng.tensor_tensor(Y[:, o], Y[:, o], ps[:, YM].unsqueeze(1).to_broadcast([P, HC, T]), ALU.subtract))

                    def scale(o):
                        rs.wait(eng, i, o + 2)
                        chain.link(eng, i, eng.tensor_tensor(Y[:, o], Y[:, o], R[:, 1 + o].unsqueeze(1).to_broadcast([P, HC, T]), ALU.mult))
                        for hc in range(HC):
                            ins = eng.tensor_scalar(Y[:, o, hc], Y[:, o, hc], gb[:, 0, o, hc:hc + 1], gb[:, 1, o, hc:hc + 1],
                                                    ALU.mult, ALU.add)
                        z.fire(ins)

                    def z_low(o):
                        zh.wait(eng, i, o + 1)
                        z.wait(eng, i, o + 1)
                        pj.wait(eng, i, o * TT)
                        zl.fire(eng.tensor_tensor(ZL[:], Y[:, o], ZH[:].bitcast(F32), ALU.subtract))

                    def rope(o):
                        for tt in range(TT):
                            pj.wait(eng, i, o * TT + tt + 1)
                            src = ps[:, PJ + tt].rearrange("p (h d) -> p h d", h=NH)
                            tile = bass.ds(i * TT + tt, 1)
                            cos = t["cos"][:, tile, :].to_broadcast([P, NH, HD])
                            sin = t["sin"][:, tile, :].to_broadcast([P, NH, HD])
                            a = RT[:, 0].rearrange("p (h d) -> p h d", h=NH)
                            b = RT[:, 1].rearrange("p (h d) -> p h d", h=NH)
                            hf = HD // 2
                            eng.tensor_tensor(a, src, cos, ALU.mult)
                            eng.tensor_tensor(b[:, :, 0:hf], src[:, :, hf:HD], sin[:, :, 0:hf], ALU.mult)
                            last = eng.tensor_tensor(b[:, :, hf:HD], src[:, :, 0:hf], sin[:, :, hf:HD], ALU.mult)
                            pjq_used.fire(last)
                            pjq_used.wait(eng, i, o * TT + tt + 1)
                            stored[tt].wait(eng, i, o)
                            qk_ready.fire(eng.tensor_tensor(OUT[:, tt], RT[:, 0], RT[:, 1], ALU.add))
                            qk_ready.wait(eng, i, o * TT + tt + 1)

                    for o in range(3):
                        read(o)
                    centre(0)
                    centre(1)
                    scale(0)
                    centre(2)
                    z_low(0)
                    scale(1)
                    rope(0)
                    z_low(1)
                    scale(2)
                    rope(1)
                    z_low(2)
                    chain.close()


def attention_phase(nc, io, t):
    with ExitStack() as ctx:
        def ev(name, **k):
            return Event(ctx, nc, "s2_" + name, **k)

        def sb(name, shape, dt=F32):
            return ctx.enter_context(nc.sbuf_tensor(name, shape, dt))

        G = [sb(f"G{n}", [P, KT, 2 * HD]) for n in "qkv"]
        S = [sb(f"stack_{n}", [P, KT, STACK], F32R) for n in "qk"]
        ST = [[sb(f"turned_{n}{a}", [STACK + 1, L], F32R) for a in range(2)] for n in "qk"]
        VO = [sb(f"v_ones{a}", [P, KT, 2 * HD]) for a in range(2)]
        zeros = sb("zeros", [P, KT, HD])
        MAXES = sb("maxes", [P, KT, 2])
        NM = sb("neg_max", [P, KT])
        NPT = 3
        PT = sb("probs", [P, NPT, T])
        RC = sb("recip", [HD, 2, T])
        OT = [sb(f"heads_out{a}", [HD, L]) for a in range(2)]
        ones = sb("ones_row", [STACK + 1, L])
        ps = ctx.enter_context(nc.psum_tensor("ps2", [P, 8, 512], F32))
        TR, MX, SC, O = 0, (1, 2, 7), (3, 4), (5, 6)

        MXP = [(q, a, min((q + 1) * P - a, T)) for q in range(KT) for a in range(0, (q + 1) * P, T)]
        SCP = [(h, k, max(k * P, h * T), (h + 1) * T - max(k * P, h * T))
               for h in range(L // T) for k in range((h + 1) * TT)]
        NMX, NSC = len(MXP), len(SCP)
        last_of = [max(p for p, x in enumerate(SCP) if x[0] == h) + 1 for h in range(L // T)]

        loaded = [ev(f"loaded_{n}", unit=16) for n in "qkv"]
        high, low, v_in = ev("high", credit=1), ev("low", credit=1), ev("v_in", credit=1)
        tr = ev("tr", per=4)
        tr_dve, tr_act = ev("tr_dve", per=2), ev("tr_act", per=2)
        mx, mx_read = ev("mx", per=NMX), ev("mx_read", per=NMX, credit=3)
        nm = ev("nm")
        row, row_out = ev("row", per=2), ev("row_out", per=2, credit=1)
        sc, ex, pv = ev("sc", per=NSC), ev("ex", per=NSC, credit=2), ev("pv", per=NSC, credit=NPT)
        o_out = ev("o_out", per=2, credit=2)
        o_ln, o_part = ev("o_ln", per=2), ev("o_part", per=2)
        stored = [ev(f"stored{a}", unit=16, credit=16) for a in range(2)]
        ready, ones_in = ev("ready"), ev("ones")

        def slots(eng, slot, first=None, last=None):
            heads = B * NH
            if first:
                first()
            slot(0, 0, 0, True, False)
            with eng.Fori(0, heads // 2 - 1) as i:
                slot(i * 2 + 1, 1, i, True, True)
                slot(i * 2 + 2, 0, i + 1, True, True)
            slot(heads - 1, 1, heads // 2 - 1, True, True)
            slot(heads, 0, heads // 2, False, True)

        with nc.Block() as block:
            @block.sync
            def _(eng):
                for a in range(2):
                    eng.sem_inc(stored[a].sem, 16)

                def load(pair, n):
                    for e in (high, low, v_in):
                        e.wait(eng, n, 0)
                    for o in range(3):
                        loaded[o].fire(eng.dma_start(G[o][:], io["qkv_s"][:, o, bass.ds(pair, 1)]))

                def slot(n, a, pair, front, back):
                    if front and a == 1 and not (isinstance(n, int)):
                        load(pair + 1, n + 1)
                    if back:
                        o_out.wait(eng, n - 1, 2)
                        stored[1 - a].fire(eng.dma_start(io["y_s"][bass.ds(n - 1, 1)].rearrange("a d t -> (a d) t"),
                                                         OT[1 - a][:]))

                load(0, 0)
                slots(eng, slot)
                for a in range(2):
                    stored[a].wait(eng, B * NH // 2 - 1)

            @block.gpsimd
            def _(eng):
                for a in range(2):
                    eng.memset(VO[a][:], 1.0)
                eng.memset(zeros[:], 0.0)
                eng.memset(MAXES[:], -3e38).then_inc(v_in.sem, 1)
                v_in.wait(eng, 0, 0)

                def take_v(n, a, pair):
                    loaded[2].wait(eng, pair)
                    pv.wait(eng, n - 1, 0)
                    v_in.fire(eng.tensor_tensor(VO[a][:, :, 0:HD], G[2][:, :, a * HD:(a + 1) * HD], zeros[:], ALU.add))

                def slot(n, a, pair, front, back):
                    if front and not (isinstance(n, int) and n == B * NH - 1):
                        take_v(n + 1, 1 - a, pair + a)

                eng.wait_ge(loaded[2].sem, 16)
                v_in.fire(eng.tensor_tensor(VO[0][:, :, 0:HD], G[2][:, :, 0:HD], zeros[:], ALU.add))
                slots(eng, slot)

            @block.tensor
            def _(eng):
                eng.sem_inc(pv.sem, NPT)
                ready.wait(eng)

                def turn(n, a, k):
                    which, half = k // 2, k % 2
                    if k == 0:
                        high.wait(eng, n)
                        low.wait(eng, n)
                        row_out.wait(eng, n, 0)
                    elif k == 2:
                        tr_act.wait(eng, n, 1)
                    else:
                        tr_dve.wait(eng, n, (k + 1) // 2)
                    for tt in range(TT):
                        mm = eng.transpose(ps[0:STACK, TR, tt * P:(tt + 1) * P].bitcast(F32R),
                                           S[which][:, half * TT + tt], t["ident_r"][:])
                    tr.fire(mm)

                def maxima(n, a, m):
                    q, k0, w = MXP[m]
                    if m == 0:
                        tr_dve.wait(eng, n, 2)
                        tr_act.wait(eng, n, 2)
                    mx_read.wait(eng, n, m - 2)
                    bank = MX[m % 3]
                    diag = k0 + w == (q + 1) * P
                    mm = eng.matmul(ps[:, bank, 0:w], ST[0][a][0:STACK, q * P:(q + 1) * P], ST[1][a][0:STACK, k0:k0 + w],
                                    start=True, stop=not diag, skip_group_check=True)
                    if diag:
                        mm = eng.matmul(ps[:, bank, w - P:w], t["ident_r"][:], t["masks_r"][:, 1], start=False, stop=True,
                                        skip_group_check=True)
                    mx.fire(mm)

                def rows(n, a):
                    nm.wait(eng, n)
                    for r in range(2):
                        if r == 0:
                            tr_act.wait(eng, n, 2)
                        else:
                            row_out.wait(eng, n, 1)
                        for tt in range(TT):
                            mm = eng.matmul(ps[STACK:STACK + 1, TR, tt * P:(tt + 1) * P], NM[:, r * TT + tt:r * TT + tt + 1],
                                            t["ident"][:], start=True, stop=True, skip_group_check=True)
                        row.fire(mm)

                def score(v, a, p):
                    h, k, q0, w = SCP[p]
                    if p == 0:
                        row_out.wait(eng, v, 2)
                    ex.wait(eng, v, p - 1)
                    diag = q0 == k * P
                    mm = eng.matmul(ps[:, SC[p % 2], 0:w], ST[1][a][:, k * P:(k + 1) * P], ST[0][a][:, q0:q0 + w],
                                    start=True, stop=not diag, skip_group_check=True)
                    if diag:
                        mm = eng.matmul(ps[:, SC[p % 2], 0:P], t["ident_r"][:], t["masks_r"][:, 0], start=False, stop=True,
                                        skip_group_check=True)
                    sc.fire(mm)

                def weigh(v, a, p):
                    h, k, q0, w = SCP[p]
                    if p == 0:
                        v_in.wait(eng, v)
                    if k == 0:
                        o_out.wait(eng, v, h - 1)
                    ex.wait(eng, v, p + 1)
                    c = q0 - h * T
                    pv.fire(eng.matmul(ps[0:2 * HD, O[h], c:c + w], VO[a][:, k], PT[:, p % NPT, 0:w],
                                       start=k == 0, stop=p + 1 == last_of[h], skip_group_check=True))

                def slot(n, a, pair, front, back):
                    m = 0
                    for p in range(NSC):
                        if front and p < 4:
                            turn(n, a, p)
                        if back:
                            score(n - 1, 1 - a, p)
                            if p:
                                weigh(n - 1, 1 - a, p - 1)
                        while front and p >= 4 and m < min(NMX, 2 * (p - 3)):
                            maxima(n, a, m)
                            m += 1
                    if back:
                        weigh(n - 1, 1 - a, NSC - 1)
                    if front:
                        rows(n, a)

                slots(eng, slot)

            @block.scalar
            def _(eng):
                eng.sem_inc(ex.sem, 2)
                eng.sem_inc(high.sem, 1)

                def take_high(n, a, pair):
                    for o in range(2):
                        loaded[o].wait(eng, pair)
                    if not (isinstance(n, int) and n == 0):
                        tr.wait(eng, n - 1, 4)
                    c = slice(a * HD, (a + 1) * HD)
                    for o, places in ((0, (0, 1)), (1, (0, 2))):
                        for j in places:
                            ins = eng.activation(S[o][:, :, j * HD:(j + 1) * HD], G[o][:, :, c], ACT.Copy)
                    high.fire(ins)

                def out(n, a, which, half, bank_event, k):
                    tr.wait(eng, n, k)
                    tr_act.fire(eng.activation(ST[which][a][0:STACK, half * T:(half + 1) * T], ps[0:STACK, TR], ACT.Copy))

                def exp(v, a, p):
                    h, k, q0, w = SCP[p]
                    sc.wait(eng, v, p + 1)
                    pv.wait(eng, v, p + 1 - NPT)
                    ex.fire(eng.activation(PT[:, p % NPT, 0:w], ps[:, SC[p % 2], 0:w], ACT.Exp, scale=HD ** -0.5))

                def recip(v, h):
                    pv.wait(eng, v, last_of[h])
                    o_out.wait(eng, v, h - 1)
                    o_ln.fire(eng.activation(RC[:, h], ps[HD:2 * HD, O[h]], ACT.Ln))
                    o_ln.wait(eng, v, h + 1)
                    o_part.fire(eng.activation(RC[:, h], RC[:, h], ACT.Exp, scale=-1.0))

                def slot(n, a, pair, front, back):
                    for p in range(NSC):
                        if back:
                            exp(n - 1, 1 - a, p)
                        if back and p == 6:
                            recip(n - 1, 0)
                        if front and p == 0:
                            out(n, a, 0, 1, tr_act, 2)
                        if front and p == 2:
                            out(n, a, 1, 1, tr_act, 4)
                        if front and p == 5 and not (isinstance(n, int) and n == B * NH - 1):
                            take_high(n + 1, 1 - a, pair + a)
                    if back:
                        recip(n - 1, 1)

                eng.preload_act_table_set("natural_log_exp_and_others")
                take_high(0, 0, 0)
                slots(eng, slot)

            @block.vector
            def _(eng):
                eng.sem_inc(low.sem, 1)
                eng.sem_inc(mx_read.sem, 3)
                eng.sem_inc(row_out.sem, 1)
                eng.sem_inc(o_out.sem, 2)
                ones_in.fire(eng.memset(ones[:], 1.0))
                ones_in.wait(eng)
                for a in range(2):
                    ins = eng.tensor_copy(ST[1][a][STACK:STACK + 1, :], ones[STACK:STACK + 1, :])
                ready.fire(ins)

                def take_low(n, a, pair):
                    high.wait(eng, n)
                    if not (isinstance(n, int) and n == 0):
                        tr.wait(eng, n - 1, 4)
                    c = slice(a * HD, (a + 1) * HD)
                    for o, place in ((0, 2), (1, 1)):
                        ins = eng.tensor_tensor(S[o][:, :, place * HD:(place + 1) * HD], G[o][:, :, c],
                                                S[o][:, :, 0:HD].bitcast(F32), ALU.subtract)
                    low.fire(ins)

                def out(n, a, which, half, k):
                    tr.wait(eng, n, k)
                    tr_dve.fire(eng.tensor_copy(ST[which][a][0:STACK, half * T:(half + 1) * T], ps[0:STACK, TR]))

                def row_max(n, m):
                    q, k0, w = MXP[m]
                    mx.wait(eng, n, m + 1)
                    mx_read.fire(eng.tensor_reduce(MAXES[:, q, k0 // T:k0 // T + 1], ps[:, MX[m % 3], 0:w], AX.X, ALU.max))

                def head_out(v, a, h, pair):
                    pv.wait(eng, v, last_of[h])
                    if h == 0:
                        stored[a].wait(eng, pair, 0)
                    o_part.wait(eng, v, h + 1)
                    o_out.fire(eng.tensor_tensor(OT[a][:, h * T:(h + 1) * T], ps[0:HD, O[h]], RC[:, h], ALU.mult))

                def slot(n, a, pair, front, back):
                    if front:
                        out(n, a, 0, 0, 1)
                        out(n, a, 1, 0, 3)
                        for m in range(4):
                            row_max(n, m)
                    if back:
                        head_out(n - 1, 1 - a, 0, pair - 1 + a)
                    if front:
                        for m in range(4, 6):
                            row_max(n, m)
                        if not (isinstance(n, int) and n == B * NH - 1):
                            take_low(n + 1, 1 - a, pair + a)
                        for m in range(6, NMX):
                            row_max(n, m)
                        mx_read.wait(eng, n, NMX)
                        nm.fire(eng.tensor_reduce(NM[:], MAXES[:], AX.X, ALU.max, negate=True))
                        for r in range(2):
                            row.wait(eng, n, r + 1)
                            row_out.fire(eng.tensor_copy(ST[0][a][STACK:STACK + 1, r * T:(r + 1) * T],
                                                         ps[STACK:STACK + 1, TR]))
                    if back:
                        head_out(n - 1, 1 - a, 1, pair - 1 + a)

                take_low(0, 0, 0)
                slots(eng, slot)


def block_phase(nc, io, t):
    with ExitStack() as ctx:
        def ev(name, **k):
            return Event(ctx, nc, "s3_" + name, **k)

        def sb(name, shape, dt=F32):
            return ctx.enter_context(nc.sbuf_tensor(name, shape, dt))

        KB = 1024
        WA = [sb(f"wall_a{n}", [P, HC, WALL], F32R) for n in "hl"]
        EX = sb("expand_sb", [ROWS, NX, P])
        RW, GB = sb("read2_sb", [P, HC, 2, C]), sb("read2_gb_sb", [P, 2, 2, HC])
        BIAS, DUB = sb("bias_sb", [ROWS, 2]), sb("du_b_sb", [P, 2, HC])
        HS = sb("hidden", [P, NF, T])
        XR = sb("x_piece", [P, 2, HC, T])
        R = sb("rstd_b", [P, 3, T])
        base = nc.sbuf_base
        base = (base + 31) // 32 * 32
        sb("arena", [P, 112 * KB // 4])

        def at(name, kb, shape, dt=F32):
            return nc.alloc_sbuf_tensor_at(name, shape, dt, offset=base + int(kb * KB))

        Y = at("Y2", 0, [P, 2, HC, T])
        ZH, ZL = at("ZH2", 16, [P, 2, HC, T], F32R), at("ZL2", 32, [P, 2, HC, T], F32R)
        DL, SP, RG, G = at("delta", 48, [P, HC, T]), at("softplus_a", 56, [P, 3, T]), at("recip_a", 62, [P, 3, T]), at("b_over_a", 68, [P, 3, T])
        SK, SM = at("skip", 74, [P, T]), at("small", 76, [ROWS, T])
        E = [at("e0", 78, [P, HC, T]), at("e1", 86, [P, HC, T])]
        OG = at("og", 94, [P, HC, T])
        MW = 2 * HC * P + WALL
        mk = MW * 4 / KB
        RAW = [at(f"mlp_raw{a}", 48 + a * mk, [P, MW]) for a in range(2)]
        WH = [at(f"mlp_h{a}", 48 + (2 + a) * mk, [P, MW], F32R) for a in range(2)]
        WL = [at(f"mlp_l{a}", 48 + (4 + a) * mk, [P, MW], F32R) for a in range(2)]
        SG, PR = at("silu", 88, [P, T]), at("product", 90, [P, T])
        MH = [at(f"inner_h{a}", 92 + 4 * a, [P, T], F32R) for a in range(2)]
        ML = [at(f"inner_l{a}", 94 + 4 * a, [P, T], F32R) for a in range(2)]
        XD, XL, XH = at("XD", 0, [P, NF, T]), at("XL", 0, [P, NF, T], F32R), at("XH", 32, [P, NF, T], F32R)
        SRAW = [at(f"sign_raw{a}", 64 + 8 * a, [P, NF, P]) for a in range(2)]
        SH = [at(f"sign_h{a}", 80 + 8 * a, [P, NF, P], F32R) for a in range(2)]
        SL = [at(f"sign_l{a}", 96 + 8 * a, [P, NF, P], F32R) for a in range(2)]
        ps = ctx.enter_context(nc.psum_tensor("ps3", [P, 8, 512], F32))
        SMALL, X0, X1, X2 = 4, 5, 6, 7
        NE = HC + 2 * C - 1

        const = ev("const", unit=16)
        wa_raw = ev("wa_raw", unit=16)
        wa_h, wa_l = ev("wa_h"), ev("wa_l")
        hs_in, y_in = ev("hs_in", unit=16), ev("y_in", unit=16)
        yh, yl = ev("yh"), ev("yl")
        proj = ev("proj")
        small = ev("small", per=2)
        xp, relu, xr, sk = ev("xp", per=2 * NE), ev("relu", per=14), ev("xr", per=20), ev("sk", per=2)
        ln_d, ln_a, sp_d, rg = ev("ln_d", per=2), ev("ln_a", per=2), ev("sp_d", per=2), ev("rg", per=2)
        e_in, e_out = ev("e_in", per=6), ev("e_out", per=6)
        wr = ev("wr", per=2)
        y, ym, yc, sq, yv, rs, z, zh, zl = (ev("r_" + n, per=2) for n in ("y", "ym", "yc", "sq", "yv", "rs", "z", "zh", "zl"))
        raw_in = [ev(f"raw_in{a}", per=NM // 2, unit=16) for a in range(2)]
        wh, wl = ev("wh", per=NM, credit=2), ev("wl", per=NM, credit=2)
        gate, up, silu, prod, mh, ml, acc = (ev(n, per=NM) for n in ("gate", "up", "silu", "prod", "mh", "ml", "acc"))
        x_in = [ev(f"x_in{a}", per=2, unit=16) for a in range(2)]
        x2, mean2, c2, sq2, v2, rs2, n2, xh, xl = (ev("n_" + n, per=k) for n, k in
            (("x2", 4), ("mean", 1), ("c", 4), ("sq", 4), ("v", 4), ("rs", 1), ("n", 4), ("xh", 4), ("xl", 4)))
        s_in = [ev(f"s_in{a}", per=NF // 2, unit=16) for a in range(2)]
        sh, sl = ev("sh", per=NF), ev("sl", per=NF)
        ffn, fin = ev("ffn", per=NF, credit=1), ev("fin", per=NF, credit=2)
        out = [ev(f"out{a}", per=NF // 2, unit=16, credit=16) for a in range(2)]

        def bc(ap, n):
            return ap.unsqueeze(1).to_broadcast([P, n, T])

        consts = [(EX[:], io["expand"]), (RW[:], io["read2"]), (GB[:], io["read2_gb"]), (BIAS[:], io["bias"]), (DUB[:], io["du_b"])]
        RAW2 = at("wall_a_raw", 0, [P, HC, WALL])
        with nc.Block() as block:
            @block.sync
            def _(eng):
                for dst, src in consts:
                    const.fire(eng.dma_start(dst, src))
                wa_raw.fire(eng.dma_start(RAW2[:], io["wall_a"]))
                for a in range(2):
                    eng.sem_inc(out[a].sem, 16)
                with eng.Fori(0, B) as b, eng.Fori(0, L // T) as half:
                    i = b * (L // T) + half
                    for a in range(2):
                        out[a].wait(eng, i, 0)
                    ffn.wait(eng, i, 0)
                    hs_in.fire(eng.dma_start(HS[:], io["xn"][:, :, bass.ds(i * T, T)]))
                    wa_l.wait(eng)
                    y_in.fire(eng.dma_start(Y[:, 0], io["y_v"][:, bass.ds(b * HC, HC), bass.ds(half * T, T)]))

                    def load_w(m, mm, a, first):
                        if first and a == 0:
                            wr.wait(eng, i, 1)
                        if not first:
                            wh.wait(eng, i, mm - 1)
                            wl.wait(eng, i, mm - 1)
                        raw_in[a].fire(eng.dma_start(RAW[a][:], io["mlp"][bass.ds(m, 1)].rearrange("a p n -> (a p) n")))

                    for a in range(2):
                        load_w(a, a, a, True)
                    with eng.Fori(1, NM // 2) as k:
                        for a in range(2):
                            load_w(k * 2 + a, k * 2 + a, a, False)
                    for g in range(4):
                        if g >= 2:
                            x2.wait(eng, i, g - 1)
                        x_in[g % 2].fire(eng.dma_start(XR[:, g % 2], io["x"][:, g * HC:(g + 1) * HC, bass.ds(i * T, T)]))

                    def load_s(m, a):
                        s_in[a].fire(eng.dma_start(SRAW[a][:], io["sign"][bass.ds(m, 1)].rearrange("a p f o -> (a p) f o")))

                    def store(m, a):
                        fin.wait(eng, i, m + 1)
                        out[a].fire(eng.dma_start(io["out"][:, bass.ds(m, 1), bass.ds(i * T, T)], HS[:, bass.ds(m, 1)]))

                    v2.wait(eng, i, 4)
                    for a in range(2):
                        load_s(a, a)
                    with eng.Fori(1, NF // 2) as k:
                        for a in range(2):
                            m = k * 2 + a
                            sh.wait(eng, i, m - 1)
                            sl.wait(eng, i, m - 1)
                            load_s(m, a)
                            store(m - 2, a)
                    for a in range(2):
                        store(NF - 2 + a, a)
                for a in range(2):
                    out[a].wait(eng, NB - 1, NF // 2)

            @block.tensor
            def _(eng):
                eng.sem_inc(ffn.sem, 1)
                wa_h.wait(eng)
                wa_l.wait(eng)
                const.wait(eng, k=len(consts))
                with eng.Fori(0, NB) as i:
                    def three(out_ap, lh, ll, rh, rl, start, stop):
                        eng.matmul(out_ap, lh, rh, start=start, stop=False, skip_group_check=True)
                        eng.matmul(out_ap, lh, rl, start=False, stop=False, skip_group_check=True)
                        return eng.matmul(out_ap, ll, rh, start=False, stop=stop, skip_group_check=True)

                    def rows(n):
                        return slice(n * P, (n + 1) * P) if n < HC else slice(H, WALL)

                    yh.wait(eng, i)
                    yl.wait(eng, i)
                    fin.wait(eng, i, 0)
                    for n in range(HC + 1):
                        for ic in range(HC):
                            mm = three(ps[0:P if n < HC else ROWS, n], WA[0][:, ic, rows(n)], WA[1][:, ic, rows(n)],
                                       ZH[:, 0, ic], ZL[:, 0, ic], ic == 0, ic == HC - 1)
                    proj.fire(mm)

                    def expansions(w):
                        small.wait(eng, i, w + 1)
                        order = [w * HC + hc for hc in range(HC)] + [2 * HC + j for j in range(2 * C - 1)]
                        for j, e in enumerate(order):
                            if j >= 3:
                                xr.wait(eng, i, w * 10 + j - 2)
                            xp.fire(eng.matmul(ps[:, X0 + j % 3], EX[:, e], SM[:], start=True, stop=True))

                    expansions(0)
                    for o in range(2):
                        y.wait(eng, i, o + 1)
                        if o == 0:
                            sk.wait(eng, i, 1)
                        else:
                            yc.wait(eng, i, 1)
                        for hc in range(HC):
                            mm = eng.matmul(ps[:, X0], t["ones_h"][:], Y[:, o, hc], start=hc == 0, stop=hc == HC - 1)
                        ym.fire(mm)
                        sq.wait(eng, i, o + 1)
                        if o:
                            rs.wait(eng, i, 1)
                        for hc in range(HC):
                            mm = eng.matmul(ps[:, X1], t["ones_h"][:], E[o][:, hc], start=hc == 0, stop=hc == HC - 1)
                        yv.fire(mm)

                    def inner(m, a):
                        wh.wait(eng, i, m + 1)
                        wl.wait(eng, i, m + 1)
                        for o, bank, before, done in ((0, X0, silu, gate), (1, X1, prod, up)):
                            if isinstance(m, int) and m == 0:
                                zh.wait(eng, i, o + 1)
                                zl.wait(eng, i, o + 1)
                                if o == 1:
                                    rs.wait(eng, i, 2)
                            else:
                                before.wait(eng, i, m)
                            for ic in range(HC):
                                c = slice((o * HC + ic) * P, (o * HC + ic + 1) * P)
                                mm = three(ps[:, bank], WH[a][:, c], WL[a][:, c], ZH[:, o, ic], ZL[:, o, ic],
                                           ic == 0, ic == HC - 1)
                            done.fire(mm)

                    def accumulate(m, a, first, last):
                        mh.wait(eng, i, m + 1)
                        ml.wait(eng, i, m + 1)
                        if first:
                            wr.wait(eng, i, 1)
                        for n in range(HC + 1):
                            c = slice(2 * HC * P + rows(n).start, 2 * HC * P + rows(n).stop)
                            mm = three(ps[0:P if n < HC else ROWS, n], WH[a][:, c], WL[a][:, c], MH[a][:], ML[a][:], first, last)
                        acc.fire(mm)

                    inner(0, 0)
                    inner(1, 1)
                    accumulate(0, 0, True, False)
                    with eng.Fori(1, NM // 2) as k:
                        for a in range(2):
                            inner(k * 2 + a, a)
                            accumulate(k * 2 + a - 1, 1 - a, False, False)
                    accumulate(NM - 1, 1, False, True)
                    prod.wait(eng, i, NM)
                    expansions(1)
                    sk.wait(eng, i, 2)
                    xr.wait(eng, i, 20)
                    for g in range(4):
                        x2.wait(eng, i, g + 1)
                        for f in range(4 * g, 4 * g + 4):
                            mm = eng.matmul(ps[:, X0], t["ones_d"][:], HS[:, f], start=f == 0, stop=f == NF - 1)
                    mean2.fire(mm)
                    for g in range(4):
                        sq2.wait(eng, i, g + 1)
                        for f in range(4):
                            mm = eng.matmul(ps[:, X1], t["ones_d"][:], E[g % 2][:, f], start=g + f == 0, stop=g + f == 6)
                        v2.fire(mm)

                    def out_chunk(m, a):
                        sh.wait(eng, i, m + 1)
                        sl.wait(eng, i, m + 1)
                        if isinstance(m, int) and m == 0:
                            xh.wait(eng, i, 4)
                            xl.wait(eng, i, 4)
                        fin.wait(eng, i, m - 1)
                        for f in range(NF):
                            mm = three(ps[:, a], SH[a][:, f], SL[a][:, f], XH[:, f], XL[:, f], f == 0, f == NF - 1)
                        ffn.fire(mm)

                    out_chunk(0, 0)
                    out_chunk(1, 1)
                    with eng.Fori(1, NF // 2) as k:
                        for a in range(2):
                            out_chunk(k * 2 + a, a)

            @block.scalar
            def _(eng):
                eng.preload_act_table_set("natural_log_exp_and_others")
                eng.sem_inc(wh.sem, 2)
                wa_raw.wait(eng)
                wa_h.fire(eng.activation(WA[0][:], RAW2[:], ACT.Copy))
                const.wait(eng, k=len(consts))
                chain = Chain(ctx, nc, "s3_act", 9)
                with eng.Fori(0, NB) as i:
                    def link(ins):
                        chain.link(eng, i, ins)

                    y_in.wait(eng, i)
                    yh.fire(eng.activation(ZH[:, 0], Y[:, 0], ACT.Copy))

                    def write(w):
                        if w == 0:
                            proj.wait(eng, i)
                        else:
                            acc.wait(eng, i, NM)
                        small.fire(eng.activation(SM[:], ps[0:ROWS, SMALL], ACT.Identity, bias=BIAS[:, w:w + 1]))
                        for j in range(HC + 3):
                            xp.wait(eng, i, w * NE + j + 1)
                            if j < HC:
                                ins = eng.activation(DL[:, j], ps[:, X0 + j % 3], ACT.Relu, bias=DUB[:, w, j:j + 1])
                            else:
                                ins = eng.activation(SP[:, j - HC], ps[:, X0 + j % 3], ACT.Relu)
                            relu.fire(ins)
                        xr.wait(eng, i, w * 10 + HC)
                        for hc in range(HC):
                            ins = eng.activation(E[0][:, hc], E[0][:, hc], ACT.Exp, bias=DUB[:, w, hc:hc + 1])
                        link(ins)
                        ln_d.fire(eng.activation(E[0][:], E[0][:], ACT.Ln, bias=1.0))
                        xr.wait(eng, i, w * 10 + HC + 3)
                        link(eng.activation(E[1][:, 0:3], E[1][:, 0:3], ACT.Exp))
                        ln_a.fire(eng.activation(E[1][:, 0:3], E[1][:, 0:3], ACT.Ln, bias=1.0))
                        sp_d.wait(eng, i, w + 1)
                        link(eng.activation(RG[:], SP[:], ACT.Ln, bias=t["eps"][:]))
                        rg.fire(eng.activation(RG[:], RG[:], ACT.Exp, scale=-1.0))
                        xp.wait(eng, i, (w + 1) * NE)
                        sk.fire(eng.activation(SK[:], ps[:, X0 + (NE - 1) % 3], ACT.Copy))
                        for c in range(3):
                            e_in.wait(eng, i, w * 3 + c + 1)
                            e_out.fire(eng.activation(E[c % 2][:], E[c % 2][:], ACT.Exp, scale=-1.0))

                    def rstd(k, bank, done):
                        link(eng.activation(R[:, k], ps[:, bank], ACT.Ln, bias=t["eps"][:]))
                        done.fire(eng.activation(R[:, k], R[:, k], ACT.Exp, scale=-0.5))

                    write(0)
                    for o in range(2):
                        yc.wait(eng, i, o + 1)
                        if o == 0:
                            wr.wait(eng, i, 1)
                        sq.fire(eng.activation(E[o][:], Y[:, o], ACT.Square))
                        yv.wait(eng, i, o + 1)
                        rstd(o, X1, rs)

                    def z_high(o):
                        z.wait(eng, i, o + 1)
                        zh.fire(eng.activation(ZH[:, o], Y[:, o], ACT.Copy))

                    def weights(m, a, k):
                        raw_in[a].wait(eng, i, k + 1)
                        if isinstance(m, int) and m < 2:
                            yv.wait(eng, i, 2)
                        else:
                            acc.wait(eng, i, m - 1)
                        wh.fire(eng.activation(WH[a][:], RAW[a][:], ACT.Copy))

                    def inner(m, a):
                        gate.wait(eng, i, m + 1)
                        if not (isinstance(m, int) and m == 0):
                            prod.wait(eng, i, m)
                        silu.fire(eng.activation(SG[:], ps[:, X0], ACT.Silu))

                    def inner_high(m, a):
                        prod.wait(eng, i, m + 1)
                        if not (isinstance(m, int) and m < 2):
                            acc.wait(eng, i, m - 1)
                        mh.fire(eng.activation(MH[a][:], PR[:], ACT.Copy))

                    z_high(0)
                    z_high(1)
                    weights(0, 0, 0)
                    weights(1, 1, 0)
                    inner(0, 0)
                    inner_high(0, 0)
                    inner(1, 1)
                    inner_high(1, 1)
                    with eng.Fori(1, NM // 2) as k:
                        for a in range(2):
                            m = k * 2 + a
                            weights(m, a, k)
                            inner(m, a)
                            inner_high(m, a)
                    write(1)
                    for g in range(4):
                        c2.wait(eng, i, g + 1)
                        if g >= 2:
                            v2.wait(eng, i, g - 1)
                        sq2.fire(eng.activation(E[g % 2][:], XD[:, g * HC:(g + 1) * HC], ACT.Square))
                    v2.wait(eng, i, 4)
                    rstd(2, X1, rs2)
                    for g in range(4):
                        n2.wait(eng, i, g + 1)
                        xh.fire(eng.activation(XH[:, g * HC:(g + 1) * HC], XD[:, g * HC:(g + 1) * HC], ACT.Copy))

                    def signs(m, a, k):
                        s_in[a].wait(eng, i, k + 1)
                        if not (isinstance(m, int) and m < 2):
                            ffn.wait(eng, i, m - 1)
                        sh.fire(eng.activation(SH[a][:], SRAW[a][:], ACT.Copy))

                    signs(0, 0, 0)
                    signs(1, 1, 0)
                    with eng.Fori(1, NF // 2) as k:
                        for a in range(2):
                            signs(k * 2 + a, a, k)
                    chain.close()

            @block.vector
            def _(eng):
                eng.sem_inc(wl.sem, 2)
                eng.sem_inc(fin.sem, 2)
                wa_h.wait(eng)
                wa_l.fire(eng.tensor_tensor(WA[1][:], RAW2[:], WA[0][:].bitcast(F32), ALU.subtract))
                const.wait(eng, k=len(consts))
                chain = Chain(ctx, nc, "s3_dve", 38)
                TTo, STT, TS = eng.tensor_tensor, eng.scalar_tensor_tensor, eng.tensor_scalar
                with eng.Fori(0, NB) as i:
                    def link(ins):
                        chain.link(eng, i, ins)

                    yh.wait(eng, i)
                    yl.fire(TTo(ZL[:, 0], Y[:, 0], ZH[:, 0].bitcast(F32), ALU.subtract))

                    def write(w):
                        for j in range(HC + 3):
                            relu.wait(eng, i, w * 7 + j + 1)
                            src, dst = (DL[:, j], E[0][:, j]) if j < HC else (SP[:, j - HC], E[1][:, j - HC])
                            xr.fire(STT(dst, src, -2.0, ps[:, X0 + j % 3], ALU.mult, ALU.add))
                        ln_a.wait(eng, i, w + 1)
                        sp_d.fire(TTo(SP[:], SP[:], E[1][:, 0:3], ALU.add))
                        ln_d.wait(eng, i, w + 1)
                        link(TTo(DL[:], DL[:], E[0][:], ALU.add))
                        sp_d.wait(eng, i, w + 1)
                        for c in range(2):
                            e_in.fire(TTo(E[c][:], DL[:], bc(SP[:, c], HC), ALU.mult))
                        rg.wait(eng, i, w + 1)
                        for c in range(3):
                            xp.wait(eng, i, w * NE + HC + 3 + c + 1)
                            xr.fire(STT(G[:, c], ps[:, X0 + (HC + 3 + c) % 3], -1.0, RG[:, c], ALU.mult, ALU.mult))
                        if w == 0:
                            hs_in.wait(eng, i)
                        xr.wait(eng, i, w * 10 + 10)
                        for c in range(3):
                            h = HS[:, c * HC:(c + 1) * HC]
                            link(TTo(OG[:], ps[:, 0:HC], bc(G[:, c], HC), ALU.mult))
                            link(TTo(h, h, OG[:], ALU.add))
                            e_out.wait(eng, i, w * 3 + c + 1)
                            link(TTo(h, h, E[c % 2][:], ALU.mult))
                            link(TTo(h, h, OG[:], ALU.subtract))
                            if c == 0:
                                e_in.fire(TTo(E[0][:], DL[:], bc(SP[:, 2], HC), ALU.mult))
                        h = HS[:, 3 * HC:4 * HC]
                        link(TTo(OG[:], ps[:, 0:HC], DL[:], ALU.mult))
                        sk.wait(eng, i, w + 1)
                        link(TTo(OG[:], OG[:], bc(SK[:], HC), ALU.mult))
                        wr.fire(TTo(h, h, OG[:], ALU.add))
                        wr.wait(eng, i, w + 1)

                    def read(o):
                        for c in range(C):
                            for hc in range(HC):
                                ww = RW[:, hc, o, c:c + 1]
                                if c == 0:
                                    ins = TS(Y[:, o, hc], HS[:, c * HC + hc], ww, None, ALU.mult)
                                else:
                                    ins = STT(Y[:, o, hc], HS[:, c * HC + hc], ww, Y[:, o, hc], ALU.mult, ALU.add)
                            if c < C - 1:
                                link(ins)
                        y.fire(ins)

                    def centre(o):
                        ym.wait(eng, i, o + 1)
                        yc.fire(TTo(Y[:, o], Y[:, o], bc(ps[:, X0], HC), ALU.subtract))

                    def scale(o):
                        rs.wait(eng, i, o + 1)
                        link(TTo(Y[:, o], Y[:, o], bc(R[:, o], HC), ALU.mult))
                        for hc in range(HC):
                            ins = TS(Y[:, o, hc], Y[:, o, hc], GB[:, 0, o, hc:hc + 1], GB[:, 1, o, hc:hc + 1], ALU.mult, ALU.add)
                        z.fire(ins)

                    def z_low(o):
                        zh.wait(eng, i, o + 1)
                        zl.fire(TTo(ZL[:, o], Y[:, o], ZH[:, o].bitcast(F32), ALU.subtract))

                    write(0)
                    read(0)
                    read(1)
                    centre(0)
                    scale(0)
                    centre(1)
                    z_low(0)
                    scale(1)
                    z_low(1)

                    def weights_low(m, a):
                        wh.wait(eng, i, m + 1)
                        if isinstance(m, int) and m < 2:
                            yv.wait(eng, i, 2)
                        wl.fire(TTo(WL[a][:], RAW[a][:], WH[a][:].bitcast(F32), ALU.subtract))

                    def product(m, a):
                        up.wait(eng, i, m + 1)
                        silu.wait(eng, i, m + 1)
                        if not (isinstance(m, int) and m == 0):
                            mh.wait(eng, i, m)
                            ml.wait(eng, i, m)
                        prod.fire(TTo(PR[:], ps[:, X1], SG[:], ALU.mult))

                    def inner_low(m, a):
                        mh.wait(eng, i, m + 1)
                        ml.fire(TTo(ML[a][:], PR[:], MH[a][:].bitcast(F32), ALU.subtract))

                    weights_low(0, 0)
                    weights_low(1, 1)
                    for m in range(2):
                        product(m, m)
                        inner_low(m, m)
                    with eng.Fori(1, NM // 2) as k:
                        for a in range(2):
                            m = k * 2 + a
                            weights_low(m, a)
                            product(m, a)
                            inner_low(m, a)
                    write(1)
                    for g in range(4):
                        h = HS[:, g * HC:(g + 1) * HC]
                        x_in[g % 2].wait(eng, i, g // 2 + 1)
                        x2.fire(STT(h, h, t["gate"][:, 0:1], XR[:, g % 2], ALU.mult, ALU.add))
                    mean2.wait(eng, i)
                    for g in range(4):
                        c2.fire(TTo(XD[:, g * HC:(g + 1) * HC], HS[:, g * HC:(g + 1) * HC], bc(ps[:, X0], HC), ALU.subtract))
                    rs2.wait(eng, i)
                    c2.wait(eng, i, 4)
                    for g in range(4):
                        d = XD[:, g * HC:(g + 1) * HC]
                        n2.fire(TTo(d, d, bc(R[:, 2], HC), ALU.mult))
                    for g in range(4):
                        xh.wait(eng, i, g + 1)
                        xl.fire(TTo(XL[:, g * HC:(g + 1) * HC], XD[:, g * HC:(g + 1) * HC],
                                    XH[:, g * HC:(g + 1) * HC].bitcast(F32), ALU.subtract))

                    def signs_low(m, a):
                        sh.wait(eng, i, m + 1)
                        sl.fire(TTo(SL[a][:], SRAW[a][:], SH[a][:].bitcast(F32), ALU.subtract))

                    def final(m, a):
                        ffn.wait(eng, i, m + 1)
                        h = HS[:, bass.ds(m, 1)].rearrange("p a n -> p (a n)")
                        fin.fire(STT(h, ps[:, a], t["gate"][:, 1:2], h, ALU.mult, ALU.add))

                    signs_low(0, 0)
                    signs_low(1, 1)
                    with eng.Fori(1, NF // 2) as k:
                        for a in range(2):
                            signs_low(k * 2 + a, a)
                            final(k * 2 + a - 2, a)
                    final(NF - 2, 0)
                    final(NF - 1, 1)
                    chain.close()


def build(nc, args):
    io = dict(args)
    io["x"] = args["x"].rearrange("f p t -> p f t")
    io["qkv_s"] = nc.dram_tensor("qkv_scratch", [P, 3, B * NH // 2, KT, 2 * HD], F32, kind="Internal").ap()
    io["y_s"] = nc.dram_tensor("y_scratch", [B * NH, HD, L], F32, kind="Internal").ap()
    io["y_v"] = io["y_s"].rearrange("(n q) d t -> (q d) n t", q=P // HD)
    io["out"] = args["out"].rearrange("f p t -> p f t")
    io["xn"] = nc.dram_tensor("xn_scratch", [P, NF, B * L], F32, kind="Internal").ap()
    with ExitStack() as ctx:
        def sb(name, shape, dt=F32):
            return ctx.enter_context(nc.sbuf_tensor(name, shape, dt))

        t = {
            "ones_d": sb("ones_d", [P, P]), "ones_h": sb("ones_h", [P, P]), "eps": sb("eps", [P, 1]),
            "ident": sb("ident", [P, P]), "ident_r": sb("ident_r", [P, P], F32R),
            "gate": sb("gate", [P, 2]),
        }
        with ExitStack() as mid:
            def sbm(name, shape, dt=F32):
                return mid.enter_context(nc.sbuf_tensor(name, shape, dt))

            t["masks"] = sbm("masks", [P, 2, P])
            t["masks_r"] = sbm("masks_r", [P, 2, P], F32R)
            with ExitStack() as first:
                def sbf(name, shape, dt=F32):
                    return first.enter_context(nc.sbuf_tensor(name, shape, dt))

                t["cos"] = sbf("cos", [P, B * KT, HD])
                t["sin"] = sbf("sin", [P, B * KT, HD])
                t["read1"] = sbf("read1", [P, HC, 3, C])
                t["read1_gb"] = sbf("read1_gb", [P, 2, 3, HC])
                t["qkv_h"] = sbf("qkv_h", [P, 3 * HC * H], F32R)
                t["qkv_l"] = sbf("qkv_l", [P, 3 * HC * H], F32R)
                setup_phase(nc, io, t)
                read_phase(nc, io, t)
            attention_phase(nc, io, t)
        block_phase(nc, io, t)


def layouts(x, pos_BxS, ctx_1024, g_xattn, g_ffn, L0_xattn_attn_read_w, L0_xattn_attn_read_g,
            L0_xattn_attn_read_b, L0_xattn_qkv_w, L0_xattn_attn_wod_w, L0_xattn_attn_wab_w, L0_xattn_attn_wab_b,
            L0_xattn_attn_du_w, L0_xattn_attn_du_b, L0_xattn_mlp_read_w, L0_xattn_mlp_read_g, L0_xattn_mlp_read_b,
            L0_xattn_mlp_wod_w, L0_xattn_mlp_wab_w, L0_xattn_mlp_wab_b, L0_xattn_mlp_du_w, L0_xattn_mlp_du_b,
            L0_ffn_sign, L0_ffn_scale):
    import numpy as np

    def read(w, o):
        return w.reshape(HC, P, o, C).transpose(1, 0, 2, 3)

    def read_gb(g, b, o):
        return np.stack([g.reshape(o, HC, P), b.reshape(o, HC, P)]).transpose(3, 0, 1, 2)

    def small(w):
        a, bb, sk = w[:NA], w[NA:2 * NA], w[2 * NA:]
        order = [q.reshape(RH, C - 1, *q.shape[1:]).swapaxes(0, 1).reshape(NA, *q.shape[1:]) for q in (a, bb)]
        return np.concatenate([*order, sk])

    def wall(wod, wab):
        w = np.concatenate([wod, small(wab)]).T
        return w.reshape(-1, P, WALL)

    def expand(du_a, du_m):
        e = np.zeros((ROWS, NX, P), np.float32)
        e[:DR, 0:HC] = du_a.reshape(HC, P, DR).transpose(2, 0, 1)
        e[:DR, HC:2 * HC] = du_m.reshape(HC, P, DR).transpose(2, 0, 1)
        for j in range(2 * C - 1):
            for r in range(RH):
                e[DR + j * RH + r, 2 * HC + j, r::RH] = 1.0
        return e

    def small_bias(b):
        return np.concatenate([np.zeros(DR, np.float32), small(b)])

    wall_m = wall(L0_xattn_mlp_wod_w, L0_xattn_mlp_wab_w)
    up = ctx_1024.reshape(2, NM, P, HC, P).transpose(1, 4, 0, 3, 2)
    row, col = np.arange(P)[:, None], np.arange(P)[None, :]
    return {
        "x": x.reshape(B * L, HC, P, C).transpose(3, 1, 2, 0).reshape(NF, P, B * L),
        "pos": pos_BxS.reshape(B * KT, P).T,
        "inv_freq": np.broadcast_to((1.0 / 10000.0 ** (np.arange(HD // 2, dtype=np.float32) / np.float32(HD // 2))
                                     ).astype(np.float32), (P, HD // 2)),
        "gates": np.broadcast_to(np.stack([g_xattn.reshape(()), g_ffn.reshape(()), L0_ffn_scale.reshape(())]), (P, 3)),
        "ident": np.eye(P, dtype=np.float32),
        "masks": np.stack([np.where(row > col, np.float32(NEG), np.float32(0)),
                           np.where(col > row, np.float32(NEG), np.float32(0))], 1),
        "read1": read(L0_xattn_attn_read_w, 3),
        "read1_gb": read_gb(L0_xattn_attn_read_g, L0_xattn_attn_read_b, 3),
        "read2": read(L0_xattn_mlp_read_w, 2),
        "read2_gb": read_gb(L0_xattn_mlp_read_g, L0_xattn_mlp_read_b, 2),
        "qkv": L0_xattn_qkv_w.reshape(3, H, HC, P).transpose(3, 0, 2, 1).reshape(P, 3 * HC * H),
        "wall_a": wall(L0_xattn_attn_wod_w, L0_xattn_attn_wab_w).transpose(1, 0, 2),
        "expand": expand(L0_xattn_attn_du_w, L0_xattn_mlp_du_w),
        "bias": np.stack([small_bias(L0_xattn_attn_wab_b), small_bias(L0_xattn_mlp_wab_b)], 1),
        "du_b": np.stack([L0_xattn_attn_du_b.reshape(HC, P), L0_xattn_mlp_du_b.reshape(HC, P)]).transpose(2, 0, 1),
        "mlp": np.concatenate([up.reshape(NM, P, 2 * HC * P), wall_m], axis=2),
        "sign": L0_ffn_sign.reshape(HC, P, C, HC, P, C).transpose(5, 3, 1, 2, 0, 4).reshape(NF, P, NF, P),
    }


def kernel(**inputs):
    import numpy as np
    import concourse.bacc as bacc
    from concourse.bass_utils import run_bass_kernel_spmd

    arrays = {"in_" + k: np.ascontiguousarray(v) for k, v in layouts(**{k: np.asarray(v) for k, v in inputs.items()}).items()}
    nc = bacc.Bacc("TRN2", target_bir_lowering=False, num_devices=1)
    args = {k[3:]: nc.dram_tensor(k, v.shape, mybir.dt.from_np(v.dtype), kind="ExternalInput").ap()
            for k, v in arrays.items()}
    args["out"] = nc.dram_tensor("out", [NF, P, B * L], F32, kind="ExternalOutput").ap()
    build(nc, args)
    result = run_bass_kernel_spmd(nc, [arrays], core_ids=[0]).results[0]["out"]
    return result.reshape(C, HC, P, B, L).transpose(3, 4, 1, 2, 0).reshape(B, L, D)
```

```python
from contextlib import ExitStack

import concourse.bass as bass
from concourse import mybir

F32 = mybir.dt.float32
F32R = mybir.dt.float32r
I32 = mybir.dt.int32
ALU = mybir.AluOpType
ACT = mybir.ActivationFunctionType
AX = mybir.AxisListType

P = 128
B, L = 2, 1024
H, C = 512, 4
D = H * C
NF = D // P
HC = H // P
NH, HD = 16, 32
RH = 16
DR = 8
M = 2048
NM = M // P
T = 512
NB = B * L // T
TT = T // P
KT = L // P
NA = (C - 1) * RH
ROWS = DR + 2 * NA + RH
WALL = H + ROWS
NX = 2 * HC + 2 * C - 1
EPS = 1e-5
NEG = -1e30
STACK = 3 * HD


class Event:

    def __init__(self, ctx, nc, name, per=1, unit=1, credit=0):
        self.sem = ctx.enter_context(nc.semaphore(name))
        self.per, self.unit, self.credit = per, unit, credit

    def value(self, i, k):
        return i * (self.per * self.unit) + (k * self.unit + self.credit)

    def wait(self, eng, i=0, k=1):
        assert not isinstance(k, int) or k * self.unit + self.credit > 0, "a wait's value stays positive"
        eng.wait_ge(self.sem, self.value(i, k))

    def fire(self, instruction):
        instruction.then_inc(self.sem, self.unit)


def setup_phase(nc, io, t):
    with ExitStack() as ctx:
        def ev(name, **k):
            return Event(ctx, nc, "s0_" + name, **k)

        raw = ctx.enter_context(nc.sbuf_tensor("qkv_raw", [P, 3 * HC * H], F32))
        pos_i = ctx.enter_context(nc.sbuf_tensor("pos_i", [P, B * KT], I32))
        pos_f = ctx.enter_context(nc.sbuf_tensor("pos_f", [P, B * KT], F32))
        inv = ctx.enter_context(nc.sbuf_tensor("inv_freq", [P, HD // 2], F32))
        ang = ctx.enter_context(nc.sbuf_tensor("ang", [P, 2, B * KT, HD // 2], F32))
        turns = ctx.enter_context(nc.sbuf_tensor("turns", [P, 2, B * KT, HD // 2], F32))
        gates = ctx.enter_context(nc.sbuf_tensor("gates", [P, 3], F32))
        g_tmp = ctx.enter_context(nc.sbuf_tensor("g_tmp", [P, 4], F32))
        idf = t["ident"]
        loaded = ev("loaded", unit=16)
        w_loaded = ev("w_loaded", unit=16)
        high = ev("high")
        dve = ev("dve")
        act = ev("act")
        low = ev("low")
        loads = [(pos_i[:], io["pos"]), (inv[:], io["inv_freq"]), (gates[:], io["gates"]),
                 (idf[:], io["ident"]), (t["masks"][:], io["masks"]), (t["read1"][:], io["read1"]),
                 (t["read1_gb"][:], io["read1_gb"])]
        with nc.Block() as block:
            @block.sync
            def _(eng):
                for dst, src in loads:
                    loaded.fire(eng.dma_start(dst, src))
                w_loaded.fire(eng.dma_start(raw[:], io["qkv"]))
                loaded.wait(eng, k=len(loads))
                w_loaded.wait(eng)

            @block.vector
            def _(eng):
                n = 0

                def link(ins):
                    nonlocal n
                    n += 1
                    dve.fire(ins)
                    dve.wait(eng, k=n)

                link(eng.memset(t["ones_d"][:], 1.0 / D))
                link(eng.memset(t["ones_h"][:], 1.0 / H))
                link(eng.memset(t["eps"][:], EPS))
                loaded.wait(eng, k=len(loads))
                link(eng.tensor_copy(pos_f[:], pos_i[:]))
                pb = pos_f[:].unsqueeze(2).to_broadcast([P, B * KT, HD // 2])
                ib = inv[:].unsqueeze(1).to_broadcast([P, B * KT, HD // 2])
                link(eng.tensor_tensor(ang[:, 0], pb, ib, ALU.mult))
                link(eng.tensor_scalar(turns[:, 0], ang[:, 0], 1 / 6.283185307179586, None, ALU.mult))
                link(eng.tensor_scalar(turns[:, 1], turns[:, 0], 0.25, None, ALU.add))
                link(eng.tensor_scalar(turns[:], turns[:], 12582912.0, None, ALU.add))
                link(eng.tensor_scalar(turns[:], turns[:], -12582912.0, None, ALU.add))
                link(eng.tensor_scalar(ang[:, 1], ang[:, 0], 1.0, None, ALU.mult))
                for part in (6.28125, 0.0019350051879882812, 3.0199157663446e-07):
                    link(eng.scalar_tensor_tensor(ang[:], turns[:], -part, ang[:], ALU.mult, ALU.add))
                link(eng.tensor_scalar(ang[:, 1], ang[:, 1], 1.5707963267948966, None, ALU.add))
                link(eng.tensor_scalar(ang[:], ang[:], 3.1415925, -3.1415925, ALU.min, ALU.max))
                act.wait(eng, k=2)
                halves = t["cos"][:].rearrange("p t (a j) -> p t a j", a=2)
                sins = t["sin"][:].rearrange("p t (a j) -> p t a j", a=2)
                for a in range(2):
                    link(eng.tensor_copy(halves[:, :, a], turns[:, 1]))
                link(eng.tensor_scalar(sins[:, :, 0], turns[:, 0], -1.0, None, ALU.mult))
                link(eng.tensor_copy(sins[:, :, 1], turns[:, 0]))
                link(eng.tensor_scalar(g_tmp[:, 3:4], gates[:, 2:3], 0.0, None, ALU.max))
                link(eng.scalar_tensor_tensor(g_tmp[:, 2:3], g_tmp[:, 3:4], -2.0, gates[:, 2:3], ALU.mult, ALU.add))
                act.wait(eng, k=5)
                link(eng.tensor_tensor(g_tmp[:, 3:4], g_tmp[:, 3:4], g_tmp[:, 2:3], ALU.add))
                link(eng.tensor_tensor(t["gate"][:, 1:2], g_tmp[:, 1:2], g_tmp[:, 3:4], ALU.mult))
                link(eng.tensor_copy(t["gate"][:, 0:1], g_tmp[:, 0:1]))
                w_loaded.wait(eng)
                high.wait(eng)
                low.fire(eng.tensor_tensor(t["qkv_l"][:], raw[:], t["qkv_h"][:].bitcast(F32), ALU.subtract))
                low.wait(eng)

            @block.scalar
            def _(eng):
                n = 0

                def link(ins):
                    nonlocal n
                    n += 1
                    act.fire(ins)
                    act.wait(eng, k=n)

                w_loaded.wait(eng)
                high.fire(eng.activation(t["qkv_h"][:], raw[:], ACT.Copy))
                dve.wait(eng, k=15)
                link(eng.activation(turns[:, 0], ang[:, 0], ACT.Sin))
                link(eng.activation(turns[:, 1], ang[:, 1], ACT.Sin))
                loaded.wait(eng, k=len(loads))
                link(eng.activation(g_tmp[:, 0:2], gates[:, 0:2], ACT.Tanh))
                dve.wait(eng, k=21)
                link(eng.activation(g_tmp[:, 2:3], g_tmp[:, 2:3], ACT.Exp))
                link(eng.activation(g_tmp[:, 2:3], g_tmp[:, 2:3], ACT.Ln, bias=1.0))
                eng.activation(t["ident_r"][:], idf[:], ACT.Copy)
                link(eng.activation(t["masks_r"][:], t["masks"][:], ACT.Copy))


class Chain:

    def __init__(self, ctx, nc, name, per):
        self.event, self.at = Event(ctx, nc, name, per=per), 0

    def link(self, eng, i, instruction):
        self.at += 1
        self.event.fire(instruction)
        self.event.wait(eng, i, self.at)

    def start(self):
        self.at = 0

    def close(self):
        assert self.at == self.event.per, (self.at, self.event.per)


def read_phase(nc, io, t):
    with ExitStack() as ctx:
        def ev(name, **k):
            return Event(ctx, nc, "s1_" + name, **k)

        def sb(name, shape, dt=F32):
            return ctx.enter_context(nc.sbuf_tensor(name, shape, dt))

        X = sb("X", [P, NF, T])
        SQ = sb("SQ", [P, 2, HC, T])
        Y = sb("Y", [P, 3, HC, T])
        ZH = sb("ZH", [P, HC, T], F32R)
        ZL = sb("ZL", [P, HC, T], F32R)
        R = sb("R", [P, 4, T])
        RT = sb("RT", [P, 2, H])
        OUT = sb("OUT", [P, TT, H])
        ps = ctx.enter_context(nc.psum_tensor("ps1", [P, 8, 512], F32))
        MEAN, VAR, YM, YV, PJ = 0, 1, 2, 3, 4

        x_in = ev("x_in", unit=16)
        xn_out = ev("xn_out", unit=16, credit=16)
        mean, cent, var, xn = ev("mean"), ev("cent"), ev("var"), ev("xn")
        sq = ev("sq", per=7)
        sq_used = ev("sq_used", per=7, credit=1)
        rs = ev("rs", per=4)
        y = ev("y", per=3, credit=1)
        ym, yc, yv, z, zh, zl = (ev(n, per=3) for n in ("ym", "yc", "yv", "z", "zh", "zl"))
        pj = ev("pj", per=3 * TT, credit=1)
        pjq_used = ev("pjq_used", per=2 * TT)
        pjv_used = ev("pjv_used", per=TT, credit=TT)
        qk_ready = ev("qk_ready", per=2 * TT)
        stored = [ev(f"stored{tt}", per=3, unit=16, credit=16) for tt in range(TT)]

        with nc.Block() as block:
            @block.gpsimd
            def _(eng):
                with eng.Fori(0, NB) as i:
                    xn_out.wait(eng, i, 0)
                    y.wait(eng, i, 0)
                    x_in.fire(eng.dma_start(X[:], io["x"][:, :, bass.ds(i * T, T)]))

            @block.sync
            def _(eng):
                eng.sem_inc(xn_out.sem, 16)
                for tt in range(TT):
                    eng.sem_inc(stored[tt].sem, 16)
                with eng.Fori(0, B) as b, eng.Fori(0, L // T) as half:
                    i = b * (L // T) + half
                    xn.wait(eng, i)
                    xn_out.fire(eng.dma_start(io["xn"][:, :, bass.ds(i * T, T)], X[:]))
                    for o in range(3):
                        for tt in range(TT):
                            if o < 2:
                                qk_ready.wait(eng, i, o * TT + tt + 1)
                            else:
                                pjv_used.wait(eng, i, tt + 1)
                            stored[tt].fire(eng.dma_start(
                                io["qkv_s"][:, o, bass.ds(b * (NH // 2), NH // 2), bass.ds(half * TT + tt, 1), :],
                                OUT[:, tt].rearrange("p (h a d) -> p h a d", h=NH // 2, a=1)))
                xn_out.wait(eng, NB - 1)
                for tt in range(TT):
                    stored[tt].wait(eng, NB - 1, 3)

            @block.tensor
            def _(eng):
                with eng.Fori(0, NB) as i:
                    x_in.wait(eng, i)
                    for f in range(NF):
                        mm = eng.matmul(ps[:, MEAN], t["ones_d"][:], X[:, f], start=f == 0, stop=f == NF - 1)
                    mean.fire(mm)
                    for g in range(4):
                        sq.wait(eng, i, g + 1)
                        for f in range(4):
                            mm = eng.matmul(ps[:, VAR], t["ones_d"][:], SQ[:, g % 2, f],
                                            start=g + f == 0, stop=g + f == 6)
                        sq_used.fire(mm)

                    def y_mean(o):
                        y.wait(eng, i, o + 1)
                        if o:
                            yc.wait(eng, i, o)
                        for hc in range(HC):
                            mm = eng.matmul(ps[:, YM], t["ones_h"][:], Y[:, o, hc], start=hc == 0, stop=hc == HC - 1)
                        ym.fire(mm)

                    def y_var(o):
                        sq.wait(eng, i, 5 + o)
                        if o:
                            rs.wait(eng, i, o + 1)
                        for hc in range(HC):
                            mm = eng.matmul(ps[:, YV], t["ones_h"][:], SQ[:, o % 2, hc],
                                            start=hc == 0, stop=hc == HC - 1)
                        sq_used.fire(mm)

                    def project(o):
                        zh.wait(eng, i, o + 1)
                        zl.wait(eng, i, o + 1)
                        for tt in range(TT):
                            n = o * TT + tt
                            if o == 0:
                                pjv_used.wait(eng, i, n + 1 - TT)
                            else:
                                pjq_used.wait(eng, i, n + 1 - TT)
                            step = 0
                            for ic in range(HC):
                                for zz, ww in ((ZH, "qkv_h"), (ZL, "qkv_h"), (ZH, "qkv_l")):
                                    mm = eng.matmul(ps[:, PJ + tt], zz[:, ic, tt * P:(tt + 1) * P],
                                                    t[ww][:, bass.ts(o * HC + ic, H)],
                                                    start=step == 0, stop=step == 3 * HC - 1)
                                    step += 1
                            pj.fire(mm)

                    y_mean(0)
                    y_mean(1)
                    y_var(0)
                    y_mean(2)
                    y_var(1)
                    project(0)
                    y_var(2)
                    project(1)
                    project(2)

            @block.scalar
            def _(eng):
                eng.preload_act_table_set("natural_log_exp_and_others")
                eng.sem_inc(pjv_used.sem, TT)
                chain = Chain(ctx, nc, "s1_act", 4)
                with eng.Fori(0, NB) as i:
                    def square(k, out, src):
                        sq_used.wait(eng, i, max(k - 1, 0))
                        sq.fire(eng.activation(out, src, ACT.Square))

                    def rstd(k, bank):
                        chain.link(eng, i, eng.activation(R[:, k], ps[:, bank], ACT.Ln, bias=t["eps"][:]))
                        rs.fire(eng.activation(R[:, k], R[:, k], ACT.Exp, scale=-0.5))

                    cent.wait(eng, i)
                    for g in range(4):
                        square(g, SQ[:, g % 2], X[:, 4 * g:4 * g + 4])
                    sq_used.wait(eng, i, 4)
                    rstd(0, VAR)

                    def y_square(o):
                        yc.wait(eng, i, o + 1)
                        square(4 + o, SQ[:, o % 2], Y[:, o])

                    def y_rstd(o):
                        sq_used.wait(eng, i, 5 + o)
                        rstd(1 + o, YV)

                    def z_high(o):
                        z.wait(eng, i, o + 1)
                        pj.wait(eng, i, o * TT)
                        zh.fire(eng.activation(ZH[:], Y[:, o], ACT.Copy))

                    y_square(0)
                    y_square(1)
                    y_rstd(0)
                    y_square(2)
                    y_rstd(1)
                    z_high(0)
                    y_rstd(2)
                    z_high(1)
                    z_high(2)
                    for tt in range(TT):
                        pj.wait(eng, i, 2 * TT + tt + 1)
                        stored[tt].wait(eng, i, 2)
                        pjv_used.fire(eng.activation(OUT[:, tt], ps[:, PJ + tt], ACT.Copy))
                    chain.close()

            @block.vector
            def _(eng):
                eng.sem_inc(y.sem, 1)
                eng.sem_inc(sq_used.sem, 1)
                eng.sem_inc(pj.sem, 1)
                chain = Chain(ctx, nc, "s1_dve", 3 * 3 + 3)
                w, gb = t["read1"], t["read1_gb"]
                with eng.Fori(0, NB) as i:
                    mean.wait(eng, i)
                    cent.fire(eng.tensor_tensor(X[:], X[:], ps[:, MEAN].unsqueeze(1).to_broadcast([P, NF, T]), ALU.subtract))
                    rs.wait(eng, i, 1)
                    xn.fire(eng.tensor_tensor(X[:], X[:], R[:, 0].unsqueeze(1).to_broadcast([P, NF, T]), ALU.mult))
                    xn.wait(eng, i)

                    def read(o):
                        for c in range(C):
                            for hc in range(HC):
                                ww = w[:, hc, o, c:c + 1]
                                if c == 0:
                                    ins = eng.tensor_scalar(Y[:, o, hc], X[:, c * HC + hc], ww, None, ALU.mult)
                                else:
                                    ins = eng.scalar_tensor_tensor(Y[:, o, hc], X[:, c * HC + hc], ww, Y[:, o, hc],
                                                                   ALU.mult, ALU.add)
                            if c < C - 1:
                                chain.link(eng, i, ins)
                        y.fire(ins)

                    def centre(o):
                        ym.wait(eng, i, o + 1)
                        yc.fire(eng.tensor_tensor(Y[:, o], Y[:, o], ps[:, YM].unsqueeze(1).to_broadcast([P, HC, T]), ALU.subtract))

                    def scale(o):
                        rs.wait(eng, i, o + 2)
                        chain.link(eng, i, eng.tensor_tensor(Y[:, o], Y[:, o], R[:, 1 + o].unsqueeze(1).to_broadcast([P, HC, T]), ALU.mult))
                        for hc in range(HC):
                            ins = eng.tensor_scalar(Y[:, o, hc], Y[:, o, hc], gb[:, 0, o, hc:hc + 1], gb[:, 1, o, hc:hc + 1],
                                                    ALU.mult, ALU.add)
                        z.fire(ins)

                    def z_low(o):
                        zh.wait(eng, i, o + 1)
                        z.wait(eng, i, o + 1)
                        pj.wait(eng, i, o * TT)
                        zl.fire(eng.tensor_tensor(ZL[:], Y[:, o], ZH[:].bitcast(F32), ALU.subtract))

                    def rope(o):
                        for tt in range(TT):
                            pj.wait(eng, i, o * TT + tt + 1)
                            src = ps[:, PJ + tt].rearrange("p (h d) -> p h d", h=NH)
                            tile = bass.ds(i * TT + tt, 1)
                            cos = t["cos"][:, tile, :].to_broadcast([P, NH, HD])
                            sin = t["sin"][:, tile, :].to_broadcast([P, NH, HD])
                            a = RT[:, 0].rearrange("p (h d) -> p h d", h=NH)
                            b = RT[:, 1].rearrange("p (h d) -> p h d", h=NH)
                            hf = HD // 2
                            eng.tensor_tensor(a, src, cos, ALU.mult)
                            eng.tensor_tensor(b[:, :, 0:hf], src[:, :, hf:HD], sin[:, :, 0:hf], ALU.mult)
                            last = eng.tensor_tensor(b[:, :, hf:HD], src[:, :, 0:hf], sin[:, :, hf:HD], ALU.mult)
                            pjq_used.fire(last)
                            pjq_used.wait(eng, i, o * TT + tt + 1)
                            stored[tt].wait(eng, i, o)
                            qk_ready.fire(eng.tensor_tensor(OUT[:, tt], RT[:, 0], RT[:, 1], ALU.add))
                            qk_ready.wait(eng, i, o * TT + tt + 1)

                    for o in range(3):
                        read(o)
                    centre(0)
                    centre(1)
                    scale(0)
                    centre(2)
                    z_low(0)
                    scale(1)
                    rope(0)
                    z_low(1)
                    scale(2)
                    rope(1)
                    z_low(2)
                    chain.close()


def attention_phase(nc, io, t):
    with ExitStack() as ctx:
        def ev(name, **k):
            return Event(ctx, nc, "s2_" + name, **k)

        def sb(name, shape, dt=F32):
            return ctx.enter_context(nc.sbuf_tensor(name, shape, dt))

        G = [sb(f"G{n}", [P, KT, 2 * HD]) for n in "qkv"]
        S = [sb(f"stack_{n}", [P, KT, STACK], F32R) for n in "qk"]
        ST = [[sb(f"turned_{n}{a}", [STACK + 1, L], F32R) for a in range(2)] for n in "qk"]
        VO = [sb(f"v_ones{a}", [P, KT, 2 * HD]) for a in range(2)]
        zeros = sb("zeros", [P, KT, HD])
        MAXES = sb("maxes", [P, KT, 2])
        NM = sb("neg_max", [P, KT])
        NPT = 3
        PT = sb("probs", [P, NPT, T])
        RC = sb("recip", [HD, 2, T])
        OT = [sb(f"heads_out{a}", [HD, L]) for a in range(2)]
        ones = sb("ones_row", [STACK + 1, L])
        ps = ctx.enter_context(nc.psum_tensor("ps2", [P, 8, 512], F32))
        TR, MX, SC, O = 0, (1, 2, 7), (3, 4), (5, 6)

        MXP = [(q, a, min((q + 1) * P - a, T)) for q in range(KT) for a in range(0, (q + 1) * P, T)]
        SCP = [(h, k, max(k * P, h * T), (h + 1) * T - max(k * P, h * T))
               for h in range(L // T) for k in range((h + 1) * TT)]
        NMX, NSC = len(MXP), len(SCP)
        last_of = [max(p for p, x in enumerate(SCP) if x[0] == h) + 1 for h in range(L // T)]

        loaded = [ev(f"loaded_{n}", unit=16) for n in "qkv"]
        high, low, v_in = ev("high", credit=1), ev("low", credit=1), ev("v_in", credit=1)
        tr = ev("tr", per=4)
        tr_dve, tr_act = ev("tr_dve", per=2), ev("tr_act", per=2)
        mx, mx_read = ev("mx", per=NMX), ev("mx_read", per=NMX, credit=3)
        nm = ev("nm")
        row, row_out = ev("row", per=2), ev("row_out", per=2, credit=1)
        sc, ex, pv = ev("sc", per=NSC), ev("ex", per=NSC, credit=2), ev("pv", per=NSC, credit=NPT)
        o_out = ev("o_out", per=2, credit=2)
        o_ln, o_part = ev("o_ln", per=2), ev("o_part", per=2)
        stored = [ev(f"stored{a}", unit=16, credit=16) for a in range(2)]
        ready, ones_in = ev("ready"), ev("ones")

        def slots(eng, slot, first=None, last=None):
            heads = B * NH
            if first:
                first()
            slot(0, 0, 0, True, False)
            with eng.Fori(0, heads // 2 - 1) as i:
                slot(i * 2 + 1, 1, i, True, True)
                slot(i * 2 + 2, 0, i + 1, True, True)
            slot(heads - 1, 1, heads // 2 - 1, True, True)
            slot(heads, 0, heads // 2, False, True)

        with nc.Block() as block:
            @block.sync
            def _(eng):
                for a in range(2):
                    eng.sem_inc(stored[a].sem, 16)

                def load(pair, n):
                    for e in (high, low, v_in):
                        e.wait(eng, n, 0)
                    for o in range(3):
                        loaded[o].fire(eng.dma_start(G[o][:], io["qkv_s"][:, o, bass.ds(pair, 1)]))

                def slot(n, a, pair, front, back):
                    if front and a == 1 and not (isinstance(n, int)):
                        load(pair + 1, n + 1)
                    if back:
                        o_out.wait(eng, n - 1, 2)
                        stored[1 - a].fire(eng.dma_start(io["y_s"][bass.ds(n - 1, 1)].rearrange("a d t -> (a d) t"),
                                                         OT[1 - a][:]))

                load(0, 0)
                slots(eng, slot)
                for a in range(2):
                    stored[a].wait(eng, B * NH // 2 - 1)

            @block.gpsimd
            def _(eng):
                for a in range(2):
                    eng.memset(VO[a][:], 1.0)
                eng.memset(zeros[:], 0.0)
                eng.memset(MAXES[:], -3e38).then_inc(v_in.sem, 1)
                v_in.wait(eng, 0, 0)

                def take_v(n, a, pair):
                    loaded[2].wait(eng, pair)
                    pv.wait(eng, n - 1, 0)
                    v_in.fire(eng.tensor_tensor(VO[a][:, :, 0:HD], G[2][:, :, a * HD:(a + 1) * HD], zeros[:], ALU.add))

                def slot(n, a, pair, front, back):
                    if front and not (isinstance(n, int) and n == B * NH - 1):
                        take_v(n + 1, 1 - a, pair + a)

                eng.wait_ge(loaded[2].sem, 16)
                v_in.fire(eng.tensor_tensor(VO[0][:, :, 0:HD], G[2][:, :, 0:HD], zeros[:], ALU.add))
                slots(eng, slot)

            @block.tensor
            def _(eng):
                eng.sem_inc(pv.sem, NPT)
                ready.wait(eng)

                def turn(n, a, k):
                    which, half = k // 2, k % 2
                    if k == 0:
                        high.wait(eng, n)
                        low.wait(eng, n)
                        row_out.wait(eng, n, 0)
                    elif k == 2:
                        tr_act.wait(eng, n, 1)
                    else:
                        tr_dve.wait(eng, n, (k + 1) // 2)
                    for tt in range(TT):
                        mm = eng.transpose(ps[0:STACK, TR, tt * P:(tt + 1) * P].bitcast(F32R),
                                           S[which][:, half * TT + tt], t["ident_r"][:])
                    tr.fire(mm)

                def maxima(n, a, m):
                    q, k0, w = MXP[m]
                    if m == 0:
                        tr_dve.wait(eng, n, 2)
                        tr_act.wait(eng, n, 2)
                    mx_read.wait(eng, n, m - 2)
                    bank = MX[m % 3]
                    diag = k0 + w == (q + 1) * P
                    mm = eng.matmul(ps[:, bank, 0:w], ST[0][a][0:STACK, q * P:(q + 1) * P], ST[1][a][0:STACK, k0:k0 + w],
                                    start=True, stop=not diag, skip_group_check=True)
                    if diag:
                        mm = eng.matmul(ps[:, bank, w - P:w], t["ident_r"][:], t["masks_r"][:, 1], start=False, stop=True,
                                        skip_group_check=True)
                    mx.fire(mm)

                def rows(n, a):
                    nm.wait(eng, n)
                    for r in range(2):
                        if r == 0:
                            tr_act.wait(eng, n, 2)
                        else:
                            row_out.wait(eng, n, 1)
                        for tt in range(TT):
                            mm = eng.matmul(ps[STACK:STACK + 1, TR, tt * P:(tt + 1) * P], NM[:, r * TT + tt:r * TT + tt + 1],
                                            t["ident"][:], start=True, stop=True, skip_group_check=True)
                        row.fire(mm)

                def score(v, a, p):
                    h, k, q0, w = SCP[p]
                    if p == 0:
                        row_out.wait(eng, v, 2)
                    ex.wait(eng, v, p - 1)
                    diag = q0 == k * P
                    mm = eng.matmul(ps[:, SC[p % 2], 0:w], ST[1][a][:, k * P:(k + 1) * P], ST[0][a][:, q0:q0 + w],
                                    start=True, stop=not diag, skip_group_check=True)
                    if diag:
                        mm = eng.matmul(ps[:, SC[p % 2], 0:P], t["ident_r"][:], t["masks_r"][:, 0], start=False, stop=True,
                                        skip_group_check=True)
                    sc.fire(mm)

                def weigh(v, a, p):
                    h, k, q0, w = SCP[p]
                    if p == 0:
                        v_in.wait(eng, v)
                    if k == 0:
                        o_out.wait(eng, v, h - 1)
                    ex.wait(eng, v, p + 1)
                    c = q0 - h * T
                    pv.fire(eng.matmul(ps[0:2 * HD, O[h], c:c + w], VO[a][:, k], PT[:, p % NPT, 0:w],
                                       start=k == 0, stop=p + 1 == last_of[h], skip_group_check=True))

                def slot(n, a, pair, front, back):
                    m = 0
                    for p in range(NSC):
                        if front and p < 4:
                            turn(n, a, p)
                        if back:
                            score(n - 1, 1 - a, p)
                            if p:
                                weigh(n - 1, 1 - a, p - 1)
                        while front and p >= 4 and m < min(NMX, 2 * (p - 3)):
                            maxima(n, a, m)
                            m += 1
                    if back:
                        weigh(n - 1, 1 - a, NSC - 1)
                    if front:
                        rows(n, a)

                slots(eng, slot)

            @block.scalar
            def _(eng):
                eng.sem_inc(ex.sem, 2)
                eng.sem_inc(high.sem, 1)

                def take_high(n, a, pair):
                    for o in range(2):
                        loaded[o].wait(eng, pair)
                    if not (isinstance(n, int) and n == 0):
                        tr.wait(eng, n - 1, 4)
                    c = slice(a * HD, (a + 1) * HD)
                    for o, places in ((0, (0, 1)), (1, (0, 2))):
                        for j in places:
                            ins = eng.activation(S[o][:, :, j * HD:(j + 1) * HD], G[o][:, :, c], ACT.Copy)
                    high.fire(ins)

                def out(n, a, which, half, bank_event, k):
                    tr.wait(eng, n, k)
                    tr_act.fire(eng.activation(ST[which][a][0:STACK, half * T:(half + 1) * T], ps[0:STACK, TR], ACT.Copy))

                def exp(v, a, p):
                    h, k, q0, w = SCP[p]
                    sc.wait(eng, v, p + 1)
                    pv.wait(eng, v, p + 1 - NPT)
                    ex.fire(eng.activation(PT[:, p % NPT, 0:w], ps[:, SC[p % 2], 0:w], ACT.Exp, scale=HD ** -0.5))

                def recip(v, h):
                    pv.wait(eng, v, last_of[h])
                    o_out.wait(eng, v, h - 1)
                    o_ln.fire(eng.activation(RC[:, h], ps[HD:2 * HD, O[h]], ACT.Ln))
                    o_ln.wait(eng, v, h + 1)
                    o_part.fire(eng.activation(RC[:, h], RC[:, h], ACT.Exp, scale=-1.0))

                def slot(n, a, pair, front, back):
                    for p in range(NSC):
                        if back:
                            exp(n - 1, 1 - a, p)
                        if back and p == 6:
                            recip(n - 1, 0)
                        if front and p == 0:
                            out(n, a, 0, 1, tr_act, 2)
                        if front and p == 2:
                            out(n, a, 1, 1, tr_act, 4)
                        if front and p == 5 and not (isinstance(n, int) and n == B * NH - 1):
                            take_high(n + 1, 1 - a, pair + a)
                    if back:
                        recip(n - 1, 1)

                eng.preload_act_table_set("natural_log_exp_and_others")
                take_high(0, 0, 0)
                slots(eng, slot)

            @block.vector
            def _(eng):
                eng.sem_inc(low.sem, 1)
                eng.sem_inc(mx_read.sem, 3)
                eng.sem_inc(row_out.sem, 1)
                eng.sem_inc(o_out.sem, 2)
                ones_in.fire(eng.memset(ones[:], 1.0))
                ones_in.wait(eng)
                for a in range(2):
                    ins = eng.tensor_copy(ST[1][a][STACK:STACK + 1, :], ones[STACK:STACK + 1, :])
                ready.fire(ins)

                def take_low(n, a, pair):
                    high.wait(eng, n)
                    if not (isinstance(n, int) and n == 0):
                        tr.wait(eng, n - 1, 4)
                    c = slice(a * HD, (a + 1) * HD)
                    for o, place in ((0, 2), (1, 1)):
                        ins = eng.tensor_tensor(S[o][:, :, place * HD:(place + 1) * HD], G[o][:, :, c],
                                                S[o][:, :, 0:HD].bitcast(F32), ALU.subtract)
                    low.fire(ins)

                def out(n, a, which, half, k):
                    tr.wait(eng, n, k)
                    tr_dve.fire(eng.tensor_copy(ST[which][a][0:STACK, half * T:(half + 1) * T], ps[0:STACK, TR]))

                def row_max(n, m):
                    q, k0, w = MXP[m]
                    mx.wait(eng, n, m + 1)
                    mx_read.fire(eng.tensor_reduce(MAXES[:, q, k0 // T:k0 // T + 1], ps[:, MX[m % 3], 0:w], AX.X, ALU.max))

                def head_out(v, a, h, pair):
                    pv.wait(eng, v, last_of[h])
                    if h == 0:
                        stored[a].wait(eng, pair, 0)
                    o_part.wait(eng, v, h + 1)
                    o_out.fire(eng.tensor_tensor(OT[a][:, h * T:(h + 1) * T], ps[0:HD, O[h]], RC[:, h], ALU.mult))

                def slot(n, a, pair, front, back):
                    if front:
                        out(n, a, 0, 0, 1)
                        out(n, a, 1, 0, 3)
                        for m in range(4):
                            row_max(n, m)
                    if back:
                        head_out(n - 1, 1 - a, 0, pair - 1 + a)
                    if front:
                        for m in range(4, 6):
                            row_max(n, m)
                        if not (isinstance(n, int) and n == B * NH - 1):
                            take_low(n + 1, 1 - a, pair + a)
                        for m in range(6, NMX):
                            row_max(n, m)
                        mx_read.wait(eng, n, NMX)
                        nm.fire(eng.tensor_reduce(NM[:], MAXES[:], AX.X, ALU.max, negate=True))
                        for r in range(2):
                            row.wait(eng, n, r + 1)
                            row_out.fire(eng.tensor_copy(ST[0][a][STACK:STACK + 1, r * T:(r + 1) * T],
                                                         ps[STACK:STACK + 1, TR]))
                    if back:
                        head_out(n - 1, 1 - a, 1, pair - 1 + a)

                take_low(0, 0, 0)
                slots(eng, slot)


def block_phase(nc, io, t):
    with ExitStack() as ctx:
        def ev(name, **k):
            return Event(ctx, nc, "s3_" + name, **k)

        def sb(name, shape, dt=F32):
            return ctx.enter_context(nc.sbuf_tensor(name, shape, dt))

        KB = 1024
        EX = sb("expand_sb", [ROWS, NX, P])
        RW, GB = sb("read2_sb", [P, HC, 2, C]), sb("read2_gb_sb", [P, 2, 2, HC])
        BIAS, DUB = sb("bias_sb", [ROWS, 2]), sb("du_b_sb", [P, 2, HC])
        HS = sb("hidden", [P, NF, T])
        R2 = sb("rstd_gate", [P, T])
        RES = [sb(f"residual{a}", [P, T]) for a in range(2)]
        UW = 2 * HC * P
        uk, pk = UW * 4 / KB, WALL * 4 / KB
        raw_u0, raw_p0 = sb("up_raw0", [P, UW]), sb("proj_raw0", [P, WALL])

        def arena(name, kb):
            base = (nc.sbuf_base + 31) // 32 * 32
            sb(name, [P, kb * KB // 4])
            return lambda n, at, shape, dt=F32: nc.alloc_sbuf_tensor_at(n, shape, dt, offset=base + int(at * KB))

        a_y, a_z, a_e, a_f = (arena(n, kb) for n, kb in (("place_y", 16), ("place_z", 32), ("place_e", 16), ("place_f", 88)))
        YIN, YL, YH = a_y("y_raw", 0, [P, HC, T]), a_y("y_low", 0, [P, HC, T], F32R), a_y("y_high", 8, [P, HC, T], F32R)
        Y, XR = a_y("Y2", 0, [P, 2, HC, T]), a_y("x_piece", 0, [P, 2, HC, T])
        WA = [a_z(f"wall_a{n}", k * HC * pk, [P, HC, WALL], F32R) for k, n in enumerate("hl")]
        WRAW = a_z("wall_a_raw", 2 * HC * pk, [P, HC, WALL])
        DL, OG = a_z("delta", 0, [P, HC, T]), a_z("og", 8, [P, HC, T])
        SP, RG = a_z("softplus_a", 16, [P, 3, T]), a_z("b_over_a", 22, [P, 3, T])
        SK, SM = a_z("skip", 28, [P, T]), a_z("small", 30, [ROWS, T])
        ZH, ZL = a_z("ZH2", 0, [P, 2, HC, T], F32R), a_z("ZL2", 16, [P, 2, HC, T], F32R)
        R = a_z("rstd_read", 28, [P, 2, T])
        E = [a_e("e0", 0, [P, HC, T]), a_e("e1", 8, [P, HC, T])]
        XD, XL, XH = a_f("XD", 0, [P, NF, T]), a_f("XL", 0, [P, NF, T], F32R), a_f("XH", 32, [P, NF, T], F32R)
        SRAW, SH, SL = ([a_f(f"sign_{n}{a}", 64 + 8 * k + 4 * a, [P, NF // 2, P], d) for a in range(2)]
                        for k, (n, d) in enumerate((("raw", F32), ("h", F32R), ("l", F32R))))
        SQ = [E[0], E[1], a_f("sq2", 72, [P, HC, T]), a_f("sq3", 80, [P, HC, T])]
        RAWU, RAWP = [raw_u0, a_f("up_raw1", 0, [P, UW])], [raw_p0, a_f("proj_raw1", uk, [P, WALL])]
        f = uk + pk
        UH, UL = ([a_f(f"up_{n}{a}", f + (2 * k + a) * uk, [P, UW], F32R) for a in range(2)] for k, n in enumerate("hl"))
        f += 4 * uk
        PH, PL = ([a_f(f"proj_{n}{a}", f + (2 * k + a) * pk, [P, WALL], F32R) for a in range(2)] for k, n in enumerate("hl"))
        f += 4 * pk
        SG, PR = a_f("silu", f, [P, T]), a_f("product", f + 2, [P, T])
        MH, ML = ([a_f(f"inner_{n}{a}", f + 4 + 2 * (2 * k + a), [P, T], F32R) for a in range(2)] for k, n in enumerate("hl"))
        assert f + 12 <= 64
        ps = ctx.enter_context(nc.psum_tensor("ps3", [P, 8, 512], F32))
        SMALL, X0, X1, FB = 4, 5, 6, (4, 7)
        NE = HC + 2 * C - 1

        const = ev("const", unit=16)
        y_in, w_in = ev("y_in", unit=16), ev("w_in", unit=16)
        hs_in = [ev(f"hs_in{g}", unit=16) for g in range(4)]
        yh, yl, wah, wal, proj = (ev(n) for n in ("yh", "yl", "wah", "wal", "proj"))
        small = ev("small", per=2)
        xp, relu, xr, sk = ev("xp", per=2 * NE), ev("relu", per=14), ev("xr", per=20), ev("sk", per=2)
        ln_d, ln_a, sp_d, rg = ev("ln_d", per=2), ev("ln_a", per=2), ev("sp_d", per=2), ev("rg", per=2)
        e_in, e_out = ev("e_in", per=6), ev("e_out", per=6)
        wr = ev("wr", per=2)
        y, ym, yc, sq, yv, rs, z, zh, zl = (ev("r_" + n, per=2) for n in ("y", "ym", "yc", "sq", "yv", "rs", "z", "zh", "zl"))
        up_in = [ev(f"up_in{a}", per=NM // 2, unit=16) for a in range(2)]
        proj_in = [ev(f"proj_in{a}", per=NM // 2, unit=16) for a in range(2)]
        uh, ul, ph, pl = (ev(n, per=NM) for n in ("uh", "ul", "ph", "pl"))
        gate, up, silu, prod, mh, ml, acc = (ev(n, per=NM) for n in ("gate", "up", "silu", "prod", "mh", "ml", "acc"))
        x_in = [ev(f"x_in{a}", per=2, unit=16) for a in range(2)]
        x2, mean2, c2, xh, sq2, xl, sum2, v2, rs2, gated = (ev("n_" + n, per=k) for n, k in
            (("x2", 4), ("mean", 1), ("c", 4), ("xh", 4), ("sq", 4), ("xl", 4), ("sum", 3), ("v", 1), ("rs", 1), ("gated", 1)))
        x2_out = [ev(f"x2_out{g}", unit=16) for g in range(4)]
        s_in = [ev(f"s_in{a}", per=NF, unit=16) for a in range(2)]
        sh, sl = ev("sh", per=2 * NF), ev("sl", per=2 * NF, credit=1)
        ffn_half, ffn, fin = ev("ffn_half", per=NF), ev("ffn", per=NF), ev("fin", per=NF)
        res_in = [ev(f"res_in{a}", per=NF // 2, unit=16) for a in range(2)]
        out = [ev(f"out{a}", per=NF // 2, unit=16) for a in range(2)]

        def bc(ap, n):
            return ap.unsqueeze(1).to_broadcast([P, n, T])

        def blocks(eng, body, drain=None):
            body(0, None)
            with eng.Fori(1, NB) as i:
                body(i, i - 1)
            if drain:
                drain(NB - 1)

        def tokens(i):
            return bass.ds(i * T, T)

        consts = [(EX[:], io["expand"]), (RW[:], io["read2"]), (GB[:], io["read2_gb"]), (BIAS[:], io["bias"]), (DUB[:], io["du_b"])]
        with nc.Block() as block:
            @block.sync
            def _(eng):
                for dst, src in consts:
                    const.fire(eng.dma_start(dst, src))

                def signs(j):
                    def load(m, first=False):
                        for a in range(2):
                            sl.wait(eng, j, 0 if first else m * 2 + a - 1)
                            s_in[a].fire(eng.dma_start(SRAW[a][:], io["sign"][bass.ds(m, 1), :, a * (NF // 2):(a + 1) * (NF // 2)]
                                                       .rearrange("a p f o -> (a p) f o")))

                    load(0, True)
                    with eng.Fori(1, NF) as m:
                        load(m)

                def body(i, j):
                    if j is not None:
                        wr.wait(eng, j, 2)
                    w_in.fire(eng.dma_start(WRAW[:], io["wall_a"]))
                    if j is not None:
                        x2.wait(eng, j, 4)
                    if isinstance(i, int):
                        b, half = divmod(i, L // T)
                        y_in.fire(eng.dma_start(YIN[:], io["y_v"][:, b * HC:(b + 1) * HC, half * T:(half + 1) * T]))
                    else:
                        b = i // 2
                        y_in.fire(eng.dma_start(YIN[:], io["y_v"][:, bass.ds(b * HC, HC), bass.ds((i % 2) * T, T)]))
                    for g in range(4):
                        if j is not None:
                            x2_out[g].wait(eng, j)
                            mean2.wait(eng, j)
                            c2.wait(eng, j, 4)
                        hs_in[g].fire(eng.dma_start(HS[:, g * HC:(g + 1) * HC], io["xn"][:, g * HC:(g + 1) * HC, tokens(i)]))
                    if j is not None:
                        signs(j)

                    def load_up(m, a):
                        if a == 0 and isinstance(m, int):
                            if j is not None:
                                ul.wait(eng, j, NM)
                        elif isinstance(m, int):
                            if j is not None:
                                ffn.wait(eng, j, NF)
                        else:
                            uh.wait(eng, i, m - 1)
                            ul.wait(eng, i, m - 1)
                        up_in[a].fire(eng.dma_start(RAWU[a][:], io["mlp_up"][bass.ds(m, 1)].rearrange("a p n -> (a p) n")))

                    def load_proj(m, a):
                        if not isinstance(m, int):
                            ph.wait(eng, i, m - 1)
                            pl.wait(eng, i, m - 1)
                        proj_in[a].fire(eng.dma_start(RAWP[a][:], io["mlp_proj"][bass.ds(m, 1)].rearrange("a p n -> (a p) n")))

                    def load_x(g):
                        x_in[g % 2].fire(eng.dma_start(XR[:, g % 2], io["x"][:, g * HC:(g + 1) * HC, tokens(i)]))

                    load_up(0, 0)
                    load_proj(0, 0)
                    load_up(1, 1)
                    load_proj(1, 1)
                    zl.wait(eng, i, 2)
                    for g in range(2):
                        load_x(g)
                    with eng.Fori(1, NM // 2) as k:
                        for a in range(2):
                            load_up(k * 2 + a, a)
                            load_proj(k * 2 + a, a)
                    for g in range(4):
                        x2.wait(eng, i, g + 1)
                        if g < 2:
                            load_x(g + 2)
                        x2_out[g].fire(eng.dma_start(io["x2"][:, g * HC:(g + 1) * HC, tokens(i)], HS[:, g * HC:(g + 1) * HC]))

                blocks(eng, body, signs)
                for g in range(4):
                    x2_out[g].wait(eng, NB - 1)

            @block.gpsimd
            def _(eng):
                eng.sem_inc(sl.sem, 1)

                def signs(j):
                    def low(m):
                        for a in range(2):
                            sh.wait(eng, j, m * 2 + a + 1)
                            sl.fire(eng.tensor_tensor(SL[a][:], SRAW[a][:], SH[a][:].bitcast(F32), ALU.subtract))

                    def residual(m, a):
                        res_in[a].fire(eng.dma_start(RES[a][:], io["x2"][:, bass.ds(m, 1), tokens(j)].rearrange("p a n -> p (a n)")))

                    def store(m, a):
                        fin.wait(eng, j, m + 1)
                        out[a].fire(eng.dma_start(io["out"][:, bass.ds(m, 1), tokens(j)].rearrange("p a n -> p (a n)"), RES[a][:]))

                    for g in range(4):
                        x2_out[g].wait(eng, j)
                    for a in range(2):
                        residual(a, a)
                        low(a)
                    with eng.Fori(1, NF // 2) as k:
                        for a in range(2):
                            m = k * 2 + a
                            store(m - 2, a)
                            low(m)
                            out[a].wait(eng, j, k)
                            residual(m, a)
                    for a in range(2):
                        store(NF - 2 + a, a)
                    for a in range(2):
                        out[a].wait(eng, j, NF // 2)

                with eng.Fori(0, NB) as j:
                    signs(j)

            @block.tensor
            def _(eng):
                const.wait(eng, k=len(consts))

                def three(out_ap, lh, ll, rh, rl, start, stop):
                    eng.matmul(out_ap, lh, rh, start=start, stop=False, skip_group_check=True)
                    eng.matmul(out_ap, lh, rl, start=False, stop=False, skip_group_check=True)
                    return eng.matmul(out_ap, ll, rh, start=False, stop=stop, skip_group_check=True)

                def rows(n):
                    return slice(n * P, (n + 1) * P) if n < HC else slice(H, WALL)

                def variance(j):
                    sum2.wait(eng, j, 3)
                    for f in range(HC):
                        mm = eng.matmul(ps[:, X1], t["ones_d"][:], SQ[0][:, f], start=f == 0, stop=f == HC - 1)
                    v2.fire(mm)

                def signs(j, i, first, last):
                    def chunk(m, a):
                        for half in range(2):
                            sh.wait(eng, j, m * 2 + half + 1)
                            sl.wait(eng, j, m * 2 + half + 1)
                            for f in range(NF // 2):
                                n = half * (NF // 2) + f
                                mm = three(ps[:, FB[a]], SH[half][:, f], SL[half][:, f], XH[:, n], XL[:, n], n == 0, n == NF - 1)
                            if half == 0:
                                ffn_half.fire(mm)
                        ffn.fire(mm)

                    if first == 0:
                        xh.wait(eng, j, 4)
                        xl.wait(eng, j, 4)
                        if i is not None:
                            small.wait(eng, i, 1)
                        chunk(0, 0)
                        chunk(1, 1)
                        first = 2
                    with eng.Fori(first // 2, last // 2) as k:
                        for a in range(2):
                            fin.wait(eng, j, k * 2 + a - 1)
                            chunk(k * 2 + a, a)

                def body(i, j):
                    for e in (yh, yl, wah, wal):
                        e.wait(eng, i)
                    if j is not None:
                        wr.wait(eng, j, 2)
                    for n in range(HC + 1):
                        for ic in range(HC):
                            mm = three(ps[0:P if n < HC else ROWS, n], WA[0][:, ic, rows(n)], WA[1][:, ic, rows(n)],
                                       YH[:, ic], YL[:, ic], ic == 0, ic == HC - 1)
                    proj.fire(mm)
                    if j is not None:
                        variance(j)

                    def expansions(w):
                        small.wait(eng, i, w + 1)
                        order = [w * HC + hc for hc in range(HC)] + [2 * HC + q for q in range(2 * C - 1)]
                        for n, e in enumerate(order):
                            if n >= 2:
                                xr.wait(eng, i, w * 10 + n - 1)
                            elif w == 0 and j is not None:
                                if n == 0:
                                    c2.wait(eng, j, 4)
                                else:
                                    rs2.wait(eng, j)
                            xp.fire(eng.matmul(ps[:, X0 + n % 2], EX[:, e], SM[:], start=True, stop=True))

                    expansions(0)
                    if j is not None:
                        signs(j, i, 0, 6)
                    sk.wait(eng, i, 1)
                    xr.wait(eng, i, 10)
                    for o in range(2):
                        y.wait(eng, i, o + 1)
                        for hc in range(HC):
                            mm = eng.matmul(ps[:, X0 + o], t["ones_h"][:], Y[:, o, hc], start=hc == 0, stop=hc == HC - 1)
                        ym.fire(mm)
                    if j is not None:
                        signs(j, i, 6, 8)
                    for o in range(2):
                        yc.wait(eng, i, o + 1)
                        sq.wait(eng, i, o + 1)
                        for hc in range(HC):
                            mm = eng.matmul(ps[:, X0 + o], t["ones_h"][:], E[o][:, hc], start=hc == 0, stop=hc == HC - 1)
                        yv.fire(mm)
                    if j is not None:
                        signs(j, i, 8, NF)
                        fin.wait(eng, j, NF)

                    def inner(m, a):
                        uh.wait(eng, i, m + 1)
                        ul.wait(eng, i, m + 1)
                        for o, bank, before, done in ((0, X0, silu, gate), (1, X1, prod, up)):
                            if isinstance(m, int) and m == 0:
                                zh.wait(eng, i, o + 1)
                                zl.wait(eng, i, o + 1)
                                rs.wait(eng, i, o + 1)
                            else:
                                before.wait(eng, i, m)
                            for ic in range(HC):
                                c = slice((o * HC + ic) * P, (o * HC + ic + 1) * P)
                                mm = three(ps[:, bank], UH[a][:, c], UL[a][:, c], ZH[:, o, ic], ZL[:, o, ic],
                                           ic == 0, ic == HC - 1)
                            done.fire(mm)

                    def accumulate(m, a, first, last):
                        for e in (ph, pl, mh, ml):
                            e.wait(eng, i, m + 1)
                        if first:
                            wr.wait(eng, i, 1)
                        for n in range(HC + 1):
                            mm = three(ps[0:P if n < HC else ROWS, n], PH[a][:, rows(n)], PL[a][:, rows(n)], MH[a][:], ML[a][:], first, last)
                        acc.fire(mm)

                    inner(0, 0)
                    inner(1, 1)
                    accumulate(0, 0, True, False)
                    with eng.Fori(1, NM // 2) as k:
                        for a in range(2):
                            inner(k * 2 + a, a)
                            accumulate(k * 2 + a - 1, 1 - a, False, False)
                    accumulate(NM - 1, 1, False, True)
                    prod.wait(eng, i, NM)
                    expansions(1)
                    sk.wait(eng, i, 2)
                    xr.wait(eng, i, 20)
                    for g in range(4):
                        x2.wait(eng, i, g + 1)
                        for f in range(4 * g, 4 * g + 4):
                            mm = eng.matmul(ps[:, X0], t["ones_d"][:], HS[:, f], start=f == 0, stop=f == NF - 1)
                    mean2.fire(mm)

                def drain(j):
                    variance(j)
                    signs(j, None, 0, NF)

                blocks(eng, body, drain)

            @block.scalar
            def _(eng):
                eng.preload_act_table_set("natural_log_exp_and_others")
                const.wait(eng, k=len(consts))
                chain = Chain(ctx, nc, "s3_act", 8)
                norm_chain = Chain(ctx, nc, "s3_act_norm", 1)

                def squares(j):
                    for g in range(4):
                        c2.wait(eng, j, g + 1)
                        sq2.fire(eng.activation(SQ[g][:], XD[:, g * HC:(g + 1) * HC], ACT.Square))

                def norm(j):
                    norm_chain.start()
                    v2.wait(eng, j)
                    norm_chain.link(eng, j, eng.activation(R2[:], ps[:, X1], ACT.Ln, bias=t["eps"][:]))
                    rs2.fire(eng.activation(R2[:], R2[:], ACT.Exp, scale=-0.5))
                    norm_chain.close()

                def sign_high(j, m, first=False):
                    for a in range(2):
                        s_in[a].wait(eng, j, m + 1)
                        if first:
                            sum2.wait(eng, j, 2)
                        else:
                            (ffn_half, ffn)[a].wait(eng, j, m)
                        sh.fire(eng.activation(SH[a][:], SRAW[a][:], ACT.Copy))

                def body(i, j):
                    chain.start()

                    def link(ins):
                        chain.link(eng, i, ins)

                    w_in.wait(eng, i)
                    wah.fire(eng.activation(WA[0][:], WRAW[:], ACT.Copy))
                    y_in.wait(eng, i)
                    yh.fire(eng.activation(YH[:], YIN[:], ACT.Copy))
                    if j is not None:
                        squares(j)
                        sign_high(j, 0, True)

                    def write(w):
                        if w == 0:
                            proj.wait(eng, i)
                        else:
                            acc.wait(eng, i, NM)
                        small.fire(eng.activation(SM[:], ps[0:ROWS, SMALL], ACT.Identity, bias=BIAS[:, w:w + 1]))
                        if w == 0 and j is not None:
                            norm(j)
                        for n in range(HC + 3):
                            xp.wait(eng, i, w * NE + n + 1)
                            if n < HC:
                                ins = eng.activation(DL[:, n], ps[:, X0 + n % 2], ACT.Relu, bias=DUB[:, w, n:n + 1])
                            else:
                                ins = eng.activation(SP[:, n - HC], ps[:, X0 + n % 2], ACT.Relu)
                            relu.fire(ins)
                        xr.wait(eng, i, w * 10 + HC)
                        for hc in range(HC):
                            ins = eng.activation(E[0][:, hc], E[0][:, hc], ACT.Exp, bias=DUB[:, w, hc:hc + 1])
                        link(ins)
                        ln_d.fire(eng.activation(E[0][:], E[0][:], ACT.Ln, bias=1.0))
                        xr.wait(eng, i, w * 10 + HC + 3)
                        link(eng.activation(E[1][:, 0:3], E[1][:, 0:3], ACT.Exp))
                        ln_a.fire(eng.activation(E[1][:, 0:3], E[1][:, 0:3], ACT.Ln, bias=1.0))
                        sp_d.wait(eng, i, w + 1)
                        link(eng.activation(RG[:], SP[:], ACT.Ln, bias=t["eps"][:]))
                        rg.fire(eng.activation(RG[:], RG[:], ACT.Exp, scale=-1.0))
                        xp.wait(eng, i, (w + 1) * NE)
                        sk.fire(eng.activation(SK[:], ps[:, X0 + (NE - 1) % 2], ACT.Copy))
                        for c in range(3):
                            if c == 2 and w == 0 and j is not None:
                                sign_high(j, 1)
                            e_in.wait(eng, i, w * 3 + c + 1)
                            e_out.fire(eng.activation(E[c % 2][:], E[c % 2][:], ACT.Exp, scale=-1.0))

                    write(0)
                    if j is not None:
                        for m in range(2, 6):
                            sign_high(j, m)
                    for o in range(2):
                        yc.wait(eng, i, o + 1)
                        wr.wait(eng, i, 1)
                        sq.fire(eng.activation(E[o][:], Y[:, o], ACT.Square))
                    if j is not None:
                        for m in range(6, 9):
                            sign_high(j, m)
                    for o in range(2):
                        yv.wait(eng, i, o + 1)
                        link(eng.activation(R[:, o], ps[:, X0 + o], ACT.Ln, bias=t["eps"][:]))
                        rs.fire(eng.activation(R[:, o], R[:, o], ACT.Exp, scale=-0.5))
                    for o in range(2):
                        z.wait(eng, i, o + 1)
                        zh.fire(eng.activation(ZH[:, o], Y[:, o], ACT.Copy))
                        if o == 0 and j is not None:
                            sign_high(j, 9)
                    if j is not None:
                        with eng.Fori(10, NF) as m:
                            sign_high(j, m)

                    def up_high(m, a, k):
                        up_in[a].wait(eng, i, k + 1)
                        if isinstance(m, int) and m < 2:
                            if j is not None:
                                ffn.wait(eng, j, NF)
                        else:
                            up.wait(eng, i, m - 1)
                        uh.fire(eng.activation(UH[a][:], RAWU[a][:], ACT.Copy))

                    def proj_high(m, a, k):
                        proj_in[a].wait(eng, i, k + 1)
                        if not (isinstance(m, int) and m < 2):
                            acc.wait(eng, i, m - 1)
                        ph.fire(eng.activation(PH[a][:], RAWP[a][:], ACT.Copy))

                    def inner(m, a):
                        gate.wait(eng, i, m + 1)
                        if not (isinstance(m, int) and m == 0):
                            prod.wait(eng, i, m)
                        silu.fire(eng.activation(SG[:], ps[:, X0], ACT.Silu))

                    def inner_high(m, a):
                        prod.wait(eng, i, m + 1)
                        if not (isinstance(m, int) and m < 2):
                            acc.wait(eng, i, m - 1)
                        mh.fire(eng.activation(MH[a][:], PR[:], ACT.Copy))

                    def inner_chunk(m, a, k, last=False):
                        if not last:
                            up_high(m + 1, 1 - a, k + a)
                        proj_high(m, a, k)
                        inner(m, a)
                        inner_high(m, a)

                    up_high(0, 0, 0)
                    inner_chunk(0, 0, 0)
                    with eng.Fori(0, NM // 2 - 1) as k:
                        inner_chunk(k * 2 + 1, 1, k)
                        inner_chunk(k * 2 + 2, 0, k + 1)
                    inner_chunk(NM - 1, 1, NM // 2 - 1, True)
                    write(1)
                    for g in range(4):
                        c2.wait(eng, i, g + 1)
                        xh.fire(eng.activation(XH[:, g * HC:(g + 1) * HC], XD[:, g * HC:(g + 1) * HC], ACT.Copy))
                    chain.close()

                def drain(j):
                    squares(j)
                    sign_high(j, 0, True)
                    norm(j)
                    with eng.Fori(1, NF) as m:
                        sign_high(j, m)

                blocks(eng, body, drain)

            @block.vector
            def _(eng):
                const.wait(eng, k=len(consts))
                chain = Chain(ctx, nc, "s3_dve", 38)
                fin_chain = Chain(ctx, nc, "s3_fin_product", NF)
                TTo, STT, TS = eng.tensor_tensor, eng.scalar_tensor_tensor, eng.tensor_scalar

                def low_and_sum(j):
                    for g in range(4):
                        d = slice(g * HC, (g + 1) * HC)
                        xh.wait(eng, j, g + 1)
                        sq2.wait(eng, j, g + 1)
                        xl.fire(TTo(XL[:, d], XD[:, d], XH[:, d].bitcast(F32), ALU.subtract))
                    for g in range(2):
                        sum2.fire(TTo(SQ[g][:], SQ[g][:], SQ[g + 2][:], ALU.add))
                    sum2.wait(eng, j, 2)
                    sum2.fire(TTo(SQ[0][:], SQ[0][:], SQ[1][:], ALU.add))
                    sum2.wait(eng, j, 3)

                def gate_norm(j):
                    rs2.wait(eng, j)
                    gated.fire(TS(R2[:], R2[:], t["gate"][:, 1:2], None, ALU.mult))
                    gated.wait(eng, j)

                def final(j, m, a, k):
                    ffn.wait(eng, j, m + 1)
                    res_in[a].wait(eng, j, k + 1)
                    ins = TTo(ps[:, FB[a]], ps[:, FB[a]], R2[:], ALU.mult)
                    fin_chain.event.fire(ins)
                    fin_chain.event.wait(eng, j, m + 1)
                    fin.fire(TTo(RES[a][:], RES[a][:], ps[:, FB[a]], ALU.add))

                def body(i, j):
                    chain.start()

                    def link(ins):
                        chain.link(eng, i, ins)

                    def some_final(*ms):
                        if j is not None:
                            for m in ms:
                                final(j, m, m % 2, m // 2)

                    wah.wait(eng, i)
                    wal.fire(TTo(WA[1][:], WRAW[:], WA[0][:].bitcast(F32), ALU.subtract))
                    yh.wait(eng, i)
                    yl.fire(TTo(YL[:], YIN[:], YH[:].bitcast(F32), ALU.subtract))
                    if j is not None:
                        low_and_sum(j)

                    def write(w):
                        proj.wait(eng, i) if w == 0 else acc.wait(eng, i, NM)
                        for n in range(HC + 3):
                            relu.wait(eng, i, w * 7 + n + 1)
                            src, dst = (DL[:, n], E[0][:, n]) if n < HC else (SP[:, n - HC], E[1][:, n - HC])
                            xr.fire(STT(dst, src, -2.0, ps[:, X0 + n % 2], ALU.mult, ALU.add))
                        if w == 0 and j is not None:
                            gate_norm(j)
                        ln_a.wait(eng, i, w + 1)
                        sp_d.fire(TTo(SP[:], SP[:], E[1][:, 0:3], ALU.add))
                        ln_d.wait(eng, i, w + 1)
                        link(TTo(DL[:], DL[:], E[0][:], ALU.add))
                        sp_d.wait(eng, i, w + 1)
                        for c in range(2):
                            e_in.fire(TTo(E[c][:], DL[:], bc(SP[:, c], HC), ALU.mult))
                        rg.wait(eng, i, w + 1)
                        for c in range(3):
                            xp.wait(eng, i, w * NE + HC + 3 + c + 1)
                            xr.fire(STT(RG[:, c], ps[:, X0 + (HC + 3 + c) % 2], -1.0, RG[:, c], ALU.mult, ALU.mult))
                        xr.wait(eng, i, w * 10 + 10)
                        for c in range(3):
                            if w == 0:
                                hs_in[c].wait(eng, i)
                            h = HS[:, c * HC:(c + 1) * HC]
                            link(TTo(OG[:], ps[:, 0:HC], bc(RG[:, c], HC), ALU.mult))
                            link(TTo(h, h, OG[:], ALU.add))
                            e_out.wait(eng, i, w * 3 + c + 1)
                            link(TTo(h, h, E[c % 2][:], ALU.mult))
                            link(TTo(h, h, OG[:], ALU.subtract))
                            if c == 0:
                                e_in.fire(TTo(E[0][:], DL[:], bc(SP[:, 2], HC), ALU.mult))
                            if w == 0:
                                some_final(c)
                        if w == 0:
                            hs_in[3].wait(eng, i)
                        h = HS[:, 3 * HC:4 * HC]
                        link(TTo(OG[:], ps[:, 0:HC], DL[:], ALU.mult))
                        sk.wait(eng, i, w + 1)
                        link(TTo(OG[:], OG[:], bc(SK[:], HC), ALU.mult))
                        wr.fire(TTo(h, h, OG[:], ALU.add))
                        wr.wait(eng, i, w + 1)

                    def read(o):
                        for c in range(C):
                            for hc in range(HC):
                                ww = RW[:, hc, o, c:c + 1]
                                if c == 0:
                                    ins = TS(Y[:, o, hc], HS[:, c * HC + hc], ww, None, ALU.mult)
                                else:
                                    ins = STT(Y[:, o, hc], HS[:, c * HC + hc], ww, Y[:, o, hc], ALU.mult, ALU.add)
                            if c < C - 1:
                                link(ins)
                        y.fire(ins)

                    def centre(o):
                        ym.wait(eng, i, o + 1)
                        yc.fire(TTo(Y[:, o], Y[:, o], bc(ps[:, X0 + o], HC), ALU.subtract))

                    def scale(o):
                        rs.wait(eng, i, o + 1)
                        yc.wait(eng, i, o + 1)
                        link(TTo(Y[:, o], Y[:, o], bc(R[:, o], HC), ALU.mult))
                        for hc in range(HC):
                            ins = TS(Y[:, o, hc], Y[:, o, hc], GB[:, 0, o, hc:hc + 1], GB[:, 1, o, hc:hc + 1], ALU.mult, ALU.add)
                        z.fire(ins)

                    def z_low(o):
                        zh.wait(eng, i, o + 1)
                        z.wait(eng, i, o + 1)
                        zl.fire(TTo(ZL[:, o], Y[:, o], ZH[:, o].bitcast(F32), ALU.subtract))

                    write(0)
                    some_final(3)
                    read(0)
                    some_final(4)
                    read(1)
                    some_final(5)
                    centre(0)
                    centre(1)
                    some_final(6, 7)
                    scale(0)
                    scale(1)
                    z_low(0)
                    z_low(1)
                    if j is not None:
                        with eng.Fori(NF // 4, NF // 2) as k:
                            for a in range(2):
                                final(j, k * 2 + a, a, k)

                    def up_low(m, a):
                        uh.wait(eng, i, m + 1)
                        ul.fire(TTo(UL[a][:], RAWU[a][:], UH[a][:].bitcast(F32), ALU.subtract))

                    def proj_low(m, a):
                        ph.wait(eng, i, m + 1)
                        pl.fire(TTo(PL[a][:], RAWP[a][:], PH[a][:].bitcast(F32), ALU.subtract))

                    def product(m, a):
                        up.wait(eng, i, m + 1)
                        silu.wait(eng, i, m + 1)
                        if not (isinstance(m, int) and m == 0):
                            mh.wait(eng, i, m)
                            ml.wait(eng, i, m)
                        prod.fire(TTo(PR[:], ps[:, X1], SG[:], ALU.mult))

                    def inner_low(m, a):
                        mh.wait(eng, i, m + 1)
                        ml.fire(TTo(ML[a][:], PR[:], MH[a][:].bitcast(F32), ALU.subtract))

                    def inner_chunk(m, a, last=False):
                        if not last:
                            up_low(m + 1, 1 - a)
                        proj_low(m, a)
                        product(m, a)
                        inner_low(m, a)

                    up_low(0, 0)
                    inner_chunk(0, 0)
                    with eng.Fori(0, NM // 2 - 1) as k:
                        inner_chunk(k * 2 + 1, 1)
                        inner_chunk(k * 2 + 2, 0)
                    inner_chunk(NM - 1, 1, True)
                    write(1)
                    for g in range(4):
                        h = HS[:, g * HC:(g + 1) * HC]
                        x_in[g % 2].wait(eng, i, g // 2 + 1)
                        x2.fire(STT(h, h, t["gate"][:, 0:1], XR[:, g % 2], ALU.mult, ALU.add))
                    mean2.wait(eng, i)
                    x2.wait(eng, i, 4)
                    for g in range(4):
                        c2.fire(TTo(XD[:, g * HC:(g + 1) * HC], HS[:, g * HC:(g + 1) * HC], bc(ps[:, X0], HC), ALU.subtract))
                    chain.close()

                def drain(j):
                    low_and_sum(j)
                    gate_norm(j)
                    with eng.Fori(0, NF // 2) as k:
                        for a in range(2):
                            final(j, k * 2 + a, a, k)

                blocks(eng, body, drain)


def build(nc, args):
    io = dict(args)
    io["x"] = args["x"].rearrange("f p t -> p f t")
    io["qkv_s"] = nc.dram_tensor("qkv_scratch", [P, 3, B * NH // 2, KT, 2 * HD], F32, kind="Internal").ap()
    io["y_s"] = nc.dram_tensor("y_scratch", [B * NH, HD, L], F32, kind="Internal").ap()
    io["y_v"] = io["y_s"].rearrange("(n q) d t -> (q d) n t", q=P // HD)
    io["x2"] = nc.dram_tensor("x2_scratch", [P, NF, B * L], F32, kind="Internal").ap()
    io["out"] = args["out"].rearrange("f p t -> p f t")
    io["xn"] = nc.dram_tensor("xn_scratch", [P, NF, B * L], F32, kind="Internal").ap()
    with ExitStack() as ctx:
        def sb(name, shape, dt=F32):
            return ctx.enter_context(nc.sbuf_tensor(name, shape, dt))

        t = {
            "ones_d": sb("ones_d", [P, P]), "ones_h": sb("ones_h", [P, P]), "eps": sb("eps", [P, 1]),
            "ident": sb("ident", [P, P]), "ident_r": sb("ident_r", [P, P], F32R),
            "gate": sb("gate", [P, 2]),
        }
        with ExitStack() as mid:
            def sbm(name, shape, dt=F32):
                return mid.enter_context(nc.sbuf_tensor(name, shape, dt))

            t["masks"] = sbm("masks", [P, 2, P])
            t["masks_r"] = sbm("masks_r", [P, 2, P], F32R)
            with ExitStack() as first:
                def sbf(name, shape, dt=F32):
                    return first.enter_context(nc.sbuf_tensor(name, shape, dt))

                t["cos"] = sbf("cos", [P, B * KT, HD])
                t["sin"] = sbf("sin", [P, B * KT, HD])
                t["read1"] = sbf("read1", [P, HC, 3, C])
                t["read1_gb"] = sbf("read1_gb", [P, 2, 3, HC])
                t["qkv_h"] = sbf("qkv_h", [P, 3 * HC * H], F32R)
                t["qkv_l"] = sbf("qkv_l", [P, 3 * HC * H], F32R)
                setup_phase(nc, io, t)
                read_phase(nc, io, t)
            attention_phase(nc, io, t)
        block_phase(nc, io, t)


def layouts(x, pos_BxS, ctx_1024, g_xattn, g_ffn, L0_xattn_attn_read_w, L0_xattn_attn_read_g,
            L0_xattn_attn_read_b, L0_xattn_qkv_w, L0_xattn_attn_wod_w, L0_xattn_attn_wab_w, L0_xattn_attn_wab_b,
            L0_xattn_attn_du_w, L0_xattn_attn_du_b, L0_xattn_mlp_read_w, L0_xattn_mlp_read_g, L0_xattn_mlp_read_b,
            L0_xattn_mlp_wod_w, L0_xattn_mlp_wab_w, L0_xattn_mlp_wab_b, L0_xattn_mlp_du_w, L0_xattn_mlp_du_b,
            L0_ffn_sign, L0_ffn_scale):
    import numpy as np

    def read(w, o):
        return w.reshape(HC, P, o, C).transpose(1, 0, 2, 3)

    def read_gb(g, b, o):
        return np.stack([g.reshape(o, HC, P), b.reshape(o, HC, P)]).transpose(3, 0, 1, 2)

    def small(w):
        a, bb, sk = w[:NA], w[NA:2 * NA], w[2 * NA:]
        order = [q.reshape(RH, C - 1, *q.shape[1:]).swapaxes(0, 1).reshape(NA, *q.shape[1:]) for q in (a, bb)]
        return np.concatenate([*order, sk])

    def wall(wod, wab):
        w = np.concatenate([wod, small(wab)]).T
        return w.reshape(-1, P, WALL)

    def expand(du_a, du_m):
        e = np.zeros((ROWS, NX, P), np.float32)
        e[:DR, 0:HC] = du_a.reshape(HC, P, DR).transpose(2, 0, 1)
        e[:DR, HC:2 * HC] = du_m.reshape(HC, P, DR).transpose(2, 0, 1)
        for j in range(2 * C - 1):
            for r in range(RH):
                e[DR + j * RH + r, 2 * HC + j, r::RH] = 1.0
        return e

    def small_bias(b):
        return np.concatenate([np.zeros(DR, np.float32), small(b)])

    wall_m = wall(L0_xattn_mlp_wod_w, L0_xattn_mlp_wab_w)
    up = ctx_1024.reshape(2, NM, P, HC, P).transpose(1, 4, 0, 3, 2)
    row, col = np.arange(P)[:, None], np.arange(P)[None, :]
    return {
        "x": x.reshape(B * L, HC, P, C).transpose(3, 1, 2, 0).reshape(NF, P, B * L),
        "pos": pos_BxS.reshape(B * KT, P).T,
        "inv_freq": np.broadcast_to((1.0 / 10000.0 ** (np.arange(HD // 2, dtype=np.float32) / np.float32(HD // 2))
                                     ).astype(np.float32), (P, HD // 2)),
        "gates": np.broadcast_to(np.stack([g_xattn.reshape(()), g_ffn.reshape(()), L0_ffn_scale.reshape(())]), (P, 3)),
        "ident": np.eye(P, dtype=np.float32),
        "masks": np.stack([np.where(row > col, np.float32(NEG), np.float32(0)),
                           np.where(col > row, np.float32(NEG), np.float32(0))], 1),
        "read1": read(L0_xattn_attn_read_w, 3),
        "read1_gb": read_gb(L0_xattn_attn_read_g, L0_xattn_attn_read_b, 3),
        "read2": read(L0_xattn_mlp_read_w, 2),
        "read2_gb": read_gb(L0_xattn_mlp_read_g, L0_xattn_mlp_read_b, 2),
        "qkv": L0_xattn_qkv_w.reshape(3, H, HC, P).transpose(3, 0, 2, 1).reshape(P, 3 * HC * H),
        "wall_a": wall(L0_xattn_attn_wod_w, L0_xattn_attn_wab_w).transpose(1, 0, 2),
        "expand": expand(L0_xattn_attn_du_w, L0_xattn_mlp_du_w),
        "bias": np.stack([small_bias(L0_xattn_attn_wab_b), small_bias(L0_xattn_mlp_wab_b)], 1),
        "du_b": np.stack([L0_xattn_attn_du_b.reshape(HC, P), L0_xattn_mlp_du_b.reshape(HC, P)]).transpose(2, 0, 1),
        "mlp_up": up.reshape(NM, P, 2 * HC * P),
        "mlp_proj": wall_m,
        "sign": L0_ffn_sign.reshape(HC, P, C, HC, P, C).transpose(5, 3, 1, 2, 0, 4).reshape(NF, P, NF, P),
    }


def kernel(**inputs):
    import numpy as np
    import concourse.bacc as bacc
    from concourse.bass_utils import run_bass_kernel_spmd

    arrays = {"in_" + k: np.ascontiguousarray(v) for k, v in layouts(**{k: np.asarray(v) for k, v in inputs.items()}).items()}
    nc = bacc.Bacc("TRN2", target_bir_lowering=False, num_devices=1)
    args = {k[3:]: nc.dram_tensor(k, v.shape, mybir.dt.from_np(v.dtype), kind="ExternalInput").ap()
            for k, v in arrays.items()}
    args["out"] = nc.dram_tensor("out", [NF, P, B * L], F32, kind="ExternalOutput").ap()
    build(nc, args)
    result = run_bass_kernel_spmd(nc, [arrays], core_ids=[0]).results[0]["out"]
    return result.reshape(C, HC, P, B, L).transpose(3, 4, 1, 2, 0).reshape(B, L, D)
```

```python
from contextlib import ExitStack

import concourse.bass as bass
from concourse import mybir

F32 = mybir.dt.float32
F32R = mybir.dt.float32r
I32 = mybir.dt.int32
ALU = mybir.AluOpType
ACT = mybir.ActivationFunctionType
AX = mybir.AxisListType

P = 128
B, L = 2, 1024
H, C = 512, 4
D = H * C
NF = D // P
HC = H // P
NH, HD = 16, 32
RH = 16
DR = 8
M = 2048
NM = M // P
T = 512
NB = B * L // T
TT = T // P
KT = L // P
NA = (C - 1) * RH
ROWS = DR + 2 * NA + RH
WALL = H + ROWS
NX = 2 * HC + 2 * C - 1
EPS = 1e-5
NEG = -1e30
STACK = 3 * HD


class Event:

    def __init__(self, ctx, nc, name, per=1, unit=1, credit=0):
        self.sem = ctx.enter_context(nc.semaphore(name))
        self.per, self.unit, self.credit = per, unit, credit

    def value(self, i, k):
        return i * (self.per * self.unit) + (k * self.unit + self.credit)

    def wait(self, eng, i=0, k=1):
        assert not isinstance(k, int) or k * self.unit + self.credit > 0, "a wait's value stays positive"
        eng.wait_ge(self.sem, self.value(i, k))

    def fire(self, instruction):
        instruction.then_inc(self.sem, self.unit)


def setup_phase(nc, io, t):
    with ExitStack() as ctx:
        def ev(name, **k):
            return Event(ctx, nc, "s0_" + name, **k)

        raw = ctx.enter_context(nc.sbuf_tensor("qkv_raw", [P, 3 * HC * H], F32))
        pos_i = ctx.enter_context(nc.sbuf_tensor("pos_i", [P, B * KT], I32))
        pos_f = ctx.enter_context(nc.sbuf_tensor("pos_f", [P, B * KT], F32))
        inv = ctx.enter_context(nc.sbuf_tensor("inv_freq", [P, HD // 2], F32))
        ang = ctx.enter_context(nc.sbuf_tensor("ang", [P, 2, B * KT, HD // 2], F32))
        turns = ctx.enter_context(nc.sbuf_tensor("turns", [P, 2, B * KT, HD // 2], F32))
        gates = ctx.enter_context(nc.sbuf_tensor("gates", [P, 3], F32))
        g_tmp = ctx.enter_context(nc.sbuf_tensor("g_tmp", [P, 4], F32))
        idf = t["ident"]
        loaded = ev("loaded", unit=16)
        w_loaded = ev("w_loaded", unit=16)
        high = ev("high")
        dve = ev("dve")
        act = ev("act")
        low = ev("low")
        loads = [(pos_i[:], io["pos"]), (inv[:], io["inv_freq"]), (gates[:], io["gates"]),
                 (idf[:], io["ident"]), (t["masks"][:], io["masks"]), (t["read1"][:], io["read1"]),
                 (t["read1_gb"][:], io["read1_gb"])]
        with nc.Block() as block:
            @block.gpsimd
            def _(eng):
                for half in range(2):
                    t["x_in"][half].fire(eng.dma_start(t["X"][:, half], io["x"][:, :, half * T:(half + 1) * T]))

            @block.sync
            def _(eng):
                for dst, src in loads:
                    loaded.fire(eng.dma_start(dst, src))
                w_loaded.fire(eng.dma_start(raw[:], io["qkv"]))
                loaded.wait(eng, k=len(loads))
                w_loaded.wait(eng)

            @block.vector
            def _(eng):
                n = 0

                def link(ins):
                    nonlocal n
                    n += 1
                    dve.fire(ins)
                    dve.wait(eng, k=n)

                link(eng.memset(t["ones_d"][:], 1.0 / D))
                link(eng.memset(t["ones_h"][:], 1.0 / H))
                link(eng.memset(t["eps"][:], EPS))
                loaded.wait(eng, k=len(loads))
                link(eng.tensor_copy(pos_f[:], pos_i[:]))
                pb = pos_f[:].unsqueeze(2).to_broadcast([P, B * KT, HD // 2])
                ib = inv[:].unsqueeze(1).to_broadcast([P, B * KT, HD // 2])
                link(eng.tensor_tensor(ang[:, 0], pb, ib, ALU.mult))
                link(eng.tensor_scalar(turns[:, 0], ang[:, 0], 1 / 6.283185307179586, None, ALU.mult))
                link(eng.tensor_scalar(turns[:, 1], turns[:, 0], 0.25, None, ALU.add))
                link(eng.tensor_scalar(turns[:], turns[:], 12582912.0, None, ALU.add))
                link(eng.tensor_scalar(turns[:], turns[:], -12582912.0, None, ALU.add))
                link(eng.tensor_scalar(ang[:, 1], ang[:, 0], 1.0, None, ALU.mult))
                for part in (6.28125, 0.0019350051879882812, 3.0199157663446e-07):
                    link(eng.scalar_tensor_tensor(ang[:], turns[:], -part, ang[:], ALU.mult, ALU.add))
                link(eng.tensor_scalar(ang[:, 1], ang[:, 1], 1.5707963267948966, None, ALU.add))
                link(eng.tensor_scalar(ang[:], ang[:], 3.1415925, -3.1415925, ALU.min, ALU.max))
                act.wait(eng, k=2)
                halves = t["cos"][:].rearrange("p t (a j) -> p t a j", a=2)
                sins = t["sin"][:].rearrange("p t (a j) -> p t a j", a=2)
                for a in range(2):
                    link(eng.tensor_copy(halves[:, :, a], turns[:, 1]))
                link(eng.tensor_scalar(sins[:, :, 0], turns[:, 0], -1.0, None, ALU.mult))
                link(eng.tensor_copy(sins[:, :, 1], turns[:, 0]))
                link(eng.tensor_scalar(g_tmp[:, 3:4], gates[:, 2:3], 0.0, None, ALU.max))
                link(eng.scalar_tensor_tensor(g_tmp[:, 2:3], g_tmp[:, 3:4], -2.0, gates[:, 2:3], ALU.mult, ALU.add))
                act.wait(eng, k=5)
                link(eng.tensor_tensor(g_tmp[:, 3:4], g_tmp[:, 3:4], g_tmp[:, 2:3], ALU.add))
                link(eng.tensor_tensor(t["gate"][:, 1:2], g_tmp[:, 1:2], g_tmp[:, 3:4], ALU.mult))
                link(eng.tensor_copy(t["gate"][:, 0:1], g_tmp[:, 0:1]))
                w_loaded.wait(eng)
                high.wait(eng)
                low.fire(eng.tensor_tensor(t["qkv_l"][:], raw[:], t["qkv_h"][:].bitcast(F32), ALU.subtract))
                low.wait(eng)

            @block.scalar
            def _(eng):
                n = 0

                def link(ins):
                    nonlocal n
                    n += 1
                    act.fire(ins)
                    act.wait(eng, k=n)

                w_loaded.wait(eng)
                high.fire(eng.activation(t["qkv_h"][:], raw[:], ACT.Copy))
                dve.wait(eng, k=15)
                link(eng.activation(turns[:, 0], ang[:, 0], ACT.Sin))
                link(eng.activation(turns[:, 1], ang[:, 1], ACT.Sin))
                loaded.wait(eng, k=len(loads))
                link(eng.activation(g_tmp[:, 0:2], gates[:, 0:2], ACT.Tanh))
                dve.wait(eng, k=21)
                link(eng.activation(g_tmp[:, 2:3], g_tmp[:, 2:3], ACT.Exp))
                link(eng.activation(g_tmp[:, 2:3], g_tmp[:, 2:3], ACT.Ln, bias=1.0))
                eng.activation(t["ident_r"][:], idf[:], ACT.Copy)
                link(eng.activation(t["masks_r"][:], t["masks"][:], ACT.Copy))


class Chain:

    def __init__(self, ctx, nc, name, per):
        self.event, self.at = Event(ctx, nc, name, per=per), 0

    def link(self, eng, i, instruction):
        self.at += 1
        self.event.fire(instruction)
        self.event.wait(eng, i, self.at)

    def start(self):
        self.at = 0

    def close(self):
        assert self.at == self.event.per, (self.at, self.event.per)


def read_phase(nc, io, t):
    with ExitStack() as ctx:
        def ev(name, **k):
            return Event(ctx, nc, "s1_" + name, **k)

        def sb(name, shape, dt=F32):
            return ctx.enter_context(nc.sbuf_tensor(name, shape, dt))

        X = t["X"]
        SQ = sb("SQ", [P, 2, HC, T])
        Y = sb("Y", [P, 3, HC, T])
        ZH = sb("ZH", [P, HC, T], F32R)
        ZL = sb("ZL", [P, HC, T], F32R)
        R = sb("R", [P, 4, T])
        RT = sb("RT", [P, 2, H])
        OUT = sb("OUT", [P, TT, H])
        ps = ctx.enter_context(nc.psum_tensor("ps1", [P, 8, 512], F32))
        MEAN, VAR, YM, YV, PJ = 0, 1, (2, 3, 1), (2, 3, 2), 4

        x_in = t["x_in"]
        xn_out = [ev(f"xn_out{a}", unit=16) for a in range(2)]
        mean, cent, xn, rsx = ev("mean"), ev("cent"), ev("xn"), ev("rsx")
        sq, sq_used = ev("sq", per=7, credit=4), ev("sq_used", per=7, credit=4)
        y, rs = ev("y", per=3), ev("rs", per=3)
        ym, yc, z, zh, zl = (ev(n, per=3) for n in ("ym", "yc", "z", "zh", "zl"))
        pj = ev("pj", per=3 * TT, credit=1)
        pjq_used = ev("pjq_used", per=2 * TT)
        pjv_used = ev("pjv_used", per=TT, credit=TT)
        qk_ready = ev("qk_ready", per=2 * TT)
        stored = [ev(f"stored{tt}", per=3, unit=16, credit=16) for tt in range(TT)]
        assert L // T == 2

        def blocks(eng, body):
            with eng.Fori(0, B - 1) as b:
                for half in range(2):
                    body(b * 2 + half, half, b, True)
            for half in range(2):
                body(NB - 2 + half, half, B - 1, half == 0)

        def slot(half, k):
            return (half + k + 1) % 2

        with nc.Block() as block:
            @block.gpsimd
            def _(eng):
                with eng.Fori(0, B - 1) as b:
                    for half in range(2):
                        xn_out[half].wait(eng, b)
                        y.wait(eng, b * 2 + half, 3)
                        x_in[half].fire(eng.dma_start(X[:, half], io["x"][:, :, bass.ds((b * 2 + half + 2) * T, T)]))

            @block.sync
            def _(eng):
                for tt in range(TT):
                    eng.sem_inc(stored[tt].sem, 16)
                with eng.Fori(0, B) as b:
                    for half in range(2):
                        i = b * 2 + half
                        xn.wait(eng, i)
                        xn_out[half].fire(eng.dma_start(io["xn"][:, :, bass.ds(i * T, T)], X[:, half]))
                        for o in range(3):
                            for tt in range(TT):
                                if o < 2:
                                    qk_ready.wait(eng, i, o * TT + tt + 1)
                                else:
                                    pjv_used.wait(eng, i, tt + 1)
                                stored[tt].fire(eng.dma_start(
                                    io["qkv_s"][:, o, bass.ds(b * (NH // 2), NH // 2), half * TT + tt:half * TT + tt + 1, :],
                                    OUT[:, tt].rearrange("p (h a d) -> p h a d", h=NH // 2, a=1)))
                for half in range(2):
                    xn_out[half].wait(eng, B - 1)
                for tt in range(TT):
                    stored[tt].wait(eng, NB - 1, 3)

            @block.tensor
            def _(eng):
                def x_mean(half, first, last):
                    for f in range(first, last):
                        mm = eng.matmul(ps[:, MEAN], t["ones_d"][:], X[:, half, f], start=f == 0, stop=f == NF - 1,
                                        skip_group_check=True)
                    return mm

                def x_var(i, k0, slot_of):
                    for g in range(4):
                        sq.wait(eng, i, k0 + g + 1)
                        for f in range(HC):
                            mm = eng.matmul(ps[:, VAR], t["ones_d"][:], SQ[:, slot_of(g), f],
                                            start=g + f == 0, stop=g + f == 6)
                        sq_used.fire(mm)

                x_in[0].wait(eng)
                mean.fire(x_mean(0, 0, NF))
                x_var(0, -4, lambda g: g % 2)

                def body(i, half, b, more):
                    def y_mean(o):
                        y.wait(eng, i, o + 1)
                        if o == 2:
                            rsx.wait(eng, i)
                        for hc in range(HC):
                            mm = eng.matmul(ps[:, YM[o]], t["ones_h"][:], Y[:, o, hc], start=hc == 0, stop=hc == HC - 1,
                                            skip_group_check=True)
                        ym.fire(mm)

                    def y_var(o):
                        sq.wait(eng, i, o + 1)
                        yc.wait(eng, i, o + 1)
                        if o == 2:
                            rs.wait(eng, i, 1)
                        for hc in range(HC):
                            mm = eng.matmul(ps[:, YV[o]], t["ones_h"][:], SQ[:, slot(half, o + 1), hc],
                                            start=hc == 0, stop=hc == HC - 1)
                        sq_used.fire(mm)

                    def project(o):
                        zh.wait(eng, i, o + 1)
                        zl.wait(eng, i, o + 1)
                        for tt in range(TT):
                            n = o * TT + tt
                            if o == 0:
                                pjv_used.wait(eng, i, n + 1 - TT)
                            else:
                                pjq_used.wait(eng, i, n + 1 - TT)
                            step = 0
                            for ic in range(HC):
                                for zz, ww in ((ZH, "qkv_h"), (ZL, "qkv_h"), (ZH, "qkv_l")):
                                    mm = eng.matmul(ps[:, PJ + tt], zz[:, ic, tt * P:(tt + 1) * P],
                                                    t[ww][:, bass.ts(o * HC + ic, H)],
                                                    start=step == 0, stop=step == 3 * HC - 1)
                                    step += 1
                            pj.fire(mm)

                    y_mean(0)
                    if more:
                        x_in[1 - half].wait(eng, b + half)
                        cent.wait(eng, i)
                        x_mean(1 - half, 0, NF // 2)
                    y_mean(1)
                    if more:
                        mean.fire(x_mean(1 - half, NF // 2, NF))
                    y_mean(2)
                    y_var(0)
                    y_var(1)
                    y_var(2)
                    project(0)
                    if more:
                        yc.wait(eng, i, 3)
                        x_var(i, 3, lambda g: slot(half, 4 + g))
                    project(1)
                    project(2)

                blocks(eng, body)

            @block.scalar
            def _(eng):
                eng.preload_act_table_set("natural_log_exp_and_others")
                eng.sem_inc(pjv_used.sem, TT)
                x_chain = Chain(ctx, nc, "s1_act_x", 1)
                chain = Chain(ctx, nc, "s1_act", 3)

                def square(i, k, s, src):
                    if not (isinstance(i, int) and i == 0 and k - 2 <= -4):
                        sq_used.wait(eng, i, k - 2)
                    sq.fire(eng.activation(SQ[:, s], src, ACT.Square))

                def rstd(k, bank, link, done):
                    link(eng.activation(R[:, k], ps[:, bank], ACT.Ln, bias=t["eps"][:]))
                    done.fire(eng.activation(R[:, k], R[:, k], ACT.Exp, scale=-0.5))

                def x_rstd(n, i, k):
                    sq_used.wait(eng, i, k)
                    x_chain.start()
                    rstd(0, VAR, lambda ins: x_chain.link(eng, n, ins), rsx)
                    x_chain.close()

                cent.wait(eng)
                for g in range(4):
                    square(0, g - 3, g % 2, X[:, 0, 4 * g:4 * g + 4])
                x_rstd(0, 0, 0)

                def body(i, half, b, more):
                    chain.start()

                    def x_square(g):
                        if more:
                            cent.wait(eng, i + 1)
                            square(i, 4 + g, slot(half, 4 + g), X[:, 1 - half, 4 * g:4 * g + 4])

                    def z_high(o):
                        z.wait(eng, i, o + 1)
                        pj.wait(eng, i, o * TT)
                        zh.fire(eng.activation(ZH[:], Y[:, o], ACT.Copy))

                    for o in range(3):
                        yc.wait(eng, i, o + 1)
                        square(i, o + 1, slot(half, o + 1), Y[:, o])
                    for o in range(3):
                        sq_used.wait(eng, i, o + 1)
                        rstd(1 + o, YV[o], lambda ins: chain.link(eng, i, ins), rs)
                    z_high(0)
                    for g in range(2):
                        x_square(g)
                    z_high(1)
                    for g in range(2, 4):
                        x_square(g)
                    if more:
                        x_rstd(i + 1, i, 7)
                    z_high(2)
                    for tt in range(TT):
                        pj.wait(eng, i, 2 * TT + tt + 1)
                        stored[tt].wait(eng, i, 2)
                        pjv_used.fire(eng.activation(OUT[:, tt], ps[:, PJ + tt], ACT.Copy))
                    chain.close()

                blocks(eng, body)

            @block.vector
            def _(eng):
                eng.sem_inc(pj.sem, 1)
                chain = Chain(ctx, nc, "s1_dve", 3 * 3 + 3)
                w, gb = t["read1"], t["read1_gb"]

                def x_centre(n, half):
                    mean.wait(eng, n)
                    cent.fire(eng.tensor_tensor(X[:, half], X[:, half], ps[:, MEAN].unsqueeze(1).to_broadcast([P, NF, T]), ALU.subtract))

                def x_scale(n, half):
                    rsx.wait(eng, n)
                    cent.wait(eng, n)
                    xn.fire(eng.tensor_tensor(X[:, half], X[:, half], R[:, 0].unsqueeze(1).to_broadcast([P, NF, T]), ALU.mult))

                x_centre(0, 0)
                x_scale(0, 0)

                def body(i, half, b, more):
                    chain.start()

                    def read(o):
                        if o == 0:
                            xn.wait(eng, i)
                        for c in range(C):
                            for hc in range(HC):
                                ww = w[:, hc, o, c:c + 1]
                                if c == 0:
                                    ins = eng.tensor_scalar(Y[:, o, hc], X[:, half, c * HC + hc], ww, None, ALU.mult)
                                else:
                                    ins = eng.scalar_tensor_tensor(Y[:, o, hc], X[:, half, c * HC + hc], ww, Y[:, o, hc],
                                                                   ALU.mult, ALU.add)
                            if c < C - 1:
                                chain.link(eng, i, ins)
                        y.fire(ins)

                    def centre(o):
                        ym.wait(eng, i, o + 1)
                        yc.fire(eng.tensor_tensor(Y[:, o], Y[:, o], ps[:, YM[o]].unsqueeze(1).to_broadcast([P, HC, T]), ALU.subtract))

                    def scale(o):
                        rs.wait(eng, i, o + 1)
                        chain.link(eng, i, eng.tensor_tensor(Y[:, o], Y[:, o], R[:, 1 + o].unsqueeze(1).to_broadcast([P, HC, T]), ALU.mult))
                        for hc in range(HC):
                            ins = eng.tensor_scalar(Y[:, o, hc], Y[:, o, hc], gb[:, 0, o, hc:hc + 1], gb[:, 1, o, hc:hc + 1],
                                                    ALU.mult, ALU.add)
                        z.fire(ins)

                    def z_low(o):
                        zh.wait(eng, i, o + 1)
                        z.wait(eng, i, o + 1)
                        pj.wait(eng, i, o * TT)
                        zl.fire(eng.tensor_tensor(ZL[:], Y[:, o], ZH[:].bitcast(F32), ALU.subtract))

                    def rope(o):
                        for tt in range(TT):
                            pj.wait(eng, i, o * TT + tt + 1)
                            src = ps[:, PJ + tt].rearrange("p (h d) -> p h d", h=NH)
                            tile = bass.ds(i * TT + tt, 1)
                            cos = t["cos"][:, tile, :].to_broadcast([P, NH, HD])
                            sin = t["sin"][:, tile, :].to_broadcast([P, NH, HD])
                            a = RT[:, 0].rearrange("p (h d) -> p h d", h=NH)
                            b = RT[:, 1].rearrange("p (h d) -> p h d", h=NH)
                            hf = HD // 2
                            eng.tensor_tensor(a, src, cos, ALU.mult)
                            eng.tensor_tensor(b[:, :, 0:hf], src[:, :, hf:HD], sin[:, :, 0:hf], ALU.mult)
                            last = eng.tensor_tensor(b[:, :, hf:HD], src[:, :, 0:hf], sin[:, :, hf:HD], ALU.mult)
                            pjq_used.fire(last)
                            pjq_used.wait(eng, i, o * TT + tt + 1)
                            stored[tt].wait(eng, i, o)
                            qk_ready.fire(eng.tensor_tensor(OUT[:, tt], RT[:, 0], RT[:, 1], ALU.add))
                            qk_ready.wait(eng, i, o * TT + tt + 1)

                    for o in range(3):
                        read(o)
                    for o in range(3):
                        centre(o)
                    if more:
                        x_centre(i + 1, 1 - half)
                    scale(0)
                    z_low(0)
                    scale(1)
                    scale(2)
                    z_low(1)
                    rope(0)
                    if more:
                        x_scale(i + 1, 1 - half)
                    z_low(2)
                    rope(1)
                    chain.close()

                blocks(eng, body)


def attention_phase(nc, io, t):
    with ExitStack() as ctx:
        def ev(name, **k):
            return Event(ctx, nc, "s2_" + name, **k)

        def sb(name, shape, dt=F32):
            return ctx.enter_context(nc.sbuf_tensor(name, shape, dt))

        G = [sb(f"G{n}", [P, KT, 2 * HD]) for n in "qkv"]
        S = [sb(f"stack_{n}", [P, KT, STACK], F32R) for n in "qk"]
        ST = [[sb(f"turned_{n}{a}", [STACK + 1, L], F32R) for a in range(2)] for n in "qk"]
        VO = [sb(f"v_ones{a}", [P, KT, 2 * HD]) for a in range(2)]
        zeros = sb("zeros", [P, KT, HD])
        MAXES = sb("maxes", [P, KT, 2])
        NM = sb("neg_max", [P, KT])
        NPT = 3
        PT = sb("probs", [P, NPT, T])
        RC = sb("recip", [HD, 2, T])
        OT = [sb(f"heads_out{a}", [HD, L]) for a in range(2)]
        ones = sb("ones_row", [STACK + 1, L])
        ps = ctx.enter_context(nc.psum_tensor("ps2", [P, 8, 512], F32))
        MX, SC, O = (1, 2, 7), (3, 4), (5, 6)
        TURN, ROW = (0, *MX), (0, MX[2])

        MXP = [(q, a, min((q + 1) * P - a, T)) for q in range(KT) for a in range(0, (q + 1) * P, T)]
        SCP = [(h, k, max(k * P, h * T), (h + 1) * T - max(k * P, h * T))
               for h in range(L // T) for k in range((h + 1) * TT)]
        NMX, NSC = len(MXP), len(SCP)
        last_of = [max(p for p, x in enumerate(SCP) if x[0] == h) + 1 for h in range(L // T)]

        loaded = [ev(f"loaded_{n}", unit=16) for n in "qkv"]
        high, low, v_in = ev("high", credit=1), ev("low", credit=1), ev("v_in", credit=1)
        tr = ev("tr", per=4)
        tr_dve, tr_act = ev("tr_dve", per=2), ev("tr_act", per=2)
        mx, mx_read = ev("mx", per=NMX), ev("mx_read", per=NMX, credit=3)
        nm = ev("nm")
        row, row_out = ev("row", per=2), ev("row_out", per=2, credit=1)
        sc, ex, pv = ev("sc", per=NSC), ev("ex", per=NSC, credit=2), ev("pv", per=NSC, credit=NPT)
        o_out = ev("o_out", per=2, credit=2)
        o_ln, o_part = ev("o_ln", per=2), ev("o_part", per=2)
        stored = [ev(f"stored{a}", unit=16, credit=16) for a in range(2)]
        ready, ones_in = ev("ready"), ev("ones")

        def slots(eng, slot, first=None, last=None):
            heads = B * NH
            if first:
                first()
            slot(0, 0, 0, True, False)
            with eng.Fori(0, heads // 2 - 1) as i:
                slot(i * 2 + 1, 1, i, True, True)
                slot(i * 2 + 2, 0, i + 1, True, True)
            slot(heads - 1, 1, heads // 2 - 1, True, True)
            slot(heads, 0, heads // 2, False, True)

        with nc.Block() as block:
            @block.sync
            def _(eng):
                for a in range(2):
                    eng.sem_inc(stored[a].sem, 16)

                def load(pair, n):
                    for e in (high, low, v_in):
                        e.wait(eng, n, 0)
                    for o in range(3):
                        loaded[o].fire(eng.dma_start(G[o][:], io["qkv_s"][:, o, bass.ds(pair, 1)]))

                def slot(n, a, pair, front, back):
                    if front and a == 1 and not (isinstance(n, int)):
                        load(pair + 1, n + 1)
                    if back:
                        o_out.wait(eng, n - 1, 2)
                        stored[1 - a].fire(eng.dma_start(io["y_s"][bass.ds(n - 1, 1)].rearrange("a d t -> (a d) t"),
                                                         OT[1 - a][:]))

                load(0, 0)
                slots(eng, slot)
                for a in range(2):
                    stored[a].wait(eng, B * NH // 2 - 1)

            @block.gpsimd
            def _(eng):
                for a in range(2):
                    eng.memset(VO[a][:], 1.0)
                eng.memset(zeros[:], 0.0)
                eng.memset(MAXES[:], -3e38).then_inc(v_in.sem, 1)
                v_in.wait(eng, 0, 0)

                def take_v(n, a, pair):
                    loaded[2].wait(eng, pair)
                    pv.wait(eng, n - 1, 0)
                    v_in.fire(eng.tensor_tensor(VO[a][:, :, 0:HD], G[2][:, :, a * HD:(a + 1) * HD], zeros[:], ALU.add))

                def slot(n, a, pair, front, back):
                    if front and not (isinstance(n, int) and n == B * NH - 1):
                        take_v(n + 1, 1 - a, pair + a)

                eng.wait_ge(loaded[2].sem, 16)
                v_in.fire(eng.tensor_tensor(VO[0][:, :, 0:HD], G[2][:, :, 0:HD], zeros[:], ALU.add))
                slots(eng, slot)

            @block.tensor
            def _(eng):
                eng.sem_inc(pv.sem, NPT)
                ready.wait(eng)

                def turn(n, a, k):
                    which, half = k // 2, k % 2
                    if k == 0:
                        high.wait(eng, n)
                        low.wait(eng, n)
                        row_out.wait(eng, n, 0)
                        mx_read.wait(eng, n, 0)
                    for tt in range(TT):
                        mm = eng.transpose(ps[0:STACK, TURN[k], tt * P:(tt + 1) * P].bitcast(F32R),
                                           S[which][:, half * TT + tt], t["ident_r"][:])
                    tr.fire(mm)

                def maxima(n, a, m):
                    q, k0, w = MXP[m]
                    if m == 0:
                        tr_dve.wait(eng, n, 2)
                        tr_act.wait(eng, n, 2)
                    mx_read.wait(eng, n, m - 2)
                    bank = MX[m % 3]
                    diag = k0 + w == (q + 1) * P
                    mm = eng.matmul(ps[:, bank, 0:w], ST[0][a][0:STACK, q * P:(q + 1) * P], ST[1][a][0:STACK, k0:k0 + w],
                                    start=True, stop=not diag, skip_group_check=True)
                    if diag:
                        mm = eng.matmul(ps[:, bank, w - P:w], t["ident_r"][:], t["masks_r"][:, 1], start=False, stop=True,
                                        skip_group_check=True)
                    mx.fire(mm)

                def rows(n, a):
                    nm.wait(eng, n)
                    for r in range(2):
                        for tt in range(TT):
                            mm = eng.matmul(ps[STACK:STACK + 1, ROW[r], tt * P:(tt + 1) * P], NM[:, r * TT + tt:r * TT + tt + 1],
                                            t["ident"][:], start=True, stop=True, skip_group_check=True)
                        row.fire(mm)

                def score(v, a, p):
                    h, k, q0, w = SCP[p]
                    if p == 0:
                        row_out.wait(eng, v, 2)
                    ex.wait(eng, v, p - 1)
                    diag = q0 == k * P
                    mm = eng.matmul(ps[:, SC[p % 2], 0:w], ST[1][a][:, k * P:(k + 1) * P], ST[0][a][:, q0:q0 + w],
                                    start=True, stop=not diag, skip_group_check=True)
                    if diag:
                        mm = eng.matmul(ps[:, SC[p % 2], 0:P], t["ident_r"][:], t["masks_r"][:, 0], start=False, stop=True,
                                        skip_group_check=True)
                    sc.fire(mm)

                def weigh(v, a, p):
                    h, k, q0, w = SCP[p]
                    if p == 0:
                        v_in.wait(eng, v)
                    if k == 0:
                        o_out.wait(eng, v, h - 1)
                    ex.wait(eng, v, p + 1)
                    c = q0 - h * T
                    pv.fire(eng.matmul(ps[0:2 * HD, O[h], c:c + w], VO[a][:, k], PT[:, p % NPT, 0:w],
                                       start=k == 0, stop=p + 1 == last_of[h], skip_group_check=True))

                def slot(n, a, pair, front, back):
                    m = 0
                    for p in range(NSC):
                        for k in range(4 if front and p == 0 else 0):
                            turn(n, a, k)
                        if back:
                            score(n - 1, 1 - a, p)
                            if p:
                                weigh(n - 1, 1 - a, p - 1)
                        while front and p and m < min(NMX, 2 * p):
                            maxima(n, a, m)
                            m += 1
                        if front and p == 10:
                            rows(n, a)
                    if back:
                        weigh(n - 1, 1 - a, NSC - 1)

                slots(eng, slot)

            @block.scalar
            def _(eng):
                eng.sem_inc(ex.sem, 2)
                eng.sem_inc(high.sem, 1)

                def take_high(n, a, pair):
                    for o in range(2):
                        loaded[o].wait(eng, pair)
                    if not (isinstance(n, int) and n == 0):
                        tr.wait(eng, n - 1, 4)
                    c = slice(a * HD, (a + 1) * HD)
                    for o, places in ((0, (0, 1)), (1, (0, 2))):
                        for j in places:
                            ins = eng.activation(S[o][:, :, j * HD:(j + 1) * HD], G[o][:, :, c], ACT.Copy)
                    high.fire(ins)

                def out(n, a, which, half, bank_event, k):
                    tr.wait(eng, n, k)
                    tr_act.fire(eng.activation(ST[which][a][0:STACK, half * T:(half + 1) * T], ps[0:STACK, TURN[k - 1]], ACT.Copy))

                def exp(v, a, p):
                    h, k, q0, w = SCP[p]
                    sc.wait(eng, v, p + 1)
                    pv.wait(eng, v, p + 1 - NPT)
                    ex.fire(eng.activation(PT[:, p % NPT, 0:w], ps[:, SC[p % 2], 0:w], ACT.Exp, scale=HD ** -0.5))

                def recip(v, h):
                    pv.wait(eng, v, last_of[h])
                    o_out.wait(eng, v, h - 1)
                    o_ln.fire(eng.activation(RC[:, h], ps[HD:2 * HD, O[h]], ACT.Ln))
                    o_ln.wait(eng, v, h + 1)
                    o_part.fire(eng.activation(RC[:, h], RC[:, h], ACT.Exp, scale=-1.0))

                def slot(n, a, pair, front, back):
                    for p in range(NSC):
                        if front and p == 0:
                            out(n, a, 0, 1, tr_act, 2)
                            out(n, a, 1, 1, tr_act, 4)
                        if back:
                            exp(n - 1, 1 - a, p)
                        if back and p == 8:
                            recip(n - 1, 0)
                        if front and p == 6 and not (isinstance(n, int) and n == B * NH - 1):
                            take_high(n + 1, 1 - a, pair + a)
                    if back:
                        recip(n - 1, 1)

                eng.preload_act_table_set("natural_log_exp_and_others")
                take_high(0, 0, 0)
                slots(eng, slot)

            @block.vector
            def _(eng):
                eng.sem_inc(low.sem, 1)
                eng.sem_inc(mx_read.sem, 3)
                eng.sem_inc(row_out.sem, 1)
                eng.sem_inc(o_out.sem, 2)
                ones_in.fire(eng.memset(ones[:], 1.0))
                ones_in.wait(eng)
                for a in range(2):
                    ins = eng.tensor_copy(ST[1][a][STACK:STACK + 1, :], ones[STACK:STACK + 1, :])
                ready.fire(ins)

                def take_low(n, a, pair):
                    high.wait(eng, n)
                    if not (isinstance(n, int) and n == 0):
                        tr.wait(eng, n - 1, 4)
                    c = slice(a * HD, (a + 1) * HD)
                    for o, place in ((0, 2), (1, 1)):
                        ins = eng.tensor_tensor(S[o][:, :, place * HD:(place + 1) * HD], G[o][:, :, c],
                                                S[o][:, :, 0:HD].bitcast(F32), ALU.subtract)
                    low.fire(ins)

                def out(n, a, which, half, k):
                    tr.wait(eng, n, k)
                    tr_dve.fire(eng.tensor_copy(ST[which][a][0:STACK, half * T:(half + 1) * T], ps[0:STACK, TURN[k - 1]]))

                def row_max(n, m):
                    q, k0, w = MXP[m]
                    mx.wait(eng, n, m + 1)
                    mx_read.fire(eng.tensor_reduce(MAXES[:, q, k0 // T:k0 // T + 1], ps[:, MX[m % 3], 0:w], AX.X, ALU.max))

                def head_out(v, a, h, pair):
                    pv.wait(eng, v, last_of[h])
                    if h == 0:
                        stored[a].wait(eng, pair, 0)
                    o_part.wait(eng, v, h + 1)
                    o_out.fire(eng.tensor_tensor(OT[a][:, h * T:(h + 1) * T], ps[0:HD, O[h]], RC[:, h], ALU.mult))

                def slot(n, a, pair, front, back):
                    if front:
                        out(n, a, 0, 0, 1)
                        out(n, a, 1, 0, 3)
                        for m in range(NMX):
                            row_max(n, m)
                        mx_read.wait(eng, n, NMX)
                        nm.fire(eng.tensor_reduce(NM[:], MAXES[:], AX.X, ALU.max, negate=True))
                        if not (isinstance(n, int) and n == B * NH - 1):
                            take_low(n + 1, 1 - a, pair + a)
                        for r in range(2):
                            row.wait(eng, n, r + 1)
                            row_out.fire(eng.tensor_copy(ST[0][a][STACK:STACK + 1, r * T:(r + 1) * T],
                                                         ps[STACK:STACK + 1, ROW[r]]))
                    if back:
                        for h in range(2):
                            head_out(n - 1, 1 - a, h, pair - 1 + a)

                take_low(0, 0, 0)
                slots(eng, slot)


def block_phase(nc, io, t):
    with ExitStack() as ctx:
        def ev(name, **k):
            return Event(ctx, nc, "s3_" + name, **k)

        def sb(name, shape, dt=F32):
            return ctx.enter_context(nc.sbuf_tensor(name, shape, dt))

        KB = 1024
        EX = sb("expand_sb", [ROWS, NX, P])
        RW, GB = sb("read2_sb", [P, HC, 2, C]), sb("read2_gb_sb", [P, 2, 2, HC])
        BIAS, DUB = sb("bias_sb", [ROWS, 2]), sb("du_b_sb", [P, 2, HC])
        HS = sb("hidden", [P, NF, T])
        R2 = sb("rstd_gate", [P, T])
        RES = [sb(f"residual{a}", [P, T]) for a in range(2)]
        UW = 2 * HC * P
        uk, pk = UW * 4 / KB, WALL * 4 / KB
        raw_u0, raw_p0 = sb("up_raw0", [P, UW]), sb("proj_raw0", [P, WALL])

        def arena(name, kb):
            base = (nc.sbuf_base + 31) // 32 * 32
            sb(name, [P, kb * KB // 4])
            return lambda n, at, shape, dt=F32: nc.alloc_sbuf_tensor_at(n, shape, dt, offset=base + int(at * KB))

        a_y, a_z, a_e, a_f = (arena(n, kb) for n, kb in (("place_y", 16), ("place_z", 32), ("place_e", 16), ("place_f", 88)))
        YIN, YL, YH = a_y("y_raw", 0, [P, HC, T]), a_y("y_low", 0, [P, HC, T], F32R), a_y("y_high", 8, [P, HC, T], F32R)
        Y = a_y("Y2", 0, [P, 2, HC, T])
        WA = [a_z(f"wall_a{n}", k * HC * pk, [P, HC, WALL], F32R) for k, n in enumerate("hl")]
        DL, OG = a_z("delta", 0, [P, HC, T]), a_z("og", 8, [P, HC, T])
        SP, RG = a_z("softplus_a", 16, [P, 3, T]), a_z("b_over_a", 22, [P, 3, T])
        SK, SM = a_z("skip", 28, [P, T]), a_z("small", 30, [ROWS, T])
        ZH, ZL = a_z("ZH2", 0, [P, 2, HC, T], F32R), a_z("ZL2", 16, [P, 2, HC, T], F32R)
        R = a_z("rstd_read", 28, [P, 2, T])
        E = [a_e("e0", 0, [P, HC, T]), a_e("e1", 8, [P, HC, T])]
        XD, XL, XH = a_f("XD", 0, [P, NF, T]), a_f("XL", 0, [P, NF, T], F32R), a_f("XH", 32, [P, NF, T], F32R)
        SRAW, SH, SL = ([a_f(f"sign_{n}{a}", 64 + 8 * k + 4 * a, [P, NF // 2, P], d) for a in range(2)]
                        for k, (n, d) in enumerate((("raw", F32), ("h", F32R), ("l", F32R))))
        SQ = [E[0], E[1], a_f("sq2", 72, [P, HC, T]), a_f("sq3", 80, [P, HC, T])]
        RAWU, RAWP = [raw_u0, a_f("up_raw1", 0, [P, UW])], [raw_p0, a_f("proj_raw1", uk, [P, WALL])]
        f = uk + pk
        UH, UL = ([a_f(f"up_{n}{a}", f + (2 * k + a) * uk, [P, UW], F32R) for a in range(2)] for k, n in enumerate("hl"))
        f += 4 * uk
        PH, PL = ([a_f(f"proj_{n}{a}", f + (2 * k + a) * pk, [P, WALL], F32R) for a in range(2)] for k, n in enumerate("hl"))
        f += 4 * pk
        SG, PR = a_f("silu", f, [P, T]), a_f("product", f + 2, [P, T])
        MH, ML = ([a_f(f"inner_{n}{a}", f + 4 + 2 * (2 * k + a), [P, T], F32R) for a in range(2)] for k, n in enumerate("hl"))
        WRAW, OG3 = a_f("wall_a_raw", 46, [P, HC, WALL]), a_f("og3", 56, [P, HC, T])
        XR = a_f("x_piece", 72, [P, 2, HC, T])
        assert f + 12 <= 46 and 46 + HC * pk <= 56
        ps = ctx.enter_context(nc.psum_tensor("ps3", [P, 8, 512], F32))
        SMALL, X0, X1, FB = 4, 5, 6, (4, 7)
        NE = HC + 2 * C - 1

        const = ev("const", unit=16)
        y_in, w_in = ev("y_in", unit=16), ev("w_in", unit=16)
        hs_in = [ev(f"hs_in{g}", unit=16) for g in range(4)]
        yh, yl, wah, wal, proj = (ev(n) for n in ("yh", "yl", "wah", "wal", "proj"))
        small = ev("small", per=2)
        xp, relu, xr, sk = ev("xp", per=2 * NE), ev("relu", per=14), ev("xr", per=20), ev("sk", per=2)
        ln_d, ln_a, sp_d, rg = ev("ln_d", per=2), ev("ln_a", per=2), ev("sp_d", per=2), ev("rg", per=2)
        e_in, e_out = ev("e_in", per=6), ev("e_out", per=6)
        wr, dl, o3, skip3 = ev("wr", per=2), ev("dl", per=2), ev("o3"), ev("skip3")
        y, ym, yc, sq, yv, rs, z, zh, zl = (ev("r_" + n, per=2) for n in ("y", "ym", "yc", "sq", "yv", "rs", "z", "zh", "zl"))
        up_in = [ev(f"up_in{a}", per=NM // 2, unit=16) for a in range(2)]
        proj_in = [ev(f"proj_in{a}", per=NM // 2, unit=16) for a in range(2)]
        uh, ul, ph, pl = (ev(n, per=NM) for n in ("uh", "ul", "ph", "pl"))
        gate, up, silu, prod, mh, ml, acc = (ev(n, per=NM) for n in ("gate", "up", "silu", "prod", "mh", "ml", "acc"))
        x_in = [ev(f"x_in{a}", per=2, unit=16) for a in range(2)]
        x2, mean2, c2, xh, sq2, xl, sum2, v2, rs2, gated = (ev("n_" + n, per=k) for n, k in
            (("x2", 4), ("mean", 1), ("c", 4), ("xh", 4), ("sq", 4), ("xl", 4), ("sum", 3), ("v", 1), ("rs", 1), ("gated", 1)))
        x2_out = [ev(f"x2_out{g}", unit=16) for g in range(4)]
        s_in = [ev(f"s_in{a}", per=NF, unit=16) for a in range(2)]
        sh, sl = ev("sh", per=2 * NF), ev("sl", per=2 * NF, credit=1)
        ffn_half, ffn, fin = ev("ffn_half", per=NF), ev("ffn", per=NF), ev("fin", per=NF)
        res_in = [ev(f"res_in{a}", per=NF // 2, unit=16) for a in range(2)]
        out = [ev(f"out{a}", per=NF // 2, unit=16) for a in range(2)]

        def bc(ap, n):
            return ap.unsqueeze(1).to_broadcast([P, n, T])

        def blocks(eng, body, drain=None):
            body(0, None)
            with eng.Fori(1, NB) as i:
                body(i, i - 1)
            if drain:
                drain(NB - 1)

        def tokens(i):
            return bass.ds(i * T, T)

        consts = [(EX[:], io["expand"]), (RW[:], io["read2"]), (GB[:], io["read2_gb"]), (BIAS[:], io["bias"]), (DUB[:], io["du_b"])]
        with nc.Block() as block:
            @block.sync
            def _(eng):
                for dst, src in consts:
                    const.fire(eng.dma_start(dst, src))

                def signs(j):
                    def load(m, first=False):
                        for a in range(2):
                            sl.wait(eng, j, 0 if first else m * 2 + a - 1)
                            s_in[a].fire(eng.dma_start(SRAW[a][:], io["sign"][bass.ds(m, 1), :, a * (NF // 2):(a + 1) * (NF // 2)]
                                                       .rearrange("a p f o -> (a p) f o")))

                    load(0, True)
                    with eng.Fori(1, NF) as m:
                        load(m)

                def load_y(i):
                    y_in.fire(eng.dma_start(YIN[:], io["y_v"][:, bass.ds(i // (L // T) * HC, HC), bass.ds(i % (L // T) * T, T)]))

                w_in.fire(eng.dma_start(WRAW[:], io["wall_a"]))
                load_y(0)

                def body(i, j):
                    for g in range(4):
                        if j is not None:
                            x2_out[g].wait(eng, j)
                            mean2.wait(eng, j)
                            c2.wait(eng, j, 4)
                        hs_in[g].fire(eng.dma_start(HS[:, g * HC:(g + 1) * HC], io["xn"][:, g * HC:(g + 1) * HC, tokens(i)]))
                    if j is not None:
                        signs(j)

                    def load_up(m, a):
                        if a == 0 and isinstance(m, int):
                            if j is not None:
                                ul.wait(eng, j, NM)
                        elif isinstance(m, int):
                            if j is not None:
                                ffn.wait(eng, j, NF)
                        else:
                            uh.wait(eng, i, m - 1)
                            ul.wait(eng, i, m - 1)
                        up_in[a].fire(eng.dma_start(RAWU[a][:], io["mlp_up"][bass.ds(m, 1)].rearrange("a p n -> (a p) n")))

                    def load_proj(m, a):
                        if not isinstance(m, int):
                            ph.wait(eng, i, m - 1)
                            pl.wait(eng, i, m - 1)
                        proj_in[a].fire(eng.dma_start(RAWP[a][:], io["mlp_proj"][bass.ds(m, 1)].rearrange("a p n -> (a p) n")))

                    def load_x(g):
                        x_in[g % 2].fire(eng.dma_start(XR[:, g % 2], io["x"][:, g * HC:(g + 1) * HC, tokens(i)]))

                    load_up(0, 0)
                    load_proj(0, 0)
                    load_up(1, 1)
                    load_proj(1, 1)
                    for g in range(2):
                        load_x(g)
                    zl.wait(eng, i, 2)
                    load_y((i + 1) % NB)
                    wal.wait(eng, i)
                    w_in.fire(eng.dma_start(WRAW[:], io["wall_a"]))
                    with eng.Fori(1, NM // 2) as k:
                        for a in range(2):
                            load_up(k * 2 + a, a)
                            load_proj(k * 2 + a, a)
                    for g in range(4):
                        x2.wait(eng, i, g + 1)
                        if g < 2:
                            load_x(g + 2)
                        x2_out[g].fire(eng.dma_start(io["x2"][:, g * HC:(g + 1) * HC, tokens(i)], HS[:, g * HC:(g + 1) * HC]))

                blocks(eng, body, signs)
                for g in range(4):
                    x2_out[g].wait(eng, NB - 1)

            @block.gpsimd
            def _(eng):
                eng.sem_inc(sl.sem, 1)

                def signs(j):
                    def low(m):
                        for a in range(2):
                            sh.wait(eng, j, m * 2 + a + 1)
                            sl.fire(eng.tensor_tensor(SL[a][:], SRAW[a][:], SH[a][:].bitcast(F32), ALU.subtract))

                    def residual(m, a):
                        res_in[a].fire(eng.dma_start(RES[a][:], io["x2"][:, bass.ds(m, 1), tokens(j)].rearrange("p a n -> p (a n)")))

                    def store(m, a):
                        fin.wait(eng, j, m + 1)
                        out[a].fire(eng.dma_start(io["out"][:, bass.ds(m, 1), tokens(j)].rearrange("p a n -> p (a n)"), RES[a][:]))

                    for g in range(4):
                        x2_out[g].wait(eng, j)
                    for a in range(2):
                        residual(a, a)
                        low(a)
                    with eng.Fori(1, NF // 2) as k:
                        for a in range(2):
                            m = k * 2 + a
                            store(m - 2, a)
                            low(m)
                            out[a].wait(eng, j, k)
                            residual(m, a)
                    for a in range(2):
                        store(NF - 2 + a, a)
                    for a in range(2):
                        out[a].wait(eng, j, NF // 2)

                chain = Chain(ctx, nc, "s3_pool", 2)

                def body(i, j):
                    if j is not None:
                        signs(j)
                    chain.start()
                    dl.wait(eng, i, 2)
                    o3.wait(eng, i)
                    chain.link(eng, i, eng.tensor_tensor(OG3[:], OG3[:], DL[:], ALU.mult))
                    sk.wait(eng, i, 2)
                    chain.link(eng, i, eng.tensor_tensor(OG3[:], OG3[:], bc(SK[:], HC), ALU.mult))
                    h = HS[:, 3 * HC:4 * HC]
                    skip3.fire(eng.tensor_tensor(h, h, OG3[:], ALU.add))
                    chain.close()

                blocks(eng, body, signs)

            @block.tensor
            def _(eng):
                const.wait(eng, k=len(consts))

                def three(out_ap, lh, ll, rh, rl, start, stop):
                    eng.matmul(out_ap, lh, rh, start=start, stop=False, skip_group_check=True)
                    eng.matmul(out_ap, lh, rl, start=False, stop=False, skip_group_check=True)
                    return eng.matmul(out_ap, ll, rh, start=False, stop=stop, skip_group_check=True)

                def rows(n):
                    return slice(n * P, (n + 1) * P) if n < HC else slice(H, WALL)

                def variance(j):
                    sum2.wait(eng, j, 3)
                    for f in range(HC):
                        mm = eng.matmul(ps[:, X1], t["ones_d"][:], SQ[0][:, f], start=f == 0, stop=f == HC - 1)
                    v2.fire(mm)

                def signs(j, i, first, last, between=None):
                    def chunk(m, a):
                        for half in range(2):
                            sh.wait(eng, j, m * 2 + half + 1)
                            sl.wait(eng, j, m * 2 + half + 1)
                            for f in range(NF // 2):
                                n = half * (NF // 2) + f
                                mm = three(ps[:, FB[a]], SH[half][:, f], SL[half][:, f], XH[:, n], XL[:, n], n == 0, n == NF - 1)
                            if half == 0:
                                ffn_half.fire(mm)
                        ffn.fire(mm)

                    if first == 0:
                        xh.wait(eng, j, 4)
                        xl.wait(eng, j, 4)
                        if i is not None:
                            small.wait(eng, i, 1)
                        chunk(0, 0)
                        chunk(1, 1)
                        if between:
                            between()
                        first = 2
                    with eng.Fori(first // 2, last // 2) as k:
                        for a in range(2):
                            fin.wait(eng, j, k * 2 + a - 1)
                            chunk(k * 2 + a, a)

                def body(i, j):
                    for e in (yh, yl, wah, wal):
                        e.wait(eng, i)
                    if j is not None:
                        wr.wait(eng, j, 2)
                        skip3.wait(eng, j)
                    for n in range(HC + 1):
                        for ic in range(HC):
                            mm = three(ps[0:P if n < HC else ROWS, n], WA[0][:, ic, rows(n)], WA[1][:, ic, rows(n)],
                                       YH[:, ic], YL[:, ic], ic == 0, ic == HC - 1)
                    proj.fire(mm)
                    if j is not None:
                        variance(j)

                    def expansion(w, n):
                        e = w * HC + n if n < HC else 2 * HC + (0, 1, 2, 6, 3, 4, 5)[n - HC]
                        if n == 9:
                            sk.wait(eng, i, w + 1)
                        elif n >= 2:
                            xr.wait(eng, i, w * 10 + min(n - 1, 8))
                        elif w == 0 and j is not None:
                            if n == 0:
                                c2.wait(eng, j, 4)
                            else:
                                rs2.wait(eng, j)
                        xp.fire(eng.matmul(ps[:, X0 + n % 2], EX[:, e], SM[:], start=True, stop=True))

                    small.wait(eng, i, 1)
                    for n in range(NE - 1):
                        expansion(0, n)
                    if j is not None:
                        signs(j, i, 0, 8, lambda: expansion(0, NE - 1))
                    else:
                        expansion(0, NE - 1)
                    sk.wait(eng, i, 1)
                    xr.wait(eng, i, 10)
                    for o in range(2):
                        y.wait(eng, i, o + 1)
                        for hc in range(HC):
                            mm = eng.matmul(ps[:, X0 + o], t["ones_h"][:], Y[:, o, hc], start=hc == 0, stop=hc == HC - 1)
                        ym.fire(mm)
                    if j is not None:
                        signs(j, i, 8, 10)
                    for o in range(2):
                        yc.wait(eng, i, o + 1)
                        sq.wait(eng, i, o + 1)
                        for hc in range(HC):
                            mm = eng.matmul(ps[:, X0 + o], t["ones_h"][:], E[o][:, hc], start=hc == 0, stop=hc == HC - 1)
                        yv.fire(mm)
                    if j is not None:
                        signs(j, i, 10, NF)
                        fin.wait(eng, j, NF)

                    def inner(m, a):
                        uh.wait(eng, i, m + 1)
                        ul.wait(eng, i, m + 1)
                        for o, bank, before, done in ((0, X0, silu, gate), (1, X1, prod, up)):
                            if isinstance(m, int) and m == 0:
                                zh.wait(eng, i, o + 1)
                                zl.wait(eng, i, o + 1)
                                rs.wait(eng, i, o + 1)
                            else:
                                before.wait(eng, i, m)
                            for ic in range(HC):
                                c = slice((o * HC + ic) * P, (o * HC + ic + 1) * P)
                                mm = three(ps[:, bank], UH[a][:, c], UL[a][:, c], ZH[:, o, ic], ZL[:, o, ic],
                                           ic == 0, ic == HC - 1)
                            done.fire(mm)

                    def accumulate(m, a, first, last):
                        for e in (ph, pl, mh, ml):
                            e.wait(eng, i, m + 1)
                        if first:
                            wr.wait(eng, i, 1)
                        for n in range(HC + 1):
                            mm = three(ps[0:P if n < HC else ROWS, n], PH[a][:, rows(n)], PL[a][:, rows(n)], MH[a][:], ML[a][:], first, last)
                        acc.fire(mm)

                    inner(0, 0)
                    inner(1, 1)
                    accumulate(0, 0, True, False)
                    with eng.Fori(1, NM // 2) as k:
                        for a in range(2):
                            inner(k * 2 + a, a)
                            accumulate(k * 2 + a - 1, 1 - a, False, False)
                    accumulate(NM - 1, 1, False, True)
                    prod.wait(eng, i, NM)
                    small.wait(eng, i, 2)
                    for n in range(NE):
                        expansion(1, n)
                    sk.wait(eng, i, 2)
                    xr.wait(eng, i, 20)
                    for g in range(4):
                        x2.wait(eng, i, g + 1)
                        for f in range(4 * g, 4 * g + 4):
                            mm = eng.matmul(ps[:, X0], t["ones_d"][:], HS[:, f], start=f == 0, stop=f == NF - 1)
                    mean2.fire(mm)

                def drain(j):
                    variance(j)
                    signs(j, None, 0, NF)

                blocks(eng, body, drain)

            @block.scalar
            def _(eng):
                eng.preload_act_table_set("natural_log_exp_and_others")
                const.wait(eng, k=len(consts))
                chain = Chain(ctx, nc, "s3_act", 8)
                norm_chain = Chain(ctx, nc, "s3_act_norm", 1)

                def squares(j):
                    for g in range(4):
                        c2.wait(eng, j, g + 1)
                        sq2.fire(eng.activation(SQ[g][:], XD[:, g * HC:(g + 1) * HC], ACT.Square))

                def norm(j):
                    norm_chain.start()
                    v2.wait(eng, j)
                    norm_chain.link(eng, j, eng.activation(R2[:], ps[:, X1], ACT.Ln, bias=t["eps"][:]))
                    rs2.fire(eng.activation(R2[:], R2[:], ACT.Exp, scale=-0.5))
                    norm_chain.close()

                def sign_high(j, m, first=False):
                    for a in range(2):
                        s_in[a].wait(eng, j, m + 1)
                        if first:
                            sum2.wait(eng, j, 2)
                        else:
                            (ffn_half, ffn)[a].wait(eng, j, m)
                        sh.fire(eng.activation(SH[a][:], SRAW[a][:], ACT.Copy))

                def operands_high(i):
                    y_in.wait(eng, i)
                    yh.fire(eng.activation(YH[:], YIN[:], ACT.Copy))
                    w_in.wait(eng, i)
                    wah.fire(eng.activation(WA[0][:], WRAW[:], ACT.Copy))

                operands_high(0)

                def body(i, j):
                    chain.start()

                    def link(ins):
                        chain.link(eng, i, ins)

                    if j is not None:
                        squares(j)
                        sign_high(j, 0, True)

                    def write(w):
                        if w == 0:
                            proj.wait(eng, i)
                        else:
                            acc.wait(eng, i, NM)
                        small.fire(eng.activation(SM[:], ps[0:ROWS, SMALL], ACT.Identity, bias=BIAS[:, w:w + 1]))
                        if w == 0 and j is not None:
                            norm(j)
                        for n in range(HC + 3):
                            xp.wait(eng, i, w * NE + n + 1)
                            if n < HC:
                                ins = eng.activation(DL[:, n], ps[:, X0 + n % 2], ACT.Relu, bias=DUB[:, w, n:n + 1])
                            else:
                                ins = eng.activation(SP[:, n - HC], ps[:, X0 + n % 2], ACT.Relu)
                            relu.fire(ins)
                        xp.wait(eng, i, w * NE + HC + C)
                        sk.fire(eng.activation(SK[:], ps[:, X0 + (HC + C - 1) % 2], ACT.Copy))
                        xr.wait(eng, i, w * 10 + HC)
                        for hc in range(HC):
                            ins = eng.activation(E[0][:, hc], E[0][:, hc], ACT.Exp, bias=DUB[:, w, hc:hc + 1])
                        link(ins)
                        ln_d.fire(eng.activation(E[0][:], E[0][:], ACT.Ln, bias=1.0))
                        xr.wait(eng, i, w * 10 + HC + 3)
                        link(eng.activation(E[1][:, 0:3], E[1][:, 0:3], ACT.Exp))
                        ln_a.fire(eng.activation(E[1][:, 0:3], E[1][:, 0:3], ACT.Ln, bias=1.0))
                        if w == 1:
                            o3.fire(eng.activation(OG3[:], ps[:, 0:HC], ACT.Copy))
                        sp_d.wait(eng, i, w + 1)
                        link(eng.activation(RG[:], SP[:], ACT.Ln, bias=t["eps"][:]))
                        rg.fire(eng.activation(RG[:], RG[:], ACT.Exp, scale=-1.0))
                        for c in range(3):
                            if c == 2 and w == 0 and j is not None:
                                sign_high(j, 1)
                            e_in.wait(eng, i, w * 3 + c + 1)
                            e_out.fire(eng.activation(E[c % 2][:], E[c % 2][:], ACT.Exp, scale=-1.0))

                    write(0)
                    if j is not None:
                        for m in range(2, 9):
                            sign_high(j, m)
                    for o in range(2):
                        yc.wait(eng, i, o + 1)
                        wr.wait(eng, i, 1)
                        sq.fire(eng.activation(E[o][:], Y[:, o], ACT.Square))
                    if j is not None:
                        for m in range(9, 11):
                            sign_high(j, m)
                    for o in range(2):
                        yv.wait(eng, i, o + 1)
                        link(eng.activation(R[:, o], ps[:, X0 + o], ACT.Ln, bias=t["eps"][:]))
                        rs.fire(eng.activation(R[:, o], R[:, o], ACT.Exp, scale=-0.5))
                    for o in range(2):
                        z.wait(eng, i, o + 1)
                        zh.fire(eng.activation(ZH[:, o], Y[:, o], ACT.Copy))
                        if o == 0 and j is not None:
                            sign_high(j, 11)
                    if j is not None:
                        with eng.Fori(12, NF) as m:
                            sign_high(j, m)

                    def up_high(m, a, k):
                        up_in[a].wait(eng, i, k + 1)
                        if isinstance(m, int) and m < 2:
                            if j is not None:
                                ffn.wait(eng, j, NF)
                        else:
                            up.wait(eng, i, m - 1)
                        uh.fire(eng.activation(UH[a][:], RAWU[a][:], ACT.Copy))

                    def proj_high(m, a, k):
                        proj_in[a].wait(eng, i, k + 1)
                        if not (isinstance(m, int) and m < 2):
                            acc.wait(eng, i, m - 1)
                        ph.fire(eng.activation(PH[a][:], RAWP[a][:], ACT.Copy))

                    def inner(m, a):
                        gate.wait(eng, i, m + 1)
                        if not (isinstance(m, int) and m == 0):
                            prod.wait(eng, i, m)
                        silu.fire(eng.activation(SG[:], ps[:, X0], ACT.Silu))

                    def inner_high(m, a):
                        prod.wait(eng, i, m + 1)
                        if not (isinstance(m, int) and m < 2):
                            acc.wait(eng, i, m - 1)
                        mh.fire(eng.activation(MH[a][:], PR[:], ACT.Copy))

                    def inner_chunk(m, a, k, last=False):
                        if not last:
                            up_high(m + 1, 1 - a, k + a)
                        proj_high(m, a, k)
                        inner(m, a)
                        inner_high(m, a)

                    up_high(0, 0, 0)
                    inner_chunk(0, 0, 0)
                    with eng.Fori(0, NM // 2 - 1) as k:
                        inner_chunk(k * 2 + 1, 1, k)
                        inner_chunk(k * 2 + 2, 0, k + 1)
                    inner_chunk(NM - 1, 1, NM // 2 - 1, True)
                    write(1)
                    wr.wait(eng, i, 2)
                    skip3.wait(eng, i)
                    operands_high(i + 1)
                    wal.wait(eng, i + 1)
                    for g in range(4):
                        c2.wait(eng, i, g + 1)
                        xh.fire(eng.activation(XH[:, g * HC:(g + 1) * HC], XD[:, g * HC:(g + 1) * HC], ACT.Copy))
                    chain.close()

                def drain(j):
                    squares(j)
                    sign_high(j, 0, True)
                    norm(j)
                    with eng.Fori(1, NF) as m:
                        sign_high(j, m)

                blocks(eng, body, drain)

            @block.vector
            def _(eng):
                const.wait(eng, k=len(consts))
                chain = Chain(ctx, nc, "s3_dve", 33)
                fin_chain = Chain(ctx, nc, "s3_fin_product", NF)
                TTo, STT, TS = eng.tensor_tensor, eng.scalar_tensor_tensor, eng.tensor_scalar

                def low_and_sum(j):
                    for g in range(4):
                        d = slice(g * HC, (g + 1) * HC)
                        xh.wait(eng, j, g + 1)
                        sq2.wait(eng, j, g + 1)
                        xl.fire(TTo(XL[:, d], XD[:, d], XH[:, d].bitcast(F32), ALU.subtract))
                    for g in range(2):
                        sum2.fire(TTo(SQ[g][:], SQ[g][:], SQ[g + 2][:], ALU.add))
                    sum2.wait(eng, j, 2)
                    sum2.fire(TTo(SQ[0][:], SQ[0][:], SQ[1][:], ALU.add))
                    sum2.wait(eng, j, 3)

                def gate_norm(j):
                    rs2.wait(eng, j)
                    gated.fire(TS(R2[:], R2[:], t["gate"][:, 1:2], None, ALU.mult))
                    gated.wait(eng, j)

                def final(j, m, a, k):
                    ffn.wait(eng, j, m + 1)
                    res_in[a].wait(eng, j, k + 1)
                    ins = TTo(ps[:, FB[a]], ps[:, FB[a]], R2[:], ALU.mult)
                    fin_chain.event.fire(ins)
                    fin_chain.event.wait(eng, j, m + 1)
                    fin.fire(TTo(RES[a][:], RES[a][:], ps[:, FB[a]], ALU.add))

                def operands_low(i):
                    yh.wait(eng, i)
                    yl.fire(TTo(YL[:], YIN[:], YH[:].bitcast(F32), ALU.subtract))
                    wah.wait(eng, i)
                    wal.fire(TTo(WA[1][:], WRAW[:], WA[0][:].bitcast(F32), ALU.subtract))

                operands_low(0)

                def body(i, j):
                    chain.start()

                    def link(ins):
                        chain.link(eng, i, ins)

                    def some_final(*ms):
                        if j is not None:
                            for m in ms:
                                final(j, m, m % 2, m // 2)

                    if j is not None:
                        low_and_sum(j)

                    def write(w):
                        proj.wait(eng, i) if w == 0 else acc.wait(eng, i, NM)
                        for n in range(HC + 3):
                            relu.wait(eng, i, w * 7 + n + 1)
                            src, dst = (DL[:, n], E[0][:, n]) if n < HC else (SP[:, n - HC], E[1][:, n - HC])
                            xr.fire(STT(dst, src, -2.0, ps[:, X0 + n % 2], ALU.mult, ALU.add))
                        if w == 0 and j is not None:
                            gate_norm(j)
                        ln_a.wait(eng, i, w + 1)
                        sp_d.fire(TTo(SP[:], SP[:], E[1][:, 0:3], ALU.add))
                        ln_d.wait(eng, i, w + 1)
                        dl.fire(TTo(DL[:], DL[:], E[0][:], ALU.add))
                        dl.wait(eng, i, w + 1)
                        sp_d.wait(eng, i, w + 1)
                        for c in range(2):
                            e_in.fire(TTo(E[c][:], DL[:], bc(SP[:, c], HC), ALU.mult))
                        rg.wait(eng, i, w + 1)
                        for c in range(3):
                            n = HC + C + c
                            xp.wait(eng, i, w * NE + n + 1)
                            xr.fire(STT(RG[:, c], ps[:, X0 + n % 2], -1.0, RG[:, c], ALU.mult, ALU.mult))
                            xr.wait(eng, i, w * 10 + n)
                            if w == 0:
                                hs_in[c].wait(eng, i)
                            h = HS[:, c * HC:(c + 1) * HC]
                            link(TTo(OG[:], ps[:, 0:HC], bc(RG[:, c], HC), ALU.mult))
                            link(TTo(h, h, OG[:], ALU.add))
                            e_out.wait(eng, i, w * 3 + c + 1)
                            link(TTo(h, h, E[c % 2][:], ALU.mult))
                            last = TTo(h, h, OG[:], ALU.subtract)
                            if w == 1 and c == 2:
                                wr.fire(last)
                                return
                            link(last)
                            if c == 0:
                                e_in.fire(TTo(E[0][:], DL[:], bc(SP[:, 2], HC), ALU.mult))
                            if w == 0:
                                some_final(c)
                        hs_in[3].wait(eng, i)
                        h = HS[:, 3 * HC:4 * HC]
                        link(TTo(OG[:], ps[:, 0:HC], DL[:], ALU.mult))
                        sk.wait(eng, i, 1)
                        link(TTo(OG[:], OG[:], bc(SK[:], HC), ALU.mult))
                        wr.fire(TTo(h, h, OG[:], ALU.add))
                        wr.wait(eng, i, 1)

                    def read(o):
                        for c in range(C):
                            for hc in range(HC):
                                ww = RW[:, hc, o, c:c + 1]
                                if c == 0:
                                    ins = TS(Y[:, o, hc], HS[:, c * HC + hc], ww, None, ALU.mult)
                                else:
                                    ins = STT(Y[:, o, hc], HS[:, c * HC + hc], ww, Y[:, o, hc], ALU.mult, ALU.add)
                            if c < C - 1:
                                link(ins)
                        y.fire(ins)

                    def centre(o):
                        ym.wait(eng, i, o + 1)
                        yc.fire(TTo(Y[:, o], Y[:, o], bc(ps[:, X0 + o], HC), ALU.subtract))

                    def scale(o):
                        rs.wait(eng, i, o + 1)
                        yc.wait(eng, i, o + 1)
                        link(TTo(Y[:, o], Y[:, o], bc(R[:, o], HC), ALU.mult))
                        for hc in range(HC):
                            ins = TS(Y[:, o, hc], Y[:, o, hc], GB[:, 0, o, hc:hc + 1], GB[:, 1, o, hc:hc + 1], ALU.mult, ALU.add)
                        z.fire(ins)

                    def z_low(o):
                        zh.wait(eng, i, o + 1)
                        z.wait(eng, i, o + 1)
                        zl.fire(TTo(ZL[:, o], Y[:, o], ZH[:, o].bitcast(F32), ALU.subtract))

                    write(0)
                    some_final(3)
                    read(0)
                    some_final(4)
                    read(1)
                    some_final(5, 6, 7)
                    centre(0)
                    centre(1)
                    some_final(8, 9)
                    scale(0)
                    scale(1)
                    z_low(0)
                    z_low(1)
                    if j is not None:
                        with eng.Fori(5, NF // 2) as k:
                            for a in range(2):
                                final(j, k * 2 + a, a, k)

                    def up_low(m, a):
                        uh.wait(eng, i, m + 1)
                        ul.fire(TTo(UL[a][:], RAWU[a][:], UH[a][:].bitcast(F32), ALU.subtract))

                    def proj_low(m, a):
                        ph.wait(eng, i, m + 1)
                        pl.fire(TTo(PL[a][:], RAWP[a][:], PH[a][:].bitcast(F32), ALU.subtract))

                    def product(m, a):
                        up.wait(eng, i, m + 1)
                        silu.wait(eng, i, m + 1)
                        if not (isinstance(m, int) and m == 0):
                            mh.wait(eng, i, m)
                            ml.wait(eng, i, m)
                        prod.fire(TTo(PR[:], ps[:, X1], SG[:], ALU.mult))

                    def inner_low(m, a):
                        mh.wait(eng, i, m + 1)
                        ml.fire(TTo(ML[a][:], PR[:], MH[a][:].bitcast(F32), ALU.subtract))

                    def inner_chunk(m, a, last=False):
                        if not last:
                            up_low(m + 1, 1 - a)
                        proj_low(m, a)
                        product(m, a)
                        inner_low(m, a)

                    up_low(0, 0)
                    inner_chunk(0, 0)
                    with eng.Fori(0, NM // 2 - 1) as k:
                        inner_chunk(k * 2 + 1, 1)
                        inner_chunk(k * 2 + 2, 0)
                    inner_chunk(NM - 1, 1, True)
                    write(1)
                    wr.wait(eng, i, 2)
                    for g in range(4):
                        if g == 3:
                            skip3.wait(eng, i)
                        h = HS[:, g * HC:(g + 1) * HC]
                        x_in[g % 2].wait(eng, i, g // 2 + 1)
                        x2.fire(STT(h, h, t["gate"][:, 0:1], XR[:, g % 2], ALU.mult, ALU.add))
                    operands_low(i + 1)
                    mean2.wait(eng, i)
                    x2.wait(eng, i, 4)
                    for g in range(4):
                        c2.fire(TTo(XD[:, g * HC:(g + 1) * HC], HS[:, g * HC:(g + 1) * HC], bc(ps[:, X0], HC), ALU.subtract))
                    chain.close()

                def drain(j):
                    low_and_sum(j)
                    gate_norm(j)
                    with eng.Fori(0, NF // 2) as k:
                        for a in range(2):
                            final(j, k * 2 + a, a, k)

                blocks(eng, body, drain)


def build(nc, args):
    io = dict(args)
    io["x"] = args["x"].rearrange("f p t -> p f t")
    io["qkv_s"] = nc.dram_tensor("qkv_scratch", [P, 3, B * NH // 2, KT, 2 * HD], F32, kind="Internal").ap()
    io["y_s"] = nc.dram_tensor("y_scratch", [B * NH, HD, L], F32, kind="Internal").ap()
    io["y_v"] = io["y_s"].rearrange("(n q) d t -> (q d) n t", q=P // HD)
    io["x2"] = nc.dram_tensor("x2_scratch", [P, NF, B * L], F32, kind="Internal").ap()
    io["out"] = args["out"].rearrange("f p t -> p f t")
    io["xn"] = nc.dram_tensor("xn_scratch", [P, NF, B * L], F32, kind="Internal").ap()
    with ExitStack() as ctx:
        def sb(name, shape, dt=F32):
            return ctx.enter_context(nc.sbuf_tensor(name, shape, dt))

        t = {
            "ones_d": sb("ones_d", [P, P]), "ones_h": sb("ones_h", [P, P]), "eps": sb("eps", [P, 1]),
            "ident": sb("ident", [P, P]), "ident_r": sb("ident_r", [P, P], F32R),
            "gate": sb("gate", [P, 2]),
        }
        with ExitStack() as mid:
            def sbm(name, shape, dt=F32):
                return mid.enter_context(nc.sbuf_tensor(name, shape, dt))

            t["masks"] = sbm("masks", [P, 2, P])
            t["masks_r"] = sbm("masks_r", [P, 2, P], F32R)
            with ExitStack() as first:
                def sbf(name, shape, dt=F32):
                    return first.enter_context(nc.sbuf_tensor(name, shape, dt))

                t["cos"] = sbf("cos", [P, B * KT, HD])
                t["sin"] = sbf("sin", [P, B * KT, HD])
                t["read1"] = sbf("read1", [P, HC, 3, C])
                t["read1_gb"] = sbf("read1_gb", [P, 2, 3, HC])
                t["qkv_h"] = sbf("qkv_h", [P, 3 * HC * H], F32R)
                t["qkv_l"] = sbf("qkv_l", [P, 3 * HC * H], F32R)
                t["X"] = sbf("X", [P, 2, NF, T])
                t["x_in"] = [Event(first, nc, f"x_in{half}", unit=16) for half in range(2)]
                setup_phase(nc, io, t)
                read_phase(nc, io, t)
            attention_phase(nc, io, t)
        block_phase(nc, io, t)


def layouts(x, pos_BxS, ctx_1024, g_xattn, g_ffn, L0_xattn_attn_read_w, L0_xattn_attn_read_g,
            L0_xattn_attn_read_b, L0_xattn_qkv_w, L0_xattn_attn_wod_w, L0_xattn_attn_wab_w, L0_xattn_attn_wab_b,
            L0_xattn_attn_du_w, L0_xattn_attn_du_b, L0_xattn_mlp_read_w, L0_xattn_mlp_read_g, L0_xattn_mlp_read_b,
            L0_xattn_mlp_wod_w, L0_xattn_mlp_wab_w, L0_xattn_mlp_wab_b, L0_xattn_mlp_du_w, L0_xattn_mlp_du_b,
            L0_ffn_sign, L0_ffn_scale):
    import numpy as np

    def read(w, o):
        return w.reshape(HC, P, o, C).transpose(1, 0, 2, 3)

    def read_gb(g, b, o):
        return np.stack([g.reshape(o, HC, P), b.reshape(o, HC, P)]).transpose(3, 0, 1, 2)

    def small(w):
        a, bb, sk = w[:NA], w[NA:2 * NA], w[2 * NA:]
        order = [q.reshape(RH, C - 1, *q.shape[1:]).swapaxes(0, 1).reshape(NA, *q.shape[1:]) for q in (a, bb)]
        return np.concatenate([*order, sk])

    def wall(wod, wab):
        w = np.concatenate([wod, small(wab)]).T
        return w.reshape(-1, P, WALL)

    def expand(du_a, du_m):
        e = np.zeros((ROWS, NX, P), np.float32)
        e[:DR, 0:HC] = du_a.reshape(HC, P, DR).transpose(2, 0, 1)
        e[:DR, HC:2 * HC] = du_m.reshape(HC, P, DR).transpose(2, 0, 1)
        for j in range(2 * C - 1):
            for r in range(RH):
                e[DR + j * RH + r, 2 * HC + j, r::RH] = 1.0
        return e

    def small_bias(b):
        return np.concatenate([np.zeros(DR, np.float32), small(b)])

    wall_m = wall(L0_xattn_mlp_wod_w, L0_xattn_mlp_wab_w)
    up = ctx_1024.reshape(2, NM, P, HC, P).transpose(1, 4, 0, 3, 2)
    row, col = np.arange(P)[:, None], np.arange(P)[None, :]
    return {
        "x": x.reshape(B * L, HC, P, C).transpose(3, 1, 2, 0).reshape(NF, P, B * L),
        "pos": pos_BxS.reshape(B * KT, P).T,
        "inv_freq": np.broadcast_to((1.0 / 10000.0 ** (np.arange(HD // 2, dtype=np.float32) / np.float32(HD // 2))
                                     ).astype(np.float32), (P, HD // 2)),
        "gates": np.broadcast_to(np.stack([g_xattn.reshape(()), g_ffn.reshape(()), L0_ffn_scale.reshape(())]), (P, 3)),
        "ident": np.eye(P, dtype=np.float32),
        "masks": np.stack([np.where(row > col, np.float32(NEG), np.float32(0)),
                           np.where(col > row, np.float32(NEG), np.float32(0))], 1),
        "read1": read(L0_xattn_attn_read_w, 3),
        "read1_gb": read_gb(L0_xattn_attn_read_g, L0_xattn_attn_read_b, 3),
        "read2": read(L0_xattn_mlp_read_w, 2),
        "read2_gb": read_gb(L0_xattn_mlp_read_g, L0_xattn_mlp_read_b, 2),
        "qkv": L0_xattn_qkv_w.reshape(3, H, HC, P).transpose(3, 0, 2, 1).reshape(P, 3 * HC * H),
        "wall_a": wall(L0_xattn_attn_wod_w, L0_xattn_attn_wab_w).transpose(1, 0, 2),
        "expand": expand(L0_xattn_attn_du_w, L0_xattn_mlp_du_w),
        "bias": np.stack([small_bias(L0_xattn_attn_wab_b), small_bias(L0_xattn_mlp_wab_b)], 1),
        "du_b": np.stack([L0_xattn_attn_du_b.reshape(HC, P), L0_xattn_mlp_du_b.reshape(HC, P)]).transpose(2, 0, 1),
        "mlp_up": up.reshape(NM, P, 2 * HC * P),
        "mlp_proj": wall_m,
        "sign": L0_ffn_sign.reshape(HC, P, C, HC, P, C).transpose(5, 3, 1, 2, 0, 4).reshape(NF, P, NF, P),
    }


def kernel(**inputs):
    import numpy as np
    import concourse.bacc as bacc
    from concourse.bass_utils import run_bass_kernel_spmd

    arrays = {"in_" + k: np.ascontiguousarray(v) for k, v in layouts(**{k: np.asarray(v) for k, v in inputs.items()}).items()}
    nc = bacc.Bacc("TRN2", target_bir_lowering=False, num_devices=1)
    args = {k[3:]: nc.dram_tensor(k, v.shape, mybir.dt.from_np(v.dtype), kind="ExternalInput").ap()
            for k, v in arrays.items()}
    args["out"] = nc.dram_tensor("out", [NF, P, B * L], F32, kind="ExternalOutput").ap()
    build(nc, args)
    result = run_bass_kernel_spmd(nc, [arrays], core_ids=[0]).results[0]["out"]
    return result.reshape(C, HC, P, B, L).transpose(3, 4, 1, 2, 0).reshape(B, L, D)
```
